# Optimizing a Trainium2 kernel written in Bass

```python
import numpy as np
import jax
import jax.numpy as jnp

def _softmax(x, axis=-1):
    return jax.nn.softmax(x, axis=axis)

def _gelu(x):
    return jax.nn.gelu(x, approximate=True)

def _silu(x):
    return jax.nn.silu(x)

def _sigmoid(x):
    return jax.nn.sigmoid(x)

def _layernorm(x, axis=-1, eps=1e-05):
    m = jnp.mean(x, axis=axis, keepdims=True)
    v = jnp.var(x, axis=axis, keepdims=True)
    return (x - m) / jnp.sqrt(v + eps)

def _scatter_add(tgt, idx, src, axis=0):
    return tgt.at[idx].add(src)

def _segment_sum(src, seg, n):
    return jax.ops.segment_sum(src, seg, n)
kernel_name = 'mk_perceiver_d2_seqx_r4_757178'

def setup_inputs(seed: int=0):
    np.random.seed(seed)
    _w = jnp.asarray

    def _rec_inputs():
        import jax
        import jax.numpy as jnp
        _rk = jax.random.key(seed)
        x = -0.0003929 + 0.9999 * jax.random.normal(jax.random.fold_in(_rk, 1), (1, 256, 512), jnp.float32)
        _lenS = 256 - jax.random.randint(jax.random.fold_in(_rk, 7), (1,), 0, max(1, 256 // 4) + 1, jnp.int32)
        _lenS2 = 4096 - jax.random.randint(jax.random.fold_in(_rk, 8), (1,), 0, max(1, 4096 // 4) + 1, jnp.int32)
        _ctx_1024P = jax.random.normal(jax.random.fold_in(_rk, 11), (1, 16, 256), jnp.float32)
        _ctx_1024c = jax.random.dirichlet(jax.random.fold_in(_rk, 511), 0.3 * jnp.ones((16,), jnp.float32), (1, 4096))
        _ctx_1024t = jnp.einsum('bsk,bkd->bsd', _ctx_1024c, _ctx_1024P)
        _ctx_1024t = _ctx_1024t * jax.lax.rsqrt(jnp.mean(jnp.square(_ctx_1024t)) + 1e-12) * 0.953939
        ctx_1024 = 0.000227908 + 0.99994 * (_ctx_1024t + 0.3 * jax.random.normal(jax.random.fold_in(_rk, 611), (1, 4096, 256), jnp.float32))
        return (x, ctx_1024)
    x, ctx_1024 = _rec_inputs()

    def _L0_xattn_setup():
        import jax, jax.numpy as jnp
        import numpy as np
        EPS = 1e-05

        def rmsnorm(x, g, eps=EPS):
            var = jnp.mean(jnp.square(x), axis=-1, keepdims=True)
            return x * jax.lax.rsqrt(var + eps) * g
        key = jax.random.key(seed)
        ks = jax.random.split(key, 8)
        B, Sq, Skv = (2, 1024, 128)
        dim, cdim, H, D = (512, 256, 16, 128)
        inner = H * D
        s = lambda f: 1.0 / np.sqrt(f)
        return {'hidden_states': jax.random.normal(ks[0], (B, Sq, dim), jnp.float32), 'encoder_hidden_states': jax.random.normal(ks[1], (B, Skv, cdim), jnp.float32), 'Wq': jax.random.normal(ks[2], (dim, inner), jnp.float32) * s(dim), 'Wk': jax.random.normal(ks[3], (cdim, inner), jnp.float32) * s(cdim), 'Wv': jax.random.normal(ks[4], (cdim, inner), jnp.float32) * s(cdim), 'Wo': jax.random.normal(ks[5], (inner, dim), jnp.float32) * s(inner), 'gq': jnp.ones((D,), jnp.float32), 'gk': jnp.ones((D,), jnp.float32)}
    _L0_xattn_all = _L0_xattn_setup()
    _L0_xattn_in = {k: v for k, v in _L0_xattn_all.items() if k in ('Wq', 'Wk', 'Wv', 'Wo', 'gq', 'gk')}
    del _L0_xattn_all

    def _L0_attn_setup():
        import jax, jax.numpy as jnp
        import numpy as np
        B, S, HID = (2, 512, 512)
        NH, NKV, HD = (16, 4, 128)
        KV_DIM = NKV * HD
        key = jax.random.key(seed)
        ks = jax.random.split(key, 7)
        sc = 0.02
        return {'hidden_states': jax.random.normal(ks[0], (B, S, HID), dtype=jnp.float32), 'Wq': jax.random.normal(ks[1], (NH * HD, HID), dtype=jnp.float32) * sc, 'Wk': jax.random.normal(ks[2], (KV_DIM, HID), dtype=jnp.float32) * sc, 'Wv': jax.random.normal(ks[3], (KV_DIM, HID), dtype=jnp.float32) * sc, 'Wo': jax.random.normal(ks[4], (HID, NH * HD), dtype=jnp.float32) * sc, 'bo': jnp.zeros((HID,), dtype=jnp.float32)}
    _L0_attn_all = _L0_attn_setup()
    _L0_attn_in = {k: v for k, v in _L0_attn_all.items() if k in ('Wq', 'Wk', 'Wv', 'Wo', 'bo')}
    del _L0_attn_all

    def _L0_ffn_setup():
        import jax, jax.numpy as jnp
        import numpy as np
        HID = 512
        INTER = 2048
        NEXP = 8
        TOPK = 2
        EPS = 1e-05

        def _mock_fused_moe(x, selected_experts, routing_weights, expert_weight):
            y = jnp.einsum('bsh,hd->bsd', x, expert_weight)
            scale = routing_weights.sum(axis=-1, keepdims=True)
            return y * scale
        key = jax.random.key(seed)
        ks = jax.random.split(key, 6)
        s = lambda fan_in: 1.0 / np.sqrt(fan_in)
        return {'hidden_states': jax.random.normal(ks[0], (4, 1024, HID), dtype=jnp.float32), 'gate_w': jax.random.uniform(ks[1], (HID, NEXP), jnp.float32, -s(HID), s(HID)), 'up_w': jax.random.uniform(ks[2], (HID, INTER), jnp.float32, -s(HID), s(HID)), 'down_w': jax.random.uniform(ks[3], (INTER, HID), jnp.float32, -s(INTER), s(INTER)), 'expert_weight': jax.random.normal(ks[4], (HID, HID), dtype=jnp.float32), 'ln_gamma': jnp.ones((HID,), jnp.float32), 'ln_beta': jnp.zeros((HID,), jnp.float32)}
    _L0_ffn_all = _L0_ffn_setup()
    _L0_ffn_in = {k: v for k, v in _L0_ffn_all.items() if k in ('gate_w', 'up_w', 'down_w', 'expert_weight', 'ln_gamma', 'ln_beta')}
    del _L0_ffn_all

    def _L1_xattn_setup():
        import jax, jax.numpy as jnp
        import numpy as np
        B, S1, S2, DCA = (2, 512, 256, 16)
        QDIM, KDIM, H = (512, 256, 16)
        HD = QDIM // H
        SCALE = HD ** (-0.5)
        EPS = 1e-06
        DCA_WEIGHT = 1.0

        def _ln(t, w, b):
            m = jnp.mean(t, axis=-1, keepdims=True)
            v = jnp.var(t, axis=-1, keepdims=True)
            return (t - m) * jax.lax.rsqrt(v + EPS) * w + b

        def _attn(q, k, v):
            s = jnp.einsum('bhqd,bhkd->bhqk', q, k) * SCALE
            p = jax.nn.softmax(s, axis=-1)
            return jnp.einsum('bhqk,bhkd->bhqd', p, v)
        key = jax.random.key(seed)
        ks = jax.random.split(key, 8)
        w = lambda k, shape: jax.random.normal(k, shape, jnp.float32) * 0.02
        return {'x': jax.random.normal(ks[0], (B, S1, QDIM), jnp.float32), 'y': jax.random.normal(ks[1], (B, S2 + DCA, KDIM), jnp.float32), 'Wq': w(ks[2], (QDIM, QDIM)), 'bq': jnp.zeros((QDIM,), jnp.float32), 'Wk': w(ks[3], (KDIM, QDIM)), 'bk': jnp.zeros((QDIM,), jnp.float32), 'Wv': w(ks[4], (KDIM, QDIM)), 'bv': jnp.zeros((QDIM,), jnp.float32), 'Wkv_dca': w(ks[5], (KDIM, 2 * QDIM)), 'bkv_dca': jnp.zeros((2 * QDIM,), jnp.float32), 'qn_w': jnp.ones((HD,), jnp.float32), 'qn_b': jnp.zeros((HD,), jnp.float32), 'kn_w': jnp.ones((HD,), jnp.float32), 'kn_b': jnp.zeros((HD,), jnp.float32), 'kn_dca_w': jnp.ones((HD,), jnp.float32), 'kn_dca_b': jnp.zeros((HD,), jnp.float32), 'Wo': w(ks[6], (QDIM, QDIM)), 'bo': jnp.zeros((QDIM,), jnp.float32)}
    _L1_xattn_all = _L1_xattn_setup()
    _L1_xattn_in = {k: v for k, v in _L1_xattn_all.items() if k in ('Wq', 'bq', 'Wk', 'bk', 'Wv', 'bv', 'Wkv_dca', 'bkv_dca', 'qn_w', 'qn_b', 'kn_w', 'kn_b', 'kn_dca_w', 'kn_dca_b', 'Wo', 'bo')}
    del _L1_xattn_all

    def _L1_attn_setup():
        import jax, jax.numpy as jnp
        import numpy as np
        EMBED = 512
        LATENT = 512
        HEADS = 16
        HEAD_DIM = LATENT // HEADS
        K = 64
        P = 4
        BATCH = 2
        SEQ = 512
        NEG_INF = float('-inf')

        def _causal_mask(S, Sk):
            col = jnp.arange(Sk)[None, :]
            row = jnp.arange(S)[:, None]
            return (col >= P) & (col - P > row)
        key = jax.random.key(seed)
        ks = jax.random.split(key, 12)
        s = 0.02
        x = jax.random.normal(ks[0], (BATCH, SEQ, EMBED), jnp.float32)
        Wq = jax.random.normal(ks[1], (EMBED, LATENT), jnp.float32) * s
        bq = jnp.zeros((LATENT,), jnp.float32)
        Wk = jax.random.normal(ks[2], (EMBED, LATENT), jnp.float32) * s
        bk = jnp.zeros((LATENT,), jnp.float32)
        Wv = jax.random.normal(ks[3], (EMBED, LATENT), jnp.float32) * s
        bv = jnp.zeros((LATENT,), jnp.float32)
        Wo = jax.random.normal(ks[4], (LATENT, EMBED), jnp.float32) * s
        bo = jnp.zeros((EMBED,), jnp.float32)
        pk = jax.random.normal(ks[5], (1, P, LATENT), jnp.float32)
        pv = jax.random.normal(ks[6], (1, P, LATENT), jnp.float32)
        return {'x': x, 'Wq': Wq, 'bq': bq, 'Wk': Wk, 'bk': bk, 'Wv': Wv, 'bv': bv, 'Wo': Wo, 'bo': bo, 'pk': pk, 'pv': pv}
    _L1_attn_all = _L1_attn_setup()
    _L1_attn_in = {k: v for k, v in _L1_attn_all.items() if k in ('Wq', 'bq', 'Wk', 'bk', 'Wv', 'bv', 'Wo', 'bo', 'pk', 'pv')}
    del _L1_attn_all

    def _L1_ffn_setup():
        import jax, jax.numpy as jnp
        import numpy as np
        EPS_LN = 1e-05
        EPS_ACT = 1e-05
        EPS_W = 1e-08

        def _layer_norm(x):
            mu = jnp.mean(x, axis=-1, keepdims=True)
            xc = x - mu
            var = jnp.mean(xc * xc, axis=-1, keepdims=True)
            return xc * jax.lax.rsqrt(var + EPS_LN)

        def _activation_quant(x):
            scale = 127.0 / jnp.clip(jnp.max(jnp.abs(x), axis=-1, keepdims=True), EPS_ACT)
            return jnp.clip(jnp.round(x * scale), -128, 127) / scale

        def _weight_quant(w):
            scale = jnp.clip(jnp.mean(jnp.abs(w)), EPS_W)
            return jnp.clip(jnp.round(w / scale), -1, 1) * scale

        def _bitlinear(x, w, b):
            xn = _layer_norm(x)
            xq = _activation_quant(xn)
            wq = _weight_quant(w)
            return jnp.einsum('bsd,fd->bsf', xq, wq) + b
        key = jax.random.key(seed)
        k1, k2, k3, k4, k5 = jax.random.split(key, 5)
        d_model, d_ff = (512, 2048)
        B, S = (4, 512)
        x = jax.random.normal(k1, (B, S, d_model), dtype=jnp.float32)
        lim1 = 1.0 / np.sqrt(d_model)
        lim2 = 1.0 / np.sqrt(d_ff)
        w1 = jax.random.uniform(k2, (d_ff, d_model), jnp.float32, -lim1, lim1)
        b1 = jax.random.uniform(k3, (d_ff,), jnp.float32, -lim1, lim1)
        w2 = jax.random.uniform(k4, (d_model, d_ff), jnp.float32, -lim2, lim2)
        b2 = jax.random.uniform(k5, (d_model,), jnp.float32, -lim2, lim2)
        return {'x': x, 'w1': w1, 'b1': b1, 'w2': w2, 'b2': b2}
    _L1_ffn_all = _L1_ffn_setup()
    _L1_ffn_in = {k: v for k, v in _L1_ffn_all.items() if k in ('w1', 'b1', 'w2', 'b2')}
    del _L1_ffn_all
    return {'x': x, 'ctx_1024': ctx_1024, 'L0_xattn_Wq': _L0_xattn_in['Wq'], 'L0_xattn_Wk': _L0_xattn_in['Wk'], 'L0_xattn_Wv': _L0_xattn_in['Wv'], 'L0_xattn_Wo': _L0_xattn_in['Wo'], 'L0_xattn_gq': _L0_xattn_in['gq'], 'L0_xattn_gk': _L0_xattn_in['gk'], 'L0_attn_Wq': _L0_attn_in['Wq'], 'L0_attn_Wk': _L0_attn_in['Wk'], 'L0_attn_Wv': _L0_attn_in['Wv'], 'L0_attn_Wo': _L0_attn_in['Wo'], 'L0_attn_bo': _L0_attn_in['bo'], 'L0_ffn_gate_w': _L0_ffn_in['gate_w'], 'L0_ffn_up_w': _L0_ffn_in['up_w'], 'L0_ffn_down_w': _L0_ffn_in['down_w'], 'L0_ffn_expert_weight': _L0_ffn_in['expert_weight'], 'L0_ffn_ln_gamma': _L0_ffn_in['ln_gamma'], 'L0_ffn_ln_beta': _L0_ffn_in['ln_beta'], 'L1_xattn_Wq': _L1_xattn_in['Wq'], 'L1_xattn_bq': _L1_xattn_in['bq'], 'L1_xattn_Wk': _L1_xattn_in['Wk'], 'L1_xattn_bk': _L1_xattn_in['bk'], 'L1_xattn_Wv': _L1_xattn_in['Wv'], 'L1_xattn_bv': _L1_xattn_in['bv'], 'L1_xattn_Wkv_dca': _L1_xattn_in['Wkv_dca'], 'L1_xattn_bkv_dca': _L1_xattn_in['bkv_dca'], 'L1_xattn_qn_w': _L1_xattn_in['qn_w'], 'L1_xattn_qn_b': _L1_xattn_in['qn_b'], 'L1_xattn_kn_w': _L1_xattn_in['kn_w'], 'L1_xattn_kn_b': _L1_xattn_in['kn_b'], 'L1_xattn_kn_dca_w': _L1_xattn_in['kn_dca_w'], 'L1_xattn_kn_dca_b': _L1_xattn_in['kn_dca_b'], 'L1_xattn_Wo': _L1_xattn_in['Wo'], 'L1_xattn_bo': _L1_xattn_in['bo'], 'L1_attn_Wq': _L1_attn_in['Wq'], 'L1_attn_bq': _L1_attn_in['bq'], 'L1_attn_Wk': _L1_attn_in['Wk'], 'L1_attn_bk': _L1_attn_in['bk'], 'L1_attn_Wv': _L1_attn_in['Wv'], 'L1_attn_bv': _L1_attn_in['bv'], 'L1_attn_Wo': _L1_attn_in['Wo'], 'L1_attn_bo': _L1_attn_in['bo'], 'L1_attn_pk': _L1_attn_in['pk'], 'L1_attn_pv': _L1_attn_in['pv'], 'L1_ffn_w1': _L1_ffn_in['w1'], 'L1_ffn_b1': _L1_ffn_in['b1'], 'L1_ffn_w2': _L1_ffn_in['w2'], 'L1_ffn_b2': _L1_ffn_in['b2']}

def reference(x, ctx_1024, L0_xattn_Wq, L0_xattn_Wk, L0_xattn_Wv, L0_xattn_Wo, L0_xattn_gq, L0_xattn_gk, L0_attn_Wq, L0_attn_Wk, L0_attn_Wv, L0_attn_Wo, L0_attn_bo, L0_ffn_gate_w, L0_ffn_up_w, L0_ffn_down_w, L0_ffn_expert_weight, L0_ffn_ln_gamma, L0_ffn_ln_beta, L1_xattn_Wq, L1_xattn_bq, L1_xattn_Wk, L1_xattn_bk, L1_xattn_Wv, L1_xattn_bv, L1_xattn_Wkv_dca, L1_xattn_bkv_dca, L1_xattn_qn_w, L1_xattn_qn_b, L1_xattn_kn_w, L1_xattn_kn_b, L1_xattn_kn_dca_w, L1_xattn_kn_dca_b, L1_xattn_Wo, L1_xattn_bo, L1_attn_Wq, L1_attn_bq, L1_attn_Wk, L1_attn_bk, L1_attn_Wv, L1_attn_bv, L1_attn_Wo, L1_attn_bo, L1_attn_pk, L1_attn_pv, L1_ffn_w1, L1_ffn_b1, L1_ffn_w2, L1_ffn_b2):
    import jax
    import jax.numpy as jnp

    def _L0_xattn_ref(hidden_states, encoder_hidden_states, Wq, Wk, Wv, Wo, gq, gk):
        import jax, jax.numpy as jnp
        import numpy as np
        EPS = 1e-05

        def rmsnorm(x, g, eps=EPS):
            var = jnp.mean(jnp.square(x), axis=-1, keepdims=True)
            return x * jax.lax.rsqrt(var + eps) * g
        B, Sq, _ = hidden_states.shape
        Skv = encoder_hidden_states.shape[1]
        D = gq.shape[0]
        H = Wq.shape[1] // D
        scale = 1.0 / np.sqrt(D)
        q = (hidden_states @ Wq).reshape(B, Sq, H, D)
        k = (encoder_hidden_states @ Wk).reshape(B, Skv, H, D)
        v = (encoder_hidden_states @ Wv).reshape(B, Skv, H, D)
        q = rmsnorm(q, gq)
        k = rmsnorm(k, gk)
        scores = jnp.einsum('bqhd,bkhd->bhqk', q, k) * scale
        attn = jax.nn.softmax(scores, axis=-1)
        out = jnp.einsum('bhqk,bkhd->bqhd', attn, v)
        out = out.reshape(B, Sq, H * D)
        return out @ Wo

    def _L0_attn_ref(hidden_states, Wq, Wk, Wv, Wo, bo):
        import jax, jax.numpy as jnp
        import numpy as np
        B, S, HID = (2, 512, 512)
        NH, NKV, HD = (16, 4, 128)
        KV_DIM = NKV * HD
        b, s, _ = hidden_states.shape
        q = (hidden_states @ Wq.T).reshape(b, s, NH, HD).transpose(0, 2, 1, 3)
        k = (hidden_states @ Wk.T).reshape(b, s, NKV, HD).transpose(0, 2, 1, 3)
        v = (hidden_states @ Wv.T).reshape(b, s, NKV, HD).transpose(0, 2, 1, 3)
        g = NH // NKV
        k_rep = jnp.repeat(k, g, axis=1)
        v_rep = jnp.repeat(v, g, axis=1)
        qf = q.astype(jnp.float32)
        kf = k_rep.astype(jnp.float32)
        scores = jnp.einsum('bhqd,bhkd->bhqk', qf, kf)
        causal = jnp.tril(jnp.ones((s, s), dtype=bool))[None, None]
        neg = jnp.finfo(scores.dtype).min
        scores = jnp.where(causal, scores, neg)
        attn = jax.nn.softmax(scores, axis=-1).astype(v.dtype)
        out = jnp.einsum('bhqk,bhkd->bhqd', attn, v_rep)
        out = out.transpose(0, 2, 1, 3).reshape(b, s, NH * HD)
        return out @ Wo.T + bo

    def _L0_ffn_ref(hidden_states, gate_w, up_w, down_w, expert_weight, ln_gamma, ln_beta):
        import jax, jax.numpy as jnp
        import numpy as np
        HID = 512
        INTER = 2048
        NEXP = 8
        TOPK = 2
        EPS = 1e-05

        def _mock_fused_moe(x, selected_experts, routing_weights, expert_weight):
            y = jnp.einsum('bsh,hd->bsd', x, expert_weight)
            scale = routing_weights.sum(axis=-1, keepdims=True)
            return y * scale
        residuals = hidden_states
        logits = jnp.einsum('bsh,he->bse', hidden_states, gate_w)
        routing_weights, selected_experts = jax.lax.top_k(logits, TOPK)
        h = jnp.einsum('bsh,hi->bsi', residuals, up_w)
        h = jnp.square(jax.nn.relu(h))
        shared_out = jnp.einsum('bsi,ih->bsh', h, down_w)
        moe_out = _mock_fused_moe(hidden_states, selected_experts, routing_weights, expert_weight)
        y = shared_out + moe_out
        mu = y.mean(axis=-1, keepdims=True)
        var = jnp.mean(jnp.square(y - mu), axis=-1, keepdims=True)
        return (y - mu) * jax.lax.rsqrt(var + EPS) * ln_gamma + ln_beta

    def _L1_xattn_ref(x, y, Wq, bq, Wk, bk, Wv, bv, Wkv_dca, bkv_dca, qn_w, qn_b, kn_w, kn_b, kn_dca_w, kn_dca_b, Wo, bo):
        import jax, jax.numpy as jnp
        import numpy as np
        B, S1, S2, DCA = (2, 512, 256, 16)
        QDIM, KDIM, H = (512, 256, 16)
        HD = QDIM // H
        SCALE = HD ** (-0.5)
        EPS = 1e-06
        DCA_WEIGHT = 1.0

        def _ln(t, w, b):
            m = jnp.mean(t, axis=-1, keepdims=True)
            v = jnp.var(t, axis=-1, keepdims=True)
            return (t - m) * jax.lax.rsqrt(v + EPS) * w + b

        def _attn(q, k, v):
            s = jnp.einsum('bhqd,bhkd->bhqk', q, k) * SCALE
            p = jax.nn.softmax(s, axis=-1)
            return jnp.einsum('bhqk,bhkd->bhqd', p, v)
        b, s1, _ = x.shape
        y_dca = y[:, -DCA:, :]
        y_main = y[:, :-DCA, :]
        kv_dca = (y_dca @ Wkv_dca + bkv_dca).reshape(b, DCA, 2, H, HD)
        k_dca = _ln(kv_dca[:, :, 0], kn_dca_w, kn_dca_b)
        v_dca = kv_dca[:, :, 1]
        s2 = y_main.shape[1]
        q = _ln((x @ Wq + bq).reshape(b, s1, H, HD), qn_w, qn_b)
        kv = jnp.concatenate([y_main @ Wk + bk, y_main @ Wv + bv], axis=-1)
        kv = kv.reshape(b, s2, H, 2 * HD)
        k = _ln(kv[..., :HD], kn_w, kn_b)
        v = kv[..., HD:]
        qT = q.transpose(0, 2, 1, 3)
        ctx = _attn(qT, k.transpose(0, 2, 1, 3), v.transpose(0, 2, 1, 3))
        ctx = ctx.transpose(0, 2, 1, 3).reshape(b, s1, QDIM)
        ctx_dca = _attn(qT, k_dca.transpose(0, 2, 1, 3), v_dca.transpose(0, 2, 1, 3))
        ctx_dca = ctx_dca.transpose(0, 2, 1, 3).reshape(b, s1, QDIM)
        ctx = ctx + DCA_WEIGHT * ctx_dca
        return ctx @ Wo + bo

    def _L1_attn_ref(x, Wq, bq, Wk, bk, Wv, bv, Wo, bo, pk, pv):
        import jax, jax.numpy as jnp
        import numpy as np
        EMBED = 512
        LATENT = 512
        HEADS = 16
        HEAD_DIM = LATENT // HEADS
        K = 64
        P = 4
        BATCH = 2
        SEQ = 512
        NEG_INF = float('-inf')

        def _causal_mask(S, Sk):
            col = jnp.arange(Sk)[None, :]
            row = jnp.arange(S)[:, None]
            return (col >= P) & (col - P > row)
        B, S, _ = x.shape
        Sk = S + P
        q = (x @ Wq + bq).reshape(B, S, HEADS, HEAD_DIM).transpose(0, 2, 1, 3)
        k = jnp.concatenate([x @ Wk + bk, jnp.broadcast_to(pk, (B, P, LATENT))], axis=1)
        v = jnp.concatenate([x @ Wv + bv, jnp.broadcast_to(pv, (B, P, LATENT))], axis=1)
        k = k.reshape(B, Sk, HEADS, HEAD_DIM).transpose(0, 2, 1, 3)
        v = v.reshape(B, Sk, HEADS, HEAD_DIM).transpose(0, 2, 1, 3)
        scores = jnp.einsum('bhqd,bhkd->bhqk', q, k) / HEAD_DIM ** 0.5
        scores = jnp.where(_causal_mask(S, Sk)[None, None], NEG_INF, scores)
        topk_vals, topk_idx = jax.lax.top_k(scores, K)
        bi = jnp.arange(B)[:, None, None, None]
        hi = jnp.arange(HEADS)[None, :, None, None]
        si = jnp.arange(S)[None, None, :, None]
        masked = jnp.full_like(scores, NEG_INF).at[bi, hi, si, topk_idx].set(topk_vals)
        attn = jax.nn.softmax(masked, axis=-1)
        out = jnp.einsum('bhqk,bhkd->bhqd', attn, v)
        out = out.transpose(0, 2, 1, 3).reshape(B, S, LATENT)
        return out @ Wo + bo

    def _L1_ffn_ref(x, w1, b1, w2, b2):
        import jax, jax.numpy as jnp
        import numpy as np
        EPS_LN = 1e-05
        EPS_ACT = 1e-05
        EPS_W = 1e-08

        def _layer_norm(x):
            mu = jnp.mean(x, axis=-1, keepdims=True)
            xc = x - mu
            var = jnp.mean(xc * xc, axis=-1, keepdims=True)
            return xc * jax.lax.rsqrt(var + EPS_LN)

        def _activation_quant(x):
            scale = 127.0 / jnp.clip(jnp.max(jnp.abs(x), axis=-1, keepdims=True), EPS_ACT)
            return jnp.clip(jnp.round(x * scale), -128, 127) / scale

        def _weight_quant(w):
            scale = jnp.clip(jnp.mean(jnp.abs(w)), EPS_W)
            return jnp.clip(jnp.round(w / scale), -1, 1) * scale

        def _bitlinear(x, w, b):
            xn = _layer_norm(x)
            xq = _activation_quant(xn)
            wq = _weight_quant(w)
            return jnp.einsum('bsd,fd->bsf', xq, wq) + b
        h = _bitlinear(x, w1, b1)
        h = jax.nn.gelu(h, approximate=False)
        return _bitlinear(h, w2, b2)
    x = x + _L0_xattn_ref(_layernorm(x, axis=-1), ctx_1024, L0_xattn_Wq, L0_xattn_Wk, L0_xattn_Wv, L0_xattn_Wo, L0_xattn_gq, L0_xattn_gk)
    x = x + _L0_attn_ref(_layernorm(x, axis=-1), L0_attn_Wq, L0_attn_Wk, L0_attn_Wv, L0_attn_Wo, L0_attn_bo)
    x = x + _L0_ffn_ref(_layernorm(x, axis=-1), L0_ffn_gate_w, L0_ffn_up_w, L0_ffn_down_w, L0_ffn_expert_weight, L0_ffn_ln_gamma, L0_ffn_ln_beta)
    x = x + _L1_xattn_ref(_layernorm(x, axis=-1), ctx_1024, L1_xattn_Wq, L1_xattn_bq, L1_xattn_Wk, L1_xattn_bk, L1_xattn_Wv, L1_xattn_bv, L1_xattn_Wkv_dca, L1_xattn_bkv_dca, L1_xattn_qn_w, L1_xattn_qn_b, L1_xattn_kn_w, L1_xattn_kn_b, L1_xattn_kn_dca_w, L1_xattn_kn_dca_b, L1_xattn_Wo, L1_xattn_bo)
    x = x + _L1_attn_ref(_layernorm(x, axis=-1), L1_attn_Wq, L1_attn_bq, L1_attn_Wk, L1_attn_bk, L1_attn_Wv, L1_attn_bv, L1_attn_Wo, L1_attn_bo, L1_attn_pk, L1_attn_pv)
    x = x + _L1_ffn_ref(_layernorm(x, axis=-1), L1_ffn_w1, L1_ffn_b1, L1_ffn_w2, L1_ffn_b2)
    return x

_drawn_inputs = setup_inputs


def setup_inputs(seed=0):
    import zlib

    import numpy as np

    out = dict(_drawn_inputs(seed))
    spreads = {'L0_xattn_gq': (1.0, 0.2),
     'L0_xattn_gk': (1.0, 0.2),
     'L0_attn_bo': (0.0, 0.1),
     'L0_ffn_ln_gamma': (1.0, 0.2),
     'L0_ffn_ln_beta': (0.0, 0.1),
     'L1_xattn_bq': (0.0, 0.652),
     'L1_xattn_bk': (0.0, 0.345),
     'L1_xattn_bv': (0.0, 0.338),
     'L1_xattn_bkv_dca': (0.0, 0.1),
     'L1_xattn_qn_w': (1.0, 0.6),
     'L1_xattn_qn_b': (0.0, 2.0),
     'L1_xattn_kn_w': (1.0, 0.6),
     'L1_xattn_kn_b': (0.0, 2.0),
     'L1_xattn_kn_dca_w': (1.0, 0.6),
     'L1_xattn_kn_dca_b': (0.0, 2.0),
     'L1_xattn_bo': (0.0, 0.1),
     'L1_attn_bq': (0.0, 0.8),
     'L1_attn_bk': (0.0, 2.0),
     'L1_attn_bv': (0.0, 0.1),
     'L1_attn_bo': (0.0, 0.1)}
    factors = {'L0_ffn_up_w': 5.038,
     'L0_ffn_down_w': 4.77,
     'L1_attn_Wq': 4.094,
     'L1_attn_Wk': 4.111,
     'L1_attn_pk': 8.0,
     'L1_attn_pv': 8.0,
     'L1_ffn_b1': 2.919,
     'L1_ffn_b2': 7.352}
    for name, (base, spread) in spreads.items():
        noise = np.random.default_rng([zlib.crc32(name.encode()), seed]).standard_normal(out[name].shape)
        drawn = base * np.exp(spread * noise) if base else spread * noise
        out[name] = jnp.asarray(drawn.astype(out[name].dtype))
    for name, factor in factors.items():
        out[name] = (out[name] * factor).astype(out[name].dtype)
    return out
```

```python
from contextlib import ExitStack

import concourse.bass as bass
from concourse import mybir

F32 = mybir.dt.float32
F32R = mybir.dt.float32r
BF16 = mybir.dt.bfloat16
ACT = mybir.ActivationFunctionType
ALU = mybir.AluOpType
AX_X = mybir.AxisListType.X

P = 128
S = 256
QT = S // P
HID = 512
HC = HID // P
KV = 4096
CD = 256
CC = CD // P
NT = KV // P
CH = 512
NCH = KV // CH
TPC = CH // P
H = 16
D = 128
LOWEST = -3.0e38
LAST_STAGE = 6


def at_least(eng, sem, value):
    if not isinstance(value, int) or value > 0:
        eng.wait_ge(sem, value)


def heads_loop(eng, nc_engine, body):
    body(0, True, False, False)
    body(1, True, True, False)
    with nc_engine.Fori(2, H) as h:
        body(h, True, True, True)
    body(H, False, True, True)
    body(H + 1, False, False, True)


class Tiles:

    def __init__(self, nc, ctx, stage, finished=None):
        self.nc, self.ctx, self.stage = nc, ctx, stage
        if finished is not None:
            self.used = []
            ctx.callback(lambda: finished.extend(self.used))

    def sb(self, name, shape, dt=F32):
        return self.ctx.enter_context(self.nc.sbuf_tensor(f"{self.stage}_{name}", shape, dt))

    def psum(self, name, shape, dt=F32):
        return self.ctx.enter_context(self.nc.psum_tensor(f"{self.stage}_{name}", shape, dt))

    def sem(self, name):
        handle = self.ctx.enter_context(self.nc.semaphore(f"{self.stage}_{name}"))
        self.used.append(handle.num)
        return handle


def clear_semaphores(nc, finished):
    with nc.Block() as block:
        @block.gpsimd
        def _(pool):
            first = None
            for n in sorted(finished):
                if first is None:
                    first = n
                if n + 1 not in finished:
                    nc.gpsimd.sem_clear(range(first, n + 1))
                    first = None
    finished.clear()


def setup_constants(nc, T, c):
    with ExitStack() as ctx:
        t = Tiles(nc, ctx, "setup", c["finished"])
        zeroed, made, loaded = t.sem("zeroed"), t.sem("made"), t.sem("loaded")
        block = ctx.enter_context(nc.Block())

        @block.sync
        def _(sp):
            sp.dma_start(c["x"][:], T["x"].rearrange("(t p) n -> p t n", p=P)).then_inc(loaded, 16)
            sp.wait_ge(loaded, 16)

        @block.scalar
        def _(act):
            nc.scalar.preload_act_table_set("natural_log_exp_and_others")

        @block.gpsimd
        def _(pool):
            nc.gpsimd.memset(c["ident"][:], 0.0).then_inc(zeroed, 1)
            nc.gpsimd.memset(c["identb"][:], 0.0).then_inc(zeroed, 1)
            nc.gpsimd.memset(c["ones"][:], 1.0)
            nc.gpsimd.memset(c["eps5"][:], 1e-5)
            nc.gpsimd.memset(c["eps6"][:], 1e-6)
            pool.wait_ge(zeroed, 2)
            for m in (c["ident"], c["identb"]):
                nc.gpsimd.affine_select(out=m[:], in_=m[:], compare_op=ALU.not_equal, fill=1.0, base=0,
                                        pattern=[[-1, P]], channel_multiplier=1).then_inc(made, 1)


def layernorm_transposed(nc, c, stage, x, xnT, prefetch=None):
    with ExitStack() as ctx:
        t = Tiles(nc, ctx, stage, c["finished"])
        stats, mv = t.sb("stats", [P, QT, 6]), t.sb("mv", [P, QT, 2])
        logvar, rstd = t.sb("logvar", [P, QT]), t.sb("rstd", [P, QT])
        xn = t.sb("xn", [P, QT, HID])
        turned = t.psum("turned", [P, QT, HID])
        stats_done, moments_done, log_done, rstd_done, normed, transposed = map(
            t.sem, ("stats_done", "moments_done", "log_done", "rstd_done", "normed", "transposed"))
        block = ctx.enter_context(nc.Block())

        if prefetch:
            @block.sync
            def _(sp):
                prefetch(sp)

        @block.vector
        def _(dve):
            for q in range(QT):
                nc.vector.bn_stats(stats[:, q, :], x[:, q, :]).then_inc(stats_done, 1)
            for q in range(QT):
                dve.wait_ge(stats_done, q + 1)
                nc.vector.bn_aggr(mv[:, q, :], stats[:, q, :]).then_inc(moments_done, 1)
            dve.wait_ge(moments_done, QT)
            dve.wait_ge(rstd_done, 1)
            for q in range(QT):
                nc.vector.tensor_scalar(xn[:, q, :], x[:, q, :], mv[:, q, 0:1], rstd[:, q:q + 1],
                                        ALU.subtract, ALU.mult).then_inc(normed, 1)

        @block.scalar
        def _(act):
            act.wait_ge(moments_done, QT)
            nc.scalar.activation(logvar[:], mv[:, :, 1], ACT.Ln, bias=c["eps5"][:]).then_inc(log_done, 1)
            act.wait_ge(log_done, 1)
            nc.scalar.activation(rstd[:], logvar[:], ACT.Exp, scale=-0.5).then_inc(rstd_done, 1)
            for q in range(QT):
                act.wait_ge(transposed, q + 1)
                nc.scalar.activation(xnT[:, :, q * P:(q + 1) * P],
                                     turned[:, q, :].rearrange("p (k t) -> p k t", k=HC), ACT.Copy)

        @block.tensor
        def _(pe):
            for q in range(QT):
                pe.wait_ge(normed, q + 1)
                for k in range(HC):
                    last = nc.tensor.transpose(turned[:, q, k * P:(k + 1) * P], xn[:, q, k * P:(k + 1) * P],
                                               c["ident"][:])
                last.then_inc(transposed, 1)


def cross0_queries(nc, T, c, xnT, qT, ctxT_hi, ctxT_lo, ctx_hl, wq, wq_loaded):
    NP = 8
    PIECE = 2048
    with ExitStack() as ctx:
        t = Tiles(nc, ctx, "queries0", c["finished"])
        raw = t.sb("raw", [P, 2, PIECE])
        gq, gk, gqk = t.sb("gq", [P, 1]), t.sb("gk", [P, 1]), t.sb("gqk", [P, 1])
        squares, log_ms, rrms = t.sb("squares", [P, 2, S]), t.sb("log_ms", [P, 2, S]), t.sb("rrms", [P, 2, S])
        q_ps = t.psum("q_ps", [P, 2, CH])
        ms_ps = t.psum("ms_ps", [P, 2, CH])
        g_loaded, g_done = t.sem("g_loaded"), t.sem("g_done")
        raw_loaded = [t.sem("raw_loaded0"), t.sem("raw_loaded1")]
        hi_done, lo_done = t.sem("hi_done"), t.sem("lo_done")
        q_done, sq_done, ms_done, log_done, rrms_done, qT_done = map(
            t.sem, ("q_done", "sq_done", "ms_done", "log_done", "rrms_done", "qT_done"))
        block = ctx.enter_context(nc.Block())

        def piece(i):
            if i < 4:
                k, half = i // 2, (i % 2) * PIECE
                src = T["ctxT"][k * P:(k + 1) * P, half:half + PIECE]
                return src, raw[:, i % 2, :], ctxT_hi[:, k, half:half + PIECE], ctxT_lo[:, k, half:half + PIECE]
            n = PIECE // CD
            tiles = slice((i - 4) * n, (i - 3) * n)
            src = T["ctx"].rearrange("(t p) n -> p t n", p=P)[:, tiles, :]
            return (src, raw[:, i % 2, :].rearrange("p (t n) -> p t n", n=CD),
                    ctx_hl[:, tiles, 0:CD], ctx_hl[:, tiles, CD:2 * CD])

        @block.sync
        def _(sp):
            sp.dma_start(gq[:], T["gq"]).then_inc(g_loaded, 16)
            sp.dma_start(gk[:], T["gk"]).then_inc(g_loaded, 16)
            for i in range(NP):
                src, dst, _, _ = piece(i)
                if i >= 2:
                    sp.wait_ge(hi_done, i - 1)
                    sp.wait_ge(lo_done, i - 1)
                sp.dma_start(dst, src).then_inc(raw_loaded[i % 2], 16)

        @block.gpsimd
        def _(pool):
            for i in range(NP):
                _, src, hi, _ = piece(i)
                pool.wait_ge(raw_loaded[i % 2], 16 * (i // 2 + 1))
                nc.gpsimd.tensor_copy(hi, src).then_inc(hi_done, 1)

        @block.vector
        def _(dve):
            dve.wait_ge(g_loaded, 32)
            nc.vector.tensor_scalar(gqk[:], gq[:], gk[:], float(D) ** -0.5, ALU.mult, ALU.mult).then_inc(g_done, 1)
            dve.wait_ge(g_done, 1)
            for h in range(H):
                dve.wait_ge(rrms_done, h + 1)
                nc.vector.scalar_tensor_tensor(qT[:, h, :], q_ps[:, h % 2, 0:S], gqk[:], rrms[:, h % 2, :],
                                               ALU.mult, ALU.mult).then_inc(qT_done, 1)
                if h % 2:
                    _, src, hi, lo = piece(h // 2)
                    dve.wait_ge(hi_done, h // 2 + 1)
                    nc.vector.tensor_tensor(lo, src, hi.bitcast(F32), ALU.subtract).then_inc(lo_done, 1)

        @block.scalar
        def _(act):
            for h in range(H):
                b = h % 2
                act.wait_ge(q_done, h + 1)
                at_least(act, ms_done, h - 1)
                nc.scalar.activation(squares[:, b, :], q_ps[:, b, 0:S], ACT.Square).then_inc(sq_done, 1)
                act.wait_ge(ms_done, h + 1)
                at_least(act, rrms_done, h - 1)
                nc.scalar.activation(log_ms[:, b, :], ms_ps[:, b, 0:S], ACT.Ln, bias=c["eps5"][:],
                                     scale=1.0 / D).then_inc(log_done, 1)
                act.wait_ge(log_done, h + 1)
                at_least(act, qT_done, h - 1)
                nc.scalar.activation(rrms[:, b, :], log_ms[:, b, :], ACT.Exp, scale=-0.5).then_inc(rrms_done, 1)

        @block.tensor
        def _(pe):
            def project(h):
                if h % 4 == 0:
                    pe.wait_ge(wq_loaded[h // 4], 16)
                at_least(pe, qT_done, h - 1)
                for k in range(HC):
                    last = nc.tensor.matmul(q_ps[:, h % 2, 0:S], wq[:, k, h * D:(h + 1) * D], xnT[:, k, :],
                                            start=(k == 0), stop=(k == HC - 1))
                last.then_inc(q_done, 1)

            project(0)
            for h in range(H):
                if h + 1 < H:
                    project(h + 1)
                pe.wait_ge(sq_done, h + 1)
                at_least(pe, log_done, h - 1)
                nc.tensor.matmul(ms_ps[:, h % 2, 0:S], c["ones"][:], squares[:, h % 2, :],
                                 start=True, stop=True).then_inc(ms_done, 1)


def cross0_attention(nc, T, c, qT, ctxT_hi, ctxT_lo, ctx_hl):
    with ExitStack() as ctx:
        t = Tiles(nc, ctx, "cross0", c["finished"])
        wk_raw = t.sb("wk_raw", [P, CC * D])
        wk_hi, wk_lo = t.sb("wk_hi", [P, CC * D], F32R), t.sb("wk_lo", [P, CC * D], F32R)
        wv = t.sb("wv", [P, CC * D])
        q_hi, q_lo = t.sb("q_hi", [P, S], F32R), t.sb("q_lo", [P, S], F32R)
        k_hi, k_lo = t.sb("k_hi", [P, CH], F32R), t.sb("k_lo", [P, CH], F32R)
        squares = t.sb("squares", [P, CH])
        log_ms, rrms = t.sb("log_ms", [P, CH]), t.sb("rrms", [P, CH])
        probs = t.sb("probs", [P, QT, KV])
        pt_hi, pt_lo = t.sb("pt_hi", [P, QT, CH], F32R), t.sb("pt_lo", [P, QT, CH], F32R)
        chunk_max, negmax = t.sb("chunk_max", [P, QT, NCH]), t.sb("negmax", [P, QT])
        chunk_sum, rowsum, rinv = t.sb("chunk_sum", [P, QT, NCH]), t.sb("rowsum", [P, QT]), t.sb("rinv", [P, QT])
        low_part = c["x"][:, 0, :].rearrange("p (q n) -> p q n", q=QT)
        pc = c["x"][:, 1, :].rearrange("p (q n) -> p q n", q=QT)
        pcT = t.sb("pcT", [P, CC * S])
        k_ps, ms_ps = t.psum("k_ps", [P, CH]), t.psum("ms_ps", [P, CH])
        s_ps, t_ps, pc_ps = (t.psum("s_ps", [P, QT, CH]), t.psum("t_ps", [P, QT, CH]),
                             t.psum("pc_ps", [P, QT, 2 * CD]))
        wk_loaded, wv_loaded = t.sem("wk_loaded"), t.sem("wv_loaded")
        wk_split, q_split = t.sem("wk_split"), t.sem("q_split")
        k_done, khi_done, klo_done, sq_done, ms_done, log_done, rrms_done = map(
            t.sem, ("k_done", "khi_done", "klo_done", "sq_done", "ms_done", "log_done", "rrms_done"))
        s_done, scored, exp_done, t_done, pthi_done, ptlo_done, pc_done = map(
            t.sem, ("s_done", "scored", "exp_done", "t_done", "pthi_done", "ptlo_done", "pc_done"))
        max_done, sum_done, rinv_done, lowpart_done, norm_done = map(
            t.sem, ("max_done", "sum_done", "rinv_done", "lowpart_done", "norm_done"))
        pcT_turned, pcT_done, out_done, stored = map(t.sem, ("pcT_turned", "pcT_done", "out_done", "stored"))
        may_score = t.sem("may_score")
        block = ctx.enter_context(nc.Block())

        @block.sync
        def _(sp):
            def load_wk(h):
                at_least(sp, wk_split, 2 * h)
                sp.dma_start(wk_raw[:], T["wk0"][bass.ds(h * P, P), :]).then_inc(wk_loaded, 16)

            def load_wv(g):
                at_least(sp, out_done, g)
                sp.dma_start(wv[:], T["wv0"][bass.ds(g * P, P), :]).then_inc(wv_loaded, 16)

            load_wk(0)
            load_wk(1)
            load_wv(0)
            with nc.sync.Fori(2, H) as h:
                load_wk(h)
                load_wv(h - 1)
            load_wv(H - 1)

        @block.tensor
        def _(pe):
            def keys(h, ch):
                if ch == 0:
                    pe.wait_ge(wk_split, 2 * h + 2)
                n = 8 * h + ch
                at_least(pe, khi_done, n)
                at_least(pe, klo_done, n)
                at_least(pe, sq_done, n)
                cols = slice(ch * CH, (ch + 1) * CH)
                for k in range(CC):
                    w = slice(k * D, (k + 1) * D)
                    nc.tensor.matmul(k_ps[:], wk_hi[:, w], ctxT_hi[:, k, cols], start=(k == 0), stop=False)
                    nc.tensor.matmul(k_ps[:], wk_hi[:, w], ctxT_lo[:, k, cols], start=False, stop=False)
                    last = nc.tensor.matmul(k_ps[:], wk_lo[:, w], ctxT_hi[:, k, cols],
                                            start=False, stop=(k == CC - 1))
                last.then_inc(k_done, 1)

            def sums(h, ch):
                pe.wait_ge(sq_done, 8 * h + ch + 1)
                at_least(pe, log_done, 8 * h + ch)
                nc.tensor.matmul(ms_ps[:], c["ones"][:], squares[:], start=True, stop=True).then_inc(ms_done, 1)

            def scores(h, ch):
                if ch == 0:
                    pe.wait_ge(q_split, 2 * h + 2)
                pe.wait_ge(khi_done, 8 * h + ch + 1)
                pe.wait_ge(klo_done, 8 * h + ch + 1)
                for q in range(QT):
                    at_least(pe, scored, 16 * h + 2 * ch + q - 1)
                    rows = slice(q * P, (q + 1) * P)
                    nc.tensor.matmul(s_ps[:, q, :], q_hi[:, rows], k_hi[:], start=True, stop=False)
                    nc.tensor.matmul(s_ps[:, q, :], q_hi[:, rows], k_lo[:], start=False, stop=False)
                    nc.tensor.matmul(s_ps[:, q, :], q_lo[:, rows], k_hi[:],
                                     start=False, stop=True).then_inc(s_done, 1)

            def transposes(g, ch):
                if ch == 0:
                    at_least(pe, stored, g)
                for q in range(QT):
                    pe.wait_ge(exp_done, 16 * g + 2 * ch + q + 1)
                    for j in range(TPC):
                        at = ch * CH + j * P
                        last = nc.tensor.transpose(t_ps[:, q, j * P:(j + 1) * P], probs[:, q, at:at + P],
                                                   c["ident"][:])
                    last.then_inc(t_done, 1)

            def values(g, ch):
                for q in range(QT):
                    pe.wait_ge(pthi_done, 16 * g + 2 * ch + q + 1)
                    pe.wait_ge(ptlo_done, 16 * g + 2 * ch + q + 1)
                    if ch == 0:
                        at_least(pe, norm_done, 2 * g + q - 1)
                    for j in range(TPC):
                        tile, cols = ch * TPC + j, slice(j * P, (j + 1) * P)
                        nc.tensor.matmul(pc_ps[:, q, :], pt_hi[:, q, cols], ctx_hl[:, tile, :],
                                         start=(tile == 0), stop=False)
                        last = nc.tensor.matmul(pc_ps[:, q, 0:CD], pt_lo[:, q, cols], ctx_hl[:, tile, 0:CD],
                                                start=False, stop=(tile == NT - 1))
                    last.then_inc(pc_done, 1)

            def body(h, has_scores, has_values, has_output):
                g, o = h - 1, h - 2
                if has_scores:
                    keys(h, 0)
                if has_output:
                    pe.wait_ge(norm_done, 2 * o + 2)
                    for q in range(QT):
                        for k in range(CC):
                            last = nc.tensor.transpose(t_ps[:, 0, k * S + q * P:k * S + (q + 1) * P],
                                                       pc[:, q, k * P:(k + 1) * P], c["ident"][:])
                    last.then_inc(pcT_turned, 1)
                if has_scores:
                    sums(h, 0)
                if has_output:
                    pe.wait_ge(pcT_done, o + 1)
                    pe.wait_ge(wv_loaded, 16 * o + 16)
                    for k in range(CC):
                        last = nc.tensor.matmul(t_ps[:, 1, 0:S], wv[:, k * D:(k + 1) * D], pcT[:, k * S:(k + 1) * S],
                                                start=(k == 0), stop=(k == CC - 1))
                    last.then_inc(out_done, 1)
                for ch in range(NCH):
                    if has_scores:
                        scores(h, ch)
                    if has_values:
                        transposes(g, ch)
                    if has_scores and ch + 1 < NCH:
                        keys(h, ch + 1)
                    if has_values:
                        values(g, ch)
                    if has_scores and ch + 1 < NCH:
                        sums(h, ch + 1)

            heads_loop(pe, nc.tensor, body)

        @block.scalar
        def _(act):
            def keys_high(h, ch):
                act.wait_ge(k_done, 8 * h + ch + 1)
                at_least(act, s_done, 16 * h + 2 * ch)
                nc.scalar.activation(k_hi[:], k_ps[:], ACT.Copy).then_inc(khi_done, 1)
                at_least(act, ms_done, 8 * h + ch)
                nc.scalar.activation(squares[:], k_ps[:], ACT.Square).then_inc(sq_done, 1)

            def keys_rrms(h, ch):
                n = 8 * h + ch
                act.wait_ge(ms_done, n + 1)
                at_least(act, rrms_done, n)
                nc.scalar.activation(log_ms[:], ms_ps[:], ACT.Ln, bias=c["eps5"][:],
                                     scale=1.0 / D).then_inc(log_done, 1)
                act.wait_ge(log_done, n + 1)
                at_least(act, scored, 2 * n)
                nc.scalar.activation(rrms[:], log_ms[:], ACT.Exp, scale=-0.5).then_inc(rrms_done, 1)

            def exps(g, ch):
                if ch == 0:
                    act.wait_ge(max_done, g + 1)
                    at_least(act, sum_done, g)
                cols = slice(ch * CH, (ch + 1) * CH)
                for q in range(QT):
                    nc.scalar.activation(probs[:, q, cols], probs[:, q, cols], ACT.Exp, bias=negmax[:, q:q + 1],
                                         accum_out=chunk_sum[:, q, ch:ch + 1]).then_inc(exp_done, 1)

            def body(h, has_scores, has_values, has_output):
                g = h - 1
                if has_values:
                    exps(g, 0)
                if has_scores:
                    keys_high(h, 0)
                    keys_rrms(h, 0)
                for ch in range(NCH):
                    if has_values:
                        for q in range(QT):
                            n = 16 * g + 2 * ch + q
                            act.wait_ge(t_done, n + 1)
                            at_least(act, pc_done, n - 1)
                            nc.scalar.activation(pt_hi[:, q, :], t_ps[:, q, :], ACT.Copy).then_inc(pthi_done, 1)
                    if has_scores and ch + 1 < NCH:
                        keys_high(h, ch + 1)
                    if has_values and ch + 1 < NCH:
                        exps(g, ch + 1)
                    if has_scores and ch + 1 < NCH:
                        keys_rrms(h, ch + 1)
                if has_values:
                    act.wait_ge(rinv_done, g + 1)
                    for q in range(QT):
                        act.wait_ge(pc_done, 16 * g + 15 + q)
                        at_least(act, norm_done, 2 * g + q - 1)
                        nc.scalar.activation(low_part[:, q, :], pc_ps[:, q, CD:2 * CD], ACT.Copy,
                                             scale=rinv[:, q:q + 1]).then_inc(lowpart_done, 1)

            heads_loop(act, nc.scalar, body)

        @block.vector
        def _(dve):
            def keys_low(h, ch):
                dve.wait_ge(sq_done, 8 * h + ch + 1)
                at_least(dve, s_done, 16 * h + 2 * ch)
                nc.vector.tensor_tensor(k_lo[:], k_ps[:], k_hi[:].bitcast(F32), ALU.subtract).then_inc(klo_done, 1)

            def body(h, has_scores, has_values, has_output):
                g, o = h - 1, h - 2
                if has_scores:
                    dve.wait_ge(wk_loaded, 16 * h + 16)
                    at_least(dve, k_done, 8 * h)
                    nc.vector.tensor_copy(wk_hi[:], wk_raw[:]).then_inc(wk_split, 1)
                    dve.wait_ge(wk_split, 2 * h + 1)
                    nc.vector.tensor_tensor(wk_lo[:], wk_raw[:], wk_hi[:].bitcast(F32),
                                            ALU.subtract).then_inc(wk_split, 1)
                    at_least(dve, s_done, 16 * h)
                    q_h = qT[:, bass.ds(h * S, S)]
                    nc.vector.tensor_scalar(q_hi[:], q_h, 1.0, None, ALU.mult).then_inc(q_split, 1)
                    dve.wait_ge(q_split, 2 * h + 1)
                    nc.vector.tensor_tensor(q_lo[:], q_h, q_hi[:].bitcast(F32), ALU.subtract).then_inc(q_split, 1)
                    keys_low(h, 0)
                if has_output:
                    dve.wait_ge(pcT_turned, o + 1)
                    at_least(dve, out_done, o)
                    nc.vector.tensor_copy(pcT[:], t_ps[:, 0, :]).then_inc(pcT_done, 1)
                    dve.wait_ge(out_done, o + 1)
                    dve.wait_ge(q_split, 2 * o + 2)
                    nc.vector.tensor_scalar(qT[:, bass.ds(o * S, S)], t_ps[:, 1, 0:S], 1.0, None,
                                            ALU.mult).then_inc(stored, 1)
                for ch in range(NCH):
                    if has_scores:
                        dve.wait_ge(rrms_done, 8 * h + ch + 1)
                        if ch == 0:
                            at_least(dve, max_done, h)
                        for q in range(QT):
                            n = 16 * h + 2 * ch + q
                            dve.wait_ge(s_done, n + 1)
                            at_least(dve, t_done, n - 15)
                            nc.vector.sem_inc(may_score, 1)
                            nc.vector.tensor_tensor_reduce(
                                out=probs[:, q, ch * CH:(ch + 1) * CH], in0=s_ps[:, q, :], in1=rrms[:], scale=1.0,
                                scalar=LOWEST, op0=ALU.mult, op1=ALU.max,
                                accum_out=chunk_max[:, q, ch:ch + 1]).then_inc(scored, 1)
                    if has_values:
                        for q in range(QT):
                            n = 16 * g + 2 * ch + q
                            dve.wait_ge(pthi_done, n + 1)
                            at_least(dve, pc_done, n - 1)
                            nc.vector.tensor_tensor(pt_lo[:, q, :], t_ps[:, q, :], pt_hi[:, q, :].bitcast(F32),
                                                    ALU.subtract).then_inc(ptlo_done, 1)
                    if has_scores and ch + 1 < NCH:
                        keys_low(h, ch + 1)
                if has_scores:
                    dve.wait_ge(scored, 16 * h + 16)
                    at_least(dve, exp_done, 16 * h)
                    nc.vector.tensor_reduce(negmax[:], chunk_max[:], AX_X, ALU.max, negate=True).then_inc(max_done, 1)
                if has_values:
                    dve.wait_ge(exp_done, 16 * g + 16)
                    at_least(dve, lowpart_done, 2 * g)
                    nc.vector.tensor_reduce(rowsum[:], chunk_sum[:], AX_X, ALU.add).then_inc(sum_done, 1)
                    dve.wait_ge(sum_done, g + 1)
                    nc.vector.reciprocal(rinv[:], rowsum[:]).then_inc(rinv_done, 1)
                    dve.wait_ge(rinv_done, g + 1)
                    at_least(dve, pcT_turned, g)
                    for q in range(QT):
                        dve.wait_ge(lowpart_done, 2 * g + q + 1)
                        nc.vector.scalar_tensor_tensor(pc[:, q, :], pc_ps[:, q, 0:CD], rinv[:, q:q + 1],
                                                       low_part[:, q, :], ALU.mult, ALU.add).then_inc(norm_done, 1)

            heads_loop(dve, nc.vector, body)


def output_projection(nc, c, stage, attnT, n_k, w, w_ready, bias_row=None):
    with ExitStack() as ctx:
        t = Tiles(nc, ctx, stage, c["finished"])
        y_ps = t.psum("y_ps", [P, QT, HID])
        y_done = t.sem("y_done")
        block = ctx.enter_context(nc.Block())

        @block.tensor
        def _(pe):
            for n, (sem, value) in enumerate(w_ready):
                pe.wait_ge(sem, value)
                for k in range(n * n_k // len(w_ready), (n + 1) * n_k // len(w_ready)):
                    for q in range(QT):
                        last = nc.tensor.matmul(y_ps[:, q, :], attnT[:, k, q * P:(q + 1) * P], w[:, k, :],
                                                start=(k == 0), stop=(k == n_k - 1 and bias_row is None))
                        if k == n_k - 1:
                            if bias_row is not None:
                                last = nc.tensor.matmul(y_ps[:, q, :], c["ones"][0:1, :], bias_row,
                                                        start=False, stop=True)
                            last.then_inc(y_done, 1)

        @block.vector
        def _(dve):
            for q in range(QT):
                dve.wait_ge(y_done, q + 1)
                nc.vector.tensor_tensor(c["x"][:, q, :], c["x"][:, q, :], y_ps[:, q, :], ALU.add)


def cross_attention_0(nc, T, c, ctxT_hi, ctxT_lo):
    with ExitStack() as ctx:
        t = Tiles(nc, ctx, "layer0cross", c["finished"])
        qT = t.sb("qT", [P, H, S])
        qT_flat = qT[:].rearrange("p h s -> p (h s)")
        with ExitStack() as ctx2:
            t2 = Tiles(nc, ctx2, "layer0cross_in", c["finished"])
            ctx_hl = t2.sb("ctx_hl", [P, NT, 2 * CD], F32R)
            with ExitStack() as ctx3:
                t3 = Tiles(nc, ctx3, "layer0cross_q", c["finished"])
                wq = t3.sb("wq", [P, HC, H * D])
                xnT = t3.sb("xnT", [P, HC, S])
                wq_loaded = [t.sem(f"wq_loaded{i}") for i in range(4)]
                setup_constants(nc, T, c)

                def load_wq(sp):
                    for i in range(4):
                        cols = slice(i * 512, (i + 1) * 512)
                        sp.dma_start(wq[:, :, cols], T["wq0"].rearrange("(k p) n -> p k n", p=P)[:, :, cols])\
                          .then_inc(wq_loaded[i], 16)

                layernorm_transposed(nc, c, "norm0", c["x"], xnT, load_wq)
                cross0_queries(nc, T, c, xnT, qT, ctxT_hi, ctxT_lo, ctx_hl, wq, wq_loaded)
            cross0_attention(nc, T, c, qT_flat, ctxT_hi, ctxT_lo, ctx_hl)
        wo = t.sb("wo", [P, H, HID])
        wo_loaded = [t.sem(f"wo_loaded{i}") for i in range(4)]
        x_loaded = t.sem("x_loaded")
        with nc.Block() as block:
            @block.sync
            def _(sp):
                sp.dma_start(c["x"][:], T["x"].rearrange("(t p) n -> p t n", p=P)).then_inc(x_loaded, 16)
                for i in range(4):
                    sp.dma_start(wo[:, 4 * i:4 * i + 4, :],
                                 T["wo0"].rearrange("(h p) n -> p h n", p=P)[:, 4 * i:4 * i + 4, :])\
                      .then_inc(wo_loaded[i], 16)
                sp.wait_ge(x_loaded, 16)
        output_projection(nc, c, "out0", qT, H, wo, [(s, 16) for s in wo_loaded])


def block_mask(nc, pool, sem, mask, blocks, rows, width):
    n = 0
    for op in range(3):
        if op == 0:
            last = nc.gpsimd.memset(mask[:], 1.0)
        elif op == 1:
            last = nc.gpsimd.affine_select(out=mask[:], in_=mask[:], compare_op=ALU.is_ge, fill=0.0, base=0,
                                           pattern=[[-rows, blocks], [0, width]], channel_multiplier=1)
        else:
            last = nc.gpsimd.affine_select(out=mask[:], in_=mask[:], compare_op=ALU.is_ge, fill=0.0, base=rows - 1,
                                           pattern=[[rows, blocks], [0, width]], channel_multiplier=-1)
        last.then_inc(sem, 1)
        n += 1
        pool.wait_ge(sem, n)


def self_attention_0(nc, T, c):
    KH = 4
    with ExitStack() as ctx:
        t = Tiles(nc, ctx, "self0", c["finished"])
        wq, wk, wv = t.sb("wq", [P, HC, H * D]), t.sb("wk", [P, HC, KH * D]), t.sb("wv", [P, HC, KH * D])
        wo, bo = t.sb("wo", [P, H, HID]), t.sb("bo", [1, HID])
        xnT = t.sb("xnT", [P, HC, S])
        attnT = t.sb("attnT", [P, H, S])
        wk_loaded, wv_loaded, wo_loaded = t.sem("wk_loaded"), t.sem("wv_loaded"), t.sem("wo_loaded")
        wq_loaded = [t.sem(f"wq_loaded{i}") for i in range(4)]

        def load_weights(sp):
            sp.dma_start(wk[:], T["wk_s0"].rearrange("(k p) n -> p k n", p=P)).then_inc(wk_loaded, 16)
            sp.dma_start(wv[:], T["wv_s0"].rearrange("(k p) n -> p k n", p=P)).then_inc(wv_loaded, 16)
            for i in range(4):
                cols = slice(i * 512, (i + 1) * 512)
                sp.dma_start(wq[:, :, cols], T["wq_s0"].rearrange("(k p) n -> p k n", p=P)[:, :, cols])\
                  .then_inc(wq_loaded[i], 16)
            sp.dma_start(wo[:], T["wo_s0"].rearrange("(h p) n -> p h n", p=P)).then_inc(wo_loaded, 16)
            sp.dma_start(bo[:], T["bo_s0"]).then_inc(wo_loaded, 16)

        layernorm_transposed(nc, c, "norm1", c["x"], xnT, load_weights)
        with ExitStack() as ctx2:
            t = Tiles(nc, ctx2, "self0a", c["finished"])
            W = 3 * P
            kT, v = t.sb("kT", [P, KH, S]), t.sb("v", [P, QT, KH * D])
            qT = t.sb("qT", [P, 2, S])
            mask = t.sb("mask", [P, W])
            scores, probsT = t.sb("scores", [P, 2, W]), t.sb("probsT", [P, 2, W])
            negmax, sums, rinv = t.sb("negmax", [P, 2, QT]), t.sb("sums", [P, 2, QT]), t.sb("rinv", [P, 2, QT])
            q_ps, s_ps, t_ps, o_ps = (t.psum(n, [P, 2, CH]) for n in ("q_ps", "s_ps", "t_ps", "o_ps"))
            mask_made, kv_done, kv_copied = t.sem("mask_made"), t.sem("kv_done"), t.sem("kv_copied")
            q_done, q_copied, s_done, masked, max_done, exp_done, rinv_done, normed = map(
                t.sem, ("q_done", "q_copied", "s_done", "masked", "max_done", "exp_done", "rinv_done", "normed"))
            t_done, t_copied, o_done, o_copied = map(t.sem, ("t_done", "t_copied", "o_done", "o_copied"))
            parts = [(0, slice(0, P)), (1, slice(P, W))]
            block = ctx2.enter_context(nc.Block())

            @block.gpsimd
            def _(pool):
                nc.gpsimd.memset(mask[:], 0.0).then_inc(mask_made, 1)
                pool.wait_ge(mask_made, 1)
                for cols in (slice(0, P), slice(2 * P, W)):
                    nc.gpsimd.affine_select(out=mask[:, cols], in_=mask[:, cols], compare_op=ALU.is_ge, fill=LOWEST,
                                            base=0, pattern=[[-1, P]], channel_multiplier=1).then_inc(mask_made, 1)

            @block.tensor
            def _(pe):
                pe.wait_ge(wk_loaded, 16)
                for kh in range(KH):
                    out = s_ps[:, kh // 2, (kh % 2) * S:(kh % 2 + 1) * S]
                    for k in range(HC):
                        last = nc.tensor.matmul(out, wk[:, k, kh * D:(kh + 1) * D], xnT[:, k, :],
                                                start=(k == 0), stop=(k == HC - 1))
                last.then_inc(kv_done, 1)
                pe.wait_ge(wv_loaded, 16)
                for q in range(QT):
                    for k in range(HC):
                        last = nc.tensor.matmul(t_ps[:, q, :], xnT[:, k, q * P:(q + 1) * P], wv[:, k, :],
                                                start=(k == 0), stop=(k == HC - 1))
                last.then_inc(kv_done, 1)
                for i in range(H + 3):
                    if i < H:
                        h = i
                        if h % 4 == 0:
                            pe.wait_ge(wq_loaded[h // 4], 16)
                        at_least(pe, q_copied, h - 1)
                        for k in range(HC):
                            last = nc.tensor.matmul(q_ps[:, h % 2, 0:S], wq[:, k, h * D:(h + 1) * D], xnT[:, k, :],
                                                    start=(k == 0), stop=(k == HC - 1))
                        last.then_inc(q_done, 1)
                    if 0 <= i - 1 < H:
                        h = i - 1
                        pe.wait_ge(q_copied, h + 1)
                        if h == 0:
                            pe.wait_ge(kv_copied, 2)
                        at_least(pe, masked, h - 1)
                        kh = h // (H // KH)
                        nc.tensor.matmul(s_ps[:, h % 2, 0:P], qT[:, h % 2, 0:P], kT[:, kh, 0:P],
                                         start=True, stop=True)
                        nc.tensor.matmul(s_ps[:, h % 2, P:W], qT[:, h % 2, P:S], kT[:, kh, :],
                                         start=True, stop=True).then_inc(s_done, 1)
                    if 0 <= i - 2 < H:
                        h = i - 2
                        pe.wait_ge(normed, 2 * h + 2)
                        at_least(pe, t_copied, h - 1)
                        for j in range(3):
                            last = nc.tensor.transpose(t_ps[:, h % 2, j * P:(j + 1) * P],
                                                       scores[:, h % 2, j * P:(j + 1) * P], c["ident"][:])
                        last.then_inc(t_done, 1)
                    if 0 <= i - 3 < H:
                        h = i - 3
                        kh = h // (H // KH)
                        pe.wait_ge(t_copied, h + 1)
                        at_least(pe, o_copied, h - 1)
                        nc.tensor.matmul(o_ps[:, h % 2, 0:S], v[:, 0, kh * D:(kh + 1) * D], probsT[:, h % 2, 0:S],
                                         start=True, stop=False)
                        nc.tensor.matmul(o_ps[:, h % 2, P:S], v[:, 1, kh * D:(kh + 1) * D], probsT[:, h % 2, S:W],
                                         start=False, stop=True).then_inc(o_done, 1)

            @block.scalar
            def _(act):
                act.wait_ge(kv_done, 1)
                nc.scalar.activation(kT[:].rearrange("p h s -> p (h s)"), s_ps[:].rearrange("p b n -> p (b n)"),
                                     ACT.Copy).then_inc(kv_copied, 1)
                act.wait_ge(kv_done, 2)
                nc.scalar.activation(v[:], t_ps[:], ACT.Copy).then_inc(kv_copied, 1)
                for i in range(H + 3):
                    if i < H:
                        act.wait_ge(q_done, i + 1)
                        at_least(act, s_done, i - 1)
                        nc.scalar.activation(qT[:, i % 2, :], q_ps[:, i % 2, 0:S], ACT.Copy).then_inc(q_copied, 1)
                    if 0 <= i - 1 < H:
                        h = i - 1
                        act.wait_ge(max_done, 2 * h + 2)
                        at_least(act, rinv_done, h - 1)
                        for q, cols in parts:
                            nc.scalar.activation(scores[:, h % 2, cols], scores[:, h % 2, cols], ACT.Exp,
                                                 bias=negmax[:, h % 2, q:q + 1],
                                                 accum_out=sums[:, h % 2, q:q + 1]).then_inc(exp_done, 1)
                    if 0 <= i - 2 < H:
                        h = i - 2
                        act.wait_ge(t_done, h + 1)
                        at_least(act, o_done, h - 1)
                        nc.scalar.activation(probsT[:, h % 2, :], t_ps[:, h % 2, 0:W], ACT.Copy).then_inc(t_copied, 1)

            @block.vector
            def _(dve):
                dve.wait_ge(mask_made, 3)
                for i in range(H + 3):
                    if i < H:
                        h = i
                        dve.wait_ge(s_done, h + 1)
                        at_least(dve, t_done, h - 1)
                        nc.vector.tensor_tensor(scores[:, h % 2, :], s_ps[:, h % 2, 0:W], mask[:],
                                                ALU.add).then_inc(masked, 1)
                        dve.wait_ge(masked, h + 1)
                        at_least(dve, exp_done, 2 * h - 2)
                        for q, cols in parts:
                            nc.vector.tensor_reduce(negmax[:, h % 2, q:q + 1], scores[:, h % 2, cols], AX_X,
                                                    ALU.max, negate=True).then_inc(max_done, 1)
                    if 0 <= i - 1 < H:
                        h = i - 1
                        dve.wait_ge(exp_done, 2 * h + 2)
                        at_least(dve, normed, 2 * h - 2)
                        nc.vector.reciprocal(rinv[:, h % 2, :], sums[:, h % 2, :]).then_inc(rinv_done, 1)
                        dve.wait_ge(rinv_done, h + 1)
                        for q, cols in parts:
                            nc.vector.tensor_scalar(scores[:, h % 2, cols], scores[:, h % 2, cols],
                                                    rinv[:, h % 2, q:q + 1], None, ALU.mult).then_inc(normed, 1)
                    if 0 <= i - 3 < H:
                        h = i - 3
                        dve.wait_ge(o_done, h + 1)
                        nc.vector.tensor_copy(attnT[:, h, :], o_ps[:, h % 2, 0:S]).then_inc(o_copied, 1)
        output_projection(nc, c, "out1", attnT, H, wo, [(wo_loaded, 32)], bo[:])


def feed_forward_0(nc, T, c):
    NI = 16
    E = 8
    with ExitStack() as ctx:
        t = Tiles(nc, ctx, "ffn0", c["finished"])
        up, down = t.sb("up", [P, HC, NI * P]), t.sb("down", [P, NI, HID])
        expert, gate = t.sb("expert", [P, HC, HID]), t.sb("gate", [P, HC, E])
        gamma, beta = t.sb("gamma", [P, HID]), t.sb("beta", [P, HID])
        xnT = t.sb("xnT", [P, HC, S])
        small_loaded, down_loaded = t.sem("small_loaded"), t.sem("down_loaded")
        up_loaded = [t.sem(f"up_loaded{i}") for i in range(4)]

        def load_weights(sp):
            sp.dma_start(gate[:], T["gate"].rearrange("(k p) n -> p k n", p=P)).then_inc(small_loaded, 16)
            sp.dma_start(expert[:], T["expert"].rearrange("(k p) n -> p k n", p=P)).then_inc(small_loaded, 16)
            for i in range(4):
                cols = slice(i * 512, (i + 1) * 512)
                sp.dma_start(up[:, :, cols], T["up"].rearrange("(k p) n -> p k n", p=P)[:, :, cols])\
                  .then_inc(up_loaded[i], 16)
            sp.dma_start(down[:], T["down"].rearrange("(i p) n -> p i n", p=P)).then_inc(down_loaded, 16)
            sp.dma_start(gamma[:], T["gamma"].to_broadcast([P, HID])).then_inc(down_loaded, 16)
            sp.dma_start(beta[:], T["beta"].to_broadcast([P, HID])).then_inc(down_loaded, 16)

        layernorm_transposed(nc, c, "norm2", c["x"], xnT, load_weights)
        with ExitStack() as ctx2:
            t = Tiles(nc, ctx2, "ffn0a", c["finished"])
            relu, hT = t.sb("relu", [P, 2, S]), t.sb("hT", [P, NI, S])
            top, route = t.sb("top", [P, QT, 8]), t.sb("route", [P, QT])
            y = t.sb("y", [P, QT, HID])
            stats, mv = t.sb("stats", [P, QT, 6]), t.sb("mv", [P, QT, 2])
            logvar, rstd = t.sb("logvar", [P, QT]), t.sb("rstd", [P, QT])
            gate_ps, expert_ps = t.psum("gate_ps", [P, QT, E]), t.psum("expert_ps", [P, QT, HID])
            up_ps, y_ps = t.psum("up_ps", [P, 2, CH]), t.psum("y_ps", [P, QT, HID])
            gate_done, up_done, relu_done, h_done, y_done, chain, moments_done, log_done, rstd_done = map(
                t.sem, ("gate_done", "up_done", "relu_done", "h_done", "y_done", "chain", "moments_done",
                        "log_done", "rstd_done"))
            block = ctx2.enter_context(nc.Block())

            @block.tensor
            def _(pe):
                pe.wait_ge(small_loaded, 32)
                for q in range(QT):
                    for k in range(HC):
                        nc.tensor.matmul(gate_ps[:, q, :], xnT[:, k, q * P:(q + 1) * P], gate[:, k, :],
                                         start=(k == 0), stop=(k == HC - 1))
                    for k in range(HC):
                        last = nc.tensor.matmul(expert_ps[:, q, :], xnT[:, k, q * P:(q + 1) * P], expert[:, k, :],
                                                start=(k == 0), stop=(k == HC - 1))
                last.then_inc(gate_done, 1)
                for i in range(NI + 1):
                    if i < NI:
                        if i % 4 == 0:
                            pe.wait_ge(up_loaded[i // 4], 16)
                        at_least(pe, relu_done, i - 1)
                        for k in range(HC):
                            last = nc.tensor.matmul(up_ps[:, i % 2, 0:S], up[:, k, i * P:(i + 1) * P], xnT[:, k, :],
                                                    start=(k == 0), stop=(k == HC - 1))
                        last.then_inc(up_done, 1)
                    if i > 0:
                        if i == 1:
                            pe.wait_ge(down_loaded, 48)
                        pe.wait_ge(h_done, i)
                        for q in range(QT):
                            last = nc.tensor.matmul(y_ps[:, q, :], hT[:, i - 1, q * P:(q + 1) * P], down[:, i - 1, :],
                                                    start=(i == 1), stop=(i == NI))
                last.then_inc(y_done, 1)

            @block.scalar
            def _(act):
                for i in range(NI):
                    act.wait_ge(up_done, i + 1)
                    at_least(act, h_done, i - 1)
                    nc.scalar.activation(relu[:, i % 2, :], up_ps[:, i % 2, 0:S], ACT.Relu).then_inc(relu_done, 1)
                act.wait_ge(moments_done, QT)
                nc.scalar.activation(logvar[:], mv[:, :, 1], ACT.Ln, bias=c["eps5"][:]).then_inc(log_done, 1)
                act.wait_ge(log_done, 1)
                nc.scalar.activation(rstd[:], logvar[:], ACT.Exp, scale=-0.5).then_inc(rstd_done, 1)

            @block.vector
            def _(dve):
                steps = [0]

                def then_wait(instruction):
                    steps[0] += 1
                    instruction.then_inc(chain, 1)
                    dve.wait_ge(chain, steps[0])

                dve.wait_ge(gate_done, 1)
                for q in range(QT):
                    then_wait(nc.vector.max(top[:, q, :], gate_ps[:, q, :]))
                then_wait(nc.vector.tensor_tensor(route[:], top[:, :, 0], top[:, :, 1], ALU.add))
                for i in range(NI):
                    dve.wait_ge(relu_done, i + 1)
                    nc.vector.tensor_tensor(hT[:, i, :], relu[:, i % 2, :], relu[:, i % 2, :],
                                            ALU.mult).then_inc(h_done, 1)
                for q in range(QT):
                    then_wait(nc.vector.tensor_scalar(y[:, q, :], expert_ps[:, q, :], route[:, q:q + 1], None,
                                                      ALU.mult))
                dve.wait_ge(y_done, 1)
                for q in range(QT):
                    then_wait(nc.vector.tensor_tensor(y[:, q, :], y[:, q, :], y_ps[:, q, :], ALU.add))
                for q in range(QT):
                    then_wait(nc.vector.bn_stats(stats[:, q, :], y[:, q, :]))
                for q in range(QT):
                    nc.vector.bn_aggr(mv[:, q, :], stats[:, q, :]).then_inc(moments_done, 1)
                dve.wait_ge(moments_done, QT)
                dve.wait_ge(rstd_done, 1)
                for q in range(QT):
                    then_wait(nc.vector.tensor_scalar(y[:, q, :], y[:, q, :], mv[:, q, 0:1], rstd[:, q:q + 1],
                                                      ALU.subtract, ALU.mult))
                for q in range(QT):
                    then_wait(nc.vector.tensor_tensor(y[:, q, :], y[:, q, :], gamma[:], ALU.mult))
                for q in range(QT):
                    then_wait(nc.vector.tensor_tensor(y[:, q, :], y[:, q, :], beta[:], ALU.add))
                nc.vector.tensor_tensor(c["x"][:], c["x"][:], y[:], ALU.add)


def group_layernorm(nc, dve, then_wait, c, tiles, src, dst, groups, width, sums_ready, rstd_ready):
    total, var_sum, rstd, centered, squares = tiles
    as_groups = lambda a: a.rearrange("p (g w) -> p g w", w=width)
    wide = lambda a: a.unsqueeze(2).to_broadcast([P, groups, width])
    then_wait(nc.vector.tensor_reduce(total, as_groups(src), AX_X, ALU.add))
    then_wait(nc.vector.tensor_scalar(total, total, -1.0 / width, None, ALU.mult))
    then_wait(nc.vector.tensor_tensor(as_groups(centered), as_groups(src), wide(total), ALU.add))
    then_wait(nc.vector.tensor_tensor(squares, centered, centered, ALU.mult))
    nc.vector.tensor_reduce(var_sum, as_groups(squares), AX_X, ALU.add).then_inc(sums_ready, 1)
    dve.wait_ge(rstd_ready, 1)
    then_wait(nc.vector.tensor_tensor(as_groups(dst), as_groups(centered), wide(rstd), ALU.mult))


def group_rstd(nc, act, c, width, var_sum, log_var, rstd, sums_ready, log_done, rstd_ready):
    act.wait_ge(sums_ready, 1)
    nc.scalar.activation(log_var, var_sum, ACT.Ln, bias=c["eps6"][:], scale=1.0 / width).then_inc(log_done, 1)
    act.wait_ge(log_done, 1)
    nc.scalar.activation(rstd, log_var, ACT.Exp, scale=-0.5).then_inc(rstd_ready, 1)


HD = 32
HG = P // HD
NG = H // HG
DCA = 16
MAIN = KV - DCA
SCALE1 = float(HD) ** -0.5


def cross1_queries(nc, T, c, xnT, qT, own, ctxT_hi, ctxT_lo):
    with ExitStack() as ctx:
        t = Tiles(nc, ctx, "queries1", c["finished"])
        wq, bq = t.sb("wq", [P, HC, HID]), t.sb("bq", [1, HID])
        wd, bd = t.sb("wd", [P, CC, 2 * HID]), t.sb("bd", [1, 2 * HID])
        bv = t.sb("bv", [P, HID])
        affine = t.sb("affine", [P, 4])
        mask_k, mask_v = t.sb("mask_k", [P, HG, DCA]), t.sb("mask_v", [P, P // DCA, HD])
        yT = t.sb("yT", [P, CC, P // DCA, DCA])
        q, qn = t.sb("q", [P, QT * HID]), t.sb("qn", [P, QT * HID])
        k, kn = t.sb("k", [P, HID]), t.sb("kn", [P, HID])
        centered, squares = t.sb("centered", [P, QT * HID]), t.sb("squares", [P, QT * HID])
        total, var_sum, log_var, rstd = (t.sb(n, [P, 4 * HID // HD]) for n in ("total", "var_sum", "log_var", "rstd"))
        kT = t.sb("kT", [P, NG, HG * DCA])
        vb = t.sb("vb", [P, 2, 8 * HD])
        prob, probT = t.sb("prob", [P, QT * H * DCA]), t.sb("probT", [P, 4 * P])
        best = t.sb("best", [P, QT * H])
        ps = t.psum("ps", [P, 8, CH])
        loaded, masks_made, mask_k_steps, mask_v_steps = map(
            t.sem, ("loaded", "masks_made", "mask_k_steps", "mask_v_steps"))
        chain, y_made, projected, sums_q, sums_k, log_q, log_k, rstd_q, rstd_k = map(
            t.sem, ("chain", "y_made", "projected", "sums_q", "sums_k", "log_q", "log_k", "rstd_q", "rstd_k"))
        q_normed, k_normed, q_turned, k_turned, operands, scored, shifted, exped, p_normed, p_turned, p_copied, \
            out_done = map(t.sem, ("q_normed", "k_normed", "q_turned", "k_turned", "operands", "scored", "shifted",
                                   "exped", "p_normed", "p_turned", "p_copied", "out_done"))
        block = ctx.enter_context(nc.Block())
        NQ, NK = QT * HID // HD, HID // HD

        @block.sync
        def _(sp):
            sp.dma_start(wq[:], T["wq1"].rearrange("(k p) n -> p k n", p=P)).then_inc(loaded, 16)
            sp.dma_start(wd[:], T["wkv_dca"].rearrange("(k p) n -> p k n", p=P)).then_inc(loaded, 16)
            sp.dma_start(bq[:], T["bq1"]).then_inc(loaded, 16)
            sp.dma_start(bd[:], T["bkv_dca"]).then_inc(loaded, 16)
            sp.dma_start(affine[:], T["affine1"]).then_inc(loaded, 16)
            sp.dma_start(bv[:], T["bv1"].to_broadcast([P, HID])).then_inc(loaded, 16)

        @block.gpsimd
        def _(pool):
            block_mask(nc, pool, mask_k_steps, mask_k, HG, HD, DCA)
            block_mask(nc, pool, mask_v_steps, mask_v, P // DCA, DCA, HD)
            nc.gpsimd.sem_inc(masks_made, 1)

        @block.tensor
        def _(pe):
            pe.wait_ge(loaded, 96)
            for qt in range(QT):
                for kk in range(HC):
                    nc.tensor.matmul(ps[:, qt, :], xnT[:, kk, qt * P:(qt + 1) * P], wq[:, kk, :],
                                     start=(kk == 0), stop=False)
                last = nc.tensor.matmul(ps[:, qt, :], c["ones"][0:1, :], bq[:], start=False, stop=True)
            last.then_inc(projected, 1)
            pe.wait_ge(y_made, CC)
            for part in range(2):
                cols = slice(part * HID, (part + 1) * HID)
                for kk in range(CC):
                    nc.tensor.matmul(ps[:, 2 + part, :], yT[:, kk].rearrange("p r t -> p (r t)"), wd[:, kk, cols],
                                     start=(kk == 0), stop=False)
                last = nc.tensor.matmul(ps[:, 2 + part, :], c["ones"][0:1, :], bd[:, cols], start=False, stop=True)
            last.then_inc(projected, 1)
            pe.wait_ge(q_normed, 1)
            for qt in range(QT):
                for g in range(NG):
                    last = nc.tensor.transpose(ps[:, 4 + qt, g * P:(g + 1) * P],
                                               qn[:, qt * HID + g * P:qt * HID + (g + 1) * P], c["ident"][:])
            last.then_inc(q_turned, 1)
            pe.wait_ge(k_normed, 1)
            for g in range(NG):
                last = nc.tensor.transpose(ps[:, 6, g * P:(g + 1) * P], kn[:, g * P:(g + 1) * P], c["ident"][:])
            last.then_inc(k_turned, 1)
            pe.wait_ge(operands, 1)
            for qt in range(QT):
                for g in range(NG):
                    at = qt * H * DCA + g * HG * DCA
                    last = nc.tensor.matmul(ps[:, 7, at:at + HG * DCA], qT[:, g, qt * P:(qt + 1) * P], kT[:, g, :],
                                            start=True, stop=True)
            last.then_inc(scored, 1)
            pe.wait_ge(p_normed, 1)
            for n in range(4):
                last = nc.tensor.transpose(ps[:, 0, n * P:(n + 1) * P], prob[:, n * P:(n + 1) * P], c["ident"][:])
            last.then_inc(p_turned, 1)
            pe.wait_ge(p_copied, 1)
            for qt in range(QT):
                for half in range(2):
                    last = nc.tensor.matmul(ps[:, 1 + qt, half * S:(half + 1) * S],
                                            probT[:, (2 * qt + half) * P:(2 * qt + half + 1) * P], vb[:, half, :],
                                            start=True, stop=True)
            last.then_inc(out_done, 1)

        @block.scalar
        def _(act):
            group_rstd(nc, act, c, HD, var_sum[:, 0:NQ], log_var[:, 0:NQ], rstd[:, 0:NQ], sums_q, log_q, rstd_q)
            group_rstd(nc, act, c, HD, var_sum[:, NQ:NQ + NK], log_var[:, NQ:NQ + NK], rstd[:, NQ:NQ + NK],
                       sums_k, log_k, rstd_k)
            act.wait_ge(shifted, 1)
            nc.scalar.activation(prob[:], prob[:], ACT.Exp, scale=SCALE1).then_inc(exped, 1)
            act.wait_ge(p_turned, 1)
            nc.scalar.activation(probT[:], ps[:, 0, :], ACT.Copy).then_inc(p_copied, 1)

        @block.vector
        def _(dve):
            steps = [0]

            def then_wait(instruction):
                steps[0] += 1
                instruction.then_inc(chain, 1)
                dve.wait_ge(chain, steps[0])

            for kk in range(CC):
                wide = lambda a: a[:, kk:kk + 1, MAIN:KV].to_broadcast([P, P // DCA, DCA])
                nc.vector.tensor_tensor(yT[:, kk], wide(ctxT_hi).bitcast(F32), wide(ctxT_lo).bitcast(F32),
                                        ALU.add).then_inc(y_made, 1)
            dve.wait_ge(projected, 1)
            for qt in range(QT):
                then_wait(nc.vector.tensor_copy(q[:, qt * HID:(qt + 1) * HID], ps[:, qt, :]))
            group_layernorm(nc, dve, then_wait, c, (total[:, 0:NQ], var_sum[:, 0:NQ], rstd[:, 0:NQ], centered[:],
                                                    squares[:]), q[:], qn[:], NQ, HD, sums_q, rstd_q)
            nc.vector.sem_inc(q_normed, 1)
            dve.wait_ge(projected, 2)
            then_wait(nc.vector.tensor_copy(k[:], ps[:, 2, :]))
            group_layernorm(nc, dve, then_wait, c,
                            (total[:, NQ:NQ + NK], var_sum[:, NQ:NQ + NK], rstd[:, NQ:NQ + NK], centered[:, 0:HID],
                             squares[:, 0:HID]), k[:], kn[:], NK, HD, sums_k, rstd_k)
            nc.vector.sem_inc(k_normed, 1)
            dve.wait_ge(masks_made, 1)
            for half in range(2):
                then_wait(nc.vector.tensor_tensor(vb[:, half, :], ps[:, 3, half * S:(half + 1) * S],
                                                  mask_v[:].rearrange("p b w -> p (b w)"), ALU.mult))
            dve.wait_ge(q_turned, 1)
            for qt in range(QT):
                then_wait(nc.vector.tensor_scalar(qT[:, :, qt * P:(qt + 1) * P],
                                                  ps[:, 4 + qt, :].rearrange("p (g s) -> p g s", g=NG),
                                                  affine[:, 0:1], affine[:, 1:2], ALU.mult, ALU.add))
            dve.wait_ge(k_turned, 1)
            for g in range(NG):
                then_wait(nc.vector.tensor_scalar(kT[:, g, :], ps[:, 6, g * P:g * P + HG * DCA],
                                                  affine[:, 2:3], affine[:, 3:4], ALU.mult, ALU.add))
                then_wait(nc.vector.tensor_tensor(kT[:, g, :], kT[:, g, :], mask_k[:].rearrange("p b w -> p (b w)"),
                                                  ALU.mult))
            nc.vector.sem_inc(operands, 1)
            dve.wait_ge(scored, 1)
            as_groups = lambda a: a.rearrange("p (g w) -> p g w", w=DCA)
            wide = best[:].unsqueeze(2).to_broadcast([P, QT * H, DCA])
            then_wait(nc.vector.tensor_reduce(best[:], as_groups(ps[:, 7, :]), AX_X, ALU.max))
            nc.vector.tensor_tensor(as_groups(prob[:]), as_groups(ps[:, 7, :]), wide, ALU.subtract)\
              .then_inc(shifted, 1)
            dve.wait_ge(exped, 1)
            then_wait(nc.vector.tensor_reduce(best[:], as_groups(prob[:]), AX_X, ALU.add))
            then_wait(nc.vector.reciprocal(best[:], best[:]))
            nc.vector.tensor_tensor(as_groups(prob[:]), as_groups(prob[:]), wide, ALU.mult).then_inc(p_normed, 1)
            dve.wait_ge(out_done, 1)
            for qt in range(QT):
                nc.vector.tensor_tensor(own[:, qt, :], ps[:, 1 + qt, :], bv[:], ALU.add)


def cross1_attention(nc, T, c, qT, attn, ctxT_hi, ctxT_lo):
    NU = NCH
    GW = 2 * HG * HD
    with ExitStack() as ctx:
        t = Tiles(nc, ctx, "cross1", c["finished"])
        w_raw = t.sb("w_raw", [P, CC, GW])
        w_hi, w_lo = t.sb("w_hi", [P, CC, GW], F32R), t.sb("w_lo", [P, CC, GW], F32R)
        bk_raw, bk_hi, bk_lo = t.sb("bk_raw", [1, P]), t.sb("bk_hi", [1, P], F32R), t.sb("bk_lo", [1, P], F32R)
        ones_r = t.sb("ones_r", [1, P], F32R)
        affine = t.sb("affine", [P, 2])
        w_mean, b_mean = t.sb("w_mean", [P, CC * HG]), t.sb("b_mean", [1, HG])
        q_hi, q_lo = t.sb("q_hi", [P, S], F32R), t.sb("q_lo", [P, S], F32R)
        kT_hi, kT_lo = t.sb("kT_hi", [P, KV], F32R), t.sb("kT_lo", [P, KV], F32R)
        v_hl = t.sb("v_hl", [P, NT, HG, 2 * HD], F32R)
        var_sum, log_var, rstd = (t.sb(n, [P, TPC * HG]) for n in ("var_sum", "log_var", "rstd"))
        probs = t.sb("probs", [P, QT, KV])
        squares, kn = probs[:, 0, 0:CH], probs[:, 0, CH:2 * CH]
        k_full = probs[:, 0, 2 * CH:4 * CH].rearrange("p (b n) -> p b n", b=2)
        pt_hi, pt_lo = t.sb("pt_hi", [P, 2, QT, CH], F32R), t.sb("pt_lo", [P, 2, QT, CH], F32R)
        chunk_max, negmax = t.sb("chunk_max", [P, QT, NCH]), t.sb("negmax", [P, QT])
        chunk_sum, rowsum, rinv = t.sb("chunk_sum", [P, QT, NCH]), t.sb("rowsum", [P, QT]), t.sb("rinv", [P, QT])
        outT = t.sb("outT", [P, S])
        low_part = t.sb("low_part", [P, QT, HD])
        ps = t.psum("ps", [P, 8, CH])
        kv_ps = [ps[:, 2 * b:2 * b + 2, :].rearrange("p b (t n) -> p (b t) n", n=GW) for b in range(2)]
        w_loaded, const_loaded, prepared, w_ready, q_ready = map(
            t.sem, ("w_loaded", "const_loaded", "prepared", "w_ready", "q_ready"))
        kv_done, sq_done, vhi_done, sums_done, log_done, rstd_done, kn_done, vlo_done = map(
            t.sem, ("kv_done", "sq_done", "vhi_done", "sums_done", "log_done", "rstd_done", "kn_done", "vlo_done"))
        kt_done, khi_done, kfull_done, klo_done = map(t.sem, ("kt_done", "khi_done", "kfull_done", "klo_done"))
        s_done, scored, exp_done, t_done, pthi_done, ptlo_done = map(
            t.sem, ("s_done", "scored", "exp_done", "t_done", "pthi_done", "ptlo_done"))
        o_done = t.sem("o_done")
        max_done, sum_done, rinv_done, outT_done, turned_back, lowpart_done, norm_done, chain_w = map(
            t.sem, ("max_done", "sum_done", "rinv_done", "outT_done", "turned_back", "lowpart_done", "norm_done",
                    "chain_w"))
        block = ctx.enter_context(nc.Block())

        def groups_loop(nc_engine, body):
            body(0)
            with nc_engine.Fori(1, NG) as g:
                body(g)

        def width(ch):
            return min(CH, MAIN - ch * CH)

        @block.sync
        def _(sp):
            sp.dma_start(affine[:], T["affine_k1"]).then_inc(const_loaded, 16)

            def body(g):
                at_least(sp, w_ready, g)
                sp.dma_start(w_raw[:].rearrange("p k n -> p (k n)"), T["wkv1"][bass.ds(g * P, P), :])\
                  .then_inc(w_loaded, 16)
                sp.dma_start(bk_raw[:], T["bk1"][0:1, bass.ds(g * P, P)]).then_inc(w_loaded, 16)

            groups_loop(nc.sync, body)

        @block.gpsimd
        def _(pool):
            nc.gpsimd.memset(probs[:, :, MAIN:KV], 0.0).then_inc(prepared, 1)

            def body(g):
                for u in range(NU):
                    n = NU * g + u
                    cols = slice(u * CH, (u + 1) * CH)
                    pool.wait_ge(kfull_done, n + 1)
                    nc.gpsimd.tensor_tensor(kT_lo[:, cols], k_full[:, u % 2, :], kT_hi[:, cols].bitcast(F32),
                                            ALU.subtract).then_inc(klo_done, 1)

            groups_loop(nc.gpsimd, body)

        @block.tensor
        def _(pe):
            def keys_values(g, u):
                n = NU * g + u
                if u < 2:
                    if u == 0:
                        pe.wait_ge(w_ready, g + 1)
                        pe.wait_ge(prepared, 2)
                else:
                    pe.wait_ge(kn_done, n - 1)
                    pe.wait_ge(vlo_done, n - 1)
                for j in range(TPC):
                    out = kv_ps[u % 2][:, j, :]
                    tile = slice((u * TPC + j) * P, (u * TPC + j + 1) * P)
                    for k in range(CC):
                        nc.tensor.matmul(out, ctxT_hi[:, k, tile], w_hi[:, k, :], start=(k == 0), stop=False)
                        nc.tensor.matmul(out, ctxT_hi[:, k, tile], w_lo[:, k, :], start=False, stop=False)
                        nc.tensor.matmul(out, ctxT_lo[:, k, tile], w_hi[:, k, :], start=False, stop=False)
                    nc.tensor.matmul(out[:, 0:P], ones_r[:], bk_hi[:], start=False, stop=False)
                    last = nc.tensor.matmul(out[:, 0:P], ones_r[:], bk_lo[:], start=False, stop=True)
                last.then_inc(kv_done, 1)

            def turn_keys(g, u):
                n = NU * g + u
                pe.wait_ge(kn_done, n + 1)
                if u >= 2:
                    pe.wait_ge(kfull_done, n - 1)
                elif u == 0:
                    at_least(pe, norm_done, 2 * HG * g)
                for j in range(TPC):
                    last = nc.tensor.transpose(ps[:, 4 + u % 2, j * P:(j + 1) * P], kn[:, j * P:(j + 1) * P],
                                               c["ident"][:])
                last.then_inc(kt_done, 1)

            def scores(g, j, ch):
                rows = slice(j * HD, (j + 1) * HD)
                cols = slice(ch * CH, ch * CH + width(ch))
                h = HG * g + j
                if j == 0 and ch == 0:
                    pe.wait_ge(q_ready, 2 * g + 2)
                if j == 0:
                    pe.wait_ge(klo_done, NU * g + ch + 1)
                for q in range(QT):
                    at_least(pe, scored, 16 * h + 2 * ch + q - 1)
                    out = ps[:, 6 + q, 0:width(ch)]
                    tokens = slice(q * P, (q + 1) * P)
                    nc.tensor.matmul(out, q_hi[rows, tokens], kT_hi[rows, cols], start=True, stop=False)
                    nc.tensor.matmul(out, q_hi[rows, tokens], kT_lo[rows, cols], start=False, stop=False)
                    nc.tensor.matmul(out, q_lo[rows, tokens], kT_hi[rows, cols],
                                     start=False, stop=True).then_inc(s_done, 1)

            def transposes(g, j, ch):
                for q in range(QT):
                    pe.wait_ge(exp_done, 16 * (HG * g + j) + 2 * ch + q + 1)
                    for i in range(TPC):
                        at = ch * CH + i * P
                        last = nc.tensor.transpose(ps[:, 2 * (ch % 2) + q, i * P:(i + 1) * P], probs[:, q, at:at + P],
                                                   c["ident"][:])
                    last.then_inc(t_done, 1)

            def values(g, j, ch):
                h = HG * g + j
                n = 16 * h + 2 * ch
                pe.wait_ge(pthi_done, n + 2)
                pe.wait_ge(ptlo_done, n + 2)
                if ch == 0:
                    at_least(pe, norm_done, 2 * h - 2)
                if ch == 0 and j == 0:
                    pe.wait_ge(kfull_done, NU * g + NU)
                    pe.wait_ge(vlo_done, NU * g + NU)
                out = ps[:, 4 + j % 2, 0:S].rearrange("p (q t) -> p q t", q=QT)
                heads = slice(j - j % 2, j - j % 2 + 2)
                for i in range(TPC):
                    tile, cols = ch * TPC + i, slice(i * P, (i + 1) * P)
                    v = v_hl[:, tile, heads, :].rearrange("p h n -> p (h n)")
                    nc.tensor.matmul(out, v, pt_hi[:, ch % 2, :, cols], start=(tile == 0), stop=False)
                    last = nc.tensor.matmul(out, v, pt_lo[:, ch % 2, :, cols], start=False, stop=(tile == NT - 1))
                last.then_inc(o_done, 1)

            def turn_back(g, j):
                pe.wait_ge(outT_done, HG * g + j + 1)
                for q in range(QT):
                    last = nc.tensor.transpose(ps[:, 4 + j % 2, S + q * P:S + (q + 1) * P],
                                               outT[:, q * P:(q + 1) * P], c["ident"][:])
                last.then_inc(turned_back, 1)

            def body(g):
                for u in range(NU + 1):
                    if u < NU:
                        keys_values(g, u)
                    if u > 0:
                        turn_keys(g, u - 1)
                for j in range(HG + 1):
                    for ch in range(NCH):
                        if j < HG:
                            scores(g, j, ch)
                        if j > 0:
                            transposes(g, j - 1, ch)
                            if ch > 0:
                                values(g, j - 1, ch - 1)
                        if j > 1 and ch == 1:
                            turn_back(g, j - 2)
                    if j > 0:
                        values(g, j - 1, NCH - 1)
                turn_back(g, HG - 1)

            groups_loop(nc.tensor, body)

        @block.scalar
        def _(act):
            nc.scalar.activation(ones_r[:], c["ones"][0:1, :], ACT.Copy).then_inc(prepared, 1)
            act.wait_ge(const_loaded, 16)

            def exps(h, ch):
                if ch == 0:
                    act.wait_ge(max_done, h + 1)
                    at_least(act, sum_done, h)
                cols = slice(ch * CH, ch * CH + width(ch))
                for q in range(QT):
                    nc.scalar.activation(probs[:, q, cols], probs[:, q, cols], ACT.Exp, bias=negmax[:, q:q + 1],
                                         accum_out=chunk_sum[:, q, ch:ch + 1]).then_inc(exp_done, 1)

            def low_parts(g, j):
                h = HG * g + j
                act.wait_ge(turned_back, h + 1)
                act.wait_ge(rinv_done, h + 1)
                at = S + j % 2 * 2 * HD + HD
                for q in range(QT):
                    at_least(act, norm_done, 2 * h + q - 1)
                    nc.scalar.activation(low_part[:, q, :], ps[:, 4 + j % 2, at + q * P:at + q * P + HD], ACT.Copy,
                                         scale=rinv[:, q:q + 1]).then_inc(lowpart_done, 1)

            def body(g):
                for u in range(NU + 1):
                    if u < NU:
                        n = NU * g + u
                        act.wait_ge(kv_done, n + 1)
                        at_least(act, sums_done, n)
                        if u == 0:
                            at_least(act, t_done, 64 * g)
                        keys = kv_ps[u % 2][:, :, 0:P]
                        nc.scalar.activation(squares.rearrange("p (t n) -> p t n", t=TPC), keys,
                                             ACT.Square).then_inc(sq_done, 1)
                        if u == 0:
                            at_least(act, o_done, 32 * g)
                        tiles = slice(u * TPC, (u + 1) * TPC)
                        nc.scalar.activation(v_hl[:, tiles, :, 0:HD],
                                             kv_ps[u % 2][:, :, P:2 * P].rearrange("p t (h d) -> p t h d", h=HG),
                                             ACT.Copy).then_inc(vhi_done, 1)
                        act.wait_ge(sums_done, n + 1)
                        at_least(act, rstd_done, n)
                        nc.scalar.activation(log_var[:], var_sum[:], ACT.Ln, bias=c["eps6"][:],
                                             scale=1.0 / HD).then_inc(log_done, 1)
                        act.wait_ge(log_done, n + 1)
                        at_least(act, kn_done, n)
                        nc.scalar.activation(rstd[:], log_var[:], ACT.Exp, scale=-0.5).then_inc(rstd_done, 1)
                    if u > 0:
                        n = NU * g + u - 1
                        cols = slice((u - 1) * CH, u * CH)
                        act.wait_ge(kt_done, n + 1)
                        if u == 1:
                            at_least(act, s_done, 64 * g)
                        nc.scalar.activation(kT_hi[:, cols], ps[:, 4 + (u - 1) % 2, :], ACT.Identity,
                                             bias=affine[:, 1:2], scale=affine[:, 0:1]).then_inc(khi_done, 1)
                for j in range(1, HG + 1):
                    h = HG * g + j - 1
                    exps(h, 0)
                    for ch in range(NCH):
                        for q in range(QT):
                            n = 16 * h + 2 * ch + q
                            act.wait_ge(t_done, n + 1)
                            at_least(act, o_done, 8 * h + ch - 1)
                            nc.scalar.activation(pt_hi[:, ch % 2, q, :], ps[:, 2 * (ch % 2) + q, :],
                                                 ACT.Copy).then_inc(pthi_done, 1)
                        if ch + 1 < NCH:
                            exps(h, ch + 1)
                        if j > 1 and ch == 1:
                            low_parts(g, j - 2)
                    act.wait_ge(o_done, 8 * h + 8)
                    at_least(act, turned_back, h)
                    nc.scalar.activation(outT[:], ps[:, 4 + (j - 1) % 2, 0:S], ACT.Copy).then_inc(outT_done, 1)
                low_parts(g, HG - 1)

            groups_loop(nc.scalar, body)

        @block.vector
        def _(dve):
            def normalise(g, j):
                h = HG * g + j
                at = S + j % 2 * 2 * HD
                dve.wait_ge(rinv_done, h + 1)
                dve.wait_ge(lowpart_done, 2 * h + 2)
                for q in range(QT):
                    nc.vector.scalar_tensor_tensor(attn[:, bass.ds(q * HID + g * P + j * HD, HD)],
                                                   ps[:, 4 + j % 2, at + q * P:at + q * P + HD], rinv[:, q:q + 1],
                                                   low_part[:, q, :], ALU.mult, ALU.add).then_inc(norm_done, 1)

            def body(g):
                steps = [0]

                def then_wait(instruction):
                    steps[0] += 1
                    instruction.then_inc(chain_w, 1)
                    dve.wait_ge(chain_w, 10 * g + steps[0])

                dve.wait_ge(w_loaded, 32 * g + 32)
                at_least(dve, kv_done, NU * g)
                keys = w_raw[:, :, 0:P].rearrange("p k (h d) -> p k h d", h=HG)
                mean = w_mean[:].rearrange("p (k h) -> p k h", h=HG)
                bias = bk_raw[:].rearrange("p (h d) -> p h d", h=HG)
                then_wait(nc.vector.tensor_reduce(mean, keys, AX_X, ALU.add))
                then_wait(nc.vector.tensor_reduce(b_mean[:], bias, AX_X, ALU.add))
                then_wait(nc.vector.tensor_scalar(w_mean[:], w_mean[:], -1.0 / HD, None, ALU.mult))
                then_wait(nc.vector.tensor_scalar(b_mean[:], b_mean[:], -1.0 / HD, None, ALU.mult))
                then_wait(nc.vector.tensor_tensor(keys, keys, mean.unsqueeze(3).to_broadcast([P, CC, HG, HD]),
                                                  ALU.add))
                then_wait(nc.vector.tensor_tensor(bias, bias, b_mean[:].unsqueeze(2).to_broadcast([1, HG, HD]),
                                                  ALU.add))
                then_wait(nc.vector.tensor_copy(w_hi[:], w_raw[:]))
                then_wait(nc.vector.tensor_copy(bk_hi[:], bk_raw[:]))
                then_wait(nc.vector.tensor_tensor(bk_lo[:], bk_raw[:], bk_hi[:].bitcast(F32), ALU.subtract))
                then_wait(nc.vector.tensor_tensor(w_lo[:], w_raw[:], w_hi[:].bitcast(F32), ALU.subtract))
                assert steps[0] == 10
                nc.vector.sem_inc(w_ready, 1)
                at_least(dve, s_done, 64 * g)
                q_g = qT[:, bass.ds(g * S, S)]
                nc.vector.tensor_scalar(q_hi[:], q_g, 1.0, None, ALU.mult).then_inc(q_ready, 1)
                dve.wait_ge(q_ready, 2 * g + 1)
                nc.vector.tensor_tensor(q_lo[:], q_g, q_hi[:].bitcast(F32), ALU.subtract).then_inc(q_ready, 1)
                for u in range(NU + 1):
                    if u < NU:
                        n = NU * g + u
                        dve.wait_ge(sq_done, n + 1)
                        at_least(dve, log_done, n)
                        nc.vector.tensor_reduce(var_sum[:], squares.rearrange("p (n d) -> p n d", d=HD), AX_X,
                                                ALU.add).then_inc(sums_done, 1)
                        dve.wait_ge(vhi_done, n + 1)
                        tiles = slice(u * TPC, (u + 1) * TPC)
                        nc.vector.tensor_tensor(
                            v_hl[:, tiles, :, HD:2 * HD],
                            kv_ps[u % 2][:, :, P:2 * P].rearrange("p t (h d) -> p t h d", h=HG),
                            v_hl[:, tiles, :, 0:HD].bitcast(F32), ALU.subtract).then_inc(vlo_done, 1)
                        dve.wait_ge(rstd_done, n + 1)
                        at_least(dve, kt_done, n)
                        nc.vector.tensor_tensor(
                            kn.rearrange("p (t h d) -> p t h d", t=TPC, h=HG),
                            kv_ps[u % 2][:, :, 0:P].rearrange("p t (h d) -> p t h d", h=HG),
                            rstd[:].rearrange("p (t h) -> p t h", t=TPC).unsqueeze(3).to_broadcast([P, TPC, HG, HD]),
                            ALU.mult).then_inc(kn_done, 1)
                    if u > 0:
                        n = NU * g + u - 1
                        dve.wait_ge(khi_done, n + 1)
                        at_least(dve, klo_done, n - 1)
                        nc.vector.tensor_scalar(k_full[:, (u - 1) % 2, :], ps[:, 4 + (u - 1) % 2, :], affine[:, 0:1],
                                                affine[:, 1:2], ALU.mult, ALU.add).then_inc(kfull_done, 1)
                for j in range(HG + 1):
                    h, before = HG * g + j, HG * g + j - 1
                    for ch in range(NCH):
                        if j < HG:
                            if ch == 0:
                                at_least(dve, max_done, h)
                            if ch == 0 and j == 0:
                                dve.wait_ge(klo_done, NU * g + NU)
                                dve.wait_ge(kt_done, NU * g + NU)
                            for q in range(QT):
                                n = 16 * h + 2 * ch + q
                                dve.wait_ge(s_done, n + 1)
                                at_least(dve, t_done, n - 15)
                                nc.vector.tensor_scalar(probs[:, q, ch * CH:ch * CH + width(ch)],
                                                        ps[:, 6 + q, 0:width(ch)], SCALE1, None, ALU.mult, ALU.max,
                                                        accum_out=chunk_max[:, q, ch:ch + 1]).then_inc(scored, 1)
                        if j > 0:
                            for q in range(QT):
                                n = 16 * before + 2 * ch + q
                                dve.wait_ge(pthi_done, n + 1)
                                at_least(dve, o_done, 8 * before + ch - 1)
                                nc.vector.tensor_tensor(pt_lo[:, ch % 2, q, :], ps[:, 2 * (ch % 2) + q, :],
                                                        pt_hi[:, ch % 2, q, :].bitcast(F32),
                                                        ALU.subtract).then_inc(ptlo_done, 1)
                        if j > 1 and ch == 1:
                            normalise(g, j - 2)
                    if j < HG:
                        dve.wait_ge(scored, 16 * h + 16)
                        at_least(dve, exp_done, 16 * h)
                        nc.vector.tensor_reduce(negmax[:], chunk_max[:], AX_X, ALU.max, negate=True)\
                          .then_inc(max_done, 1)
                    if j > 0:
                        dve.wait_ge(exp_done, 16 * before + 16)
                        at_least(dve, lowpart_done, 2 * before)
                        nc.vector.tensor_reduce(rowsum[:], chunk_sum[:], AX_X, ALU.add).then_inc(sum_done, 1)
                        dve.wait_ge(sum_done, before + 1)
                        nc.vector.reciprocal(rinv[:], rowsum[:]).then_inc(rinv_done, 1)
                normalise(g, HG - 1)

            groups_loop(nc.vector, body)


def transpose_tokens(nc, c, stage, parts, outT):
    with ExitStack() as ctx:
        t = Tiles(nc, ctx, stage, c["finished"])
        turned = t.psum("turned", [P, QT, HID])
        summed, transposed = t.sem("summed"), t.sem("transposed")
        block = ctx.enter_context(nc.Block())

        @block.vector
        def _(dve):
            for q in range(QT):
                if len(parts) == 2:
                    nc.vector.tensor_tensor(parts[0][:, q, :], parts[0][:, q, :], parts[1][:, q, :],
                                            ALU.add).then_inc(summed, 1)
                else:
                    nc.vector.sem_inc(summed, 1)

        @block.tensor
        def _(pe):
            for q in range(QT):
                pe.wait_ge(summed, q + 1)
                for k in range(HC):
                    last = nc.tensor.transpose(turned[:, q, k * P:(k + 1) * P], parts[0][:, q, k * P:(k + 1) * P],
                                               c["ident"][:])
                last.then_inc(transposed, 1)

        @block.scalar
        def _(act):
            for q in range(QT):
                act.wait_ge(transposed, q + 1)
                nc.scalar.activation(outT[:, :, q * P:(q + 1) * P],
                                     turned[:, q, :].rearrange("p (k t) -> p k t", k=HC), ACT.Copy)


def cross_attention_1(nc, T, c, ctxT_hi, ctxT_lo):
    with ExitStack() as ctx:
        t = Tiles(nc, ctx, "layer1cross", c["finished"])
        qT = t.sb("qT", [P, NG, S])
        own = t.sb("own", [P, QT, HID])
        attn = t.sb("attn", [P, QT, HID])
        with ExitStack() as ctx2:
            xnT = Tiles(nc, ctx2, "layer1cross_in", c["finished"]).sb("xnT", [P, HC, S])
            layernorm_transposed(nc, c, "norm3", c["x"], xnT)
            cross1_queries(nc, T, c, xnT, qT, own, ctxT_hi, ctxT_lo)
        cross1_attention(nc, T, c, qT[:].rearrange("p g s -> p (g s)"), attn[:].rearrange("p q n -> p (q n)"),
                         ctxT_hi, ctxT_lo)
        wo, bo = t.sb("wo", [P, HC, HID]), t.sb("bo", [1, HID])
        attnT = t.sb("attnT", [P, HC, S])
        wo_loaded = t.sem("wo_loaded")
        with nc.Block() as block:
            @block.sync
            def _(sp):
                sp.dma_start(wo[:], T["wo1"].rearrange("(k p) n -> p k n", p=P)).then_inc(wo_loaded, 16)
                sp.dma_start(bo[:], T["bo1"]).then_inc(wo_loaded, 16)
        transpose_tokens(nc, c, "turn3", (attn, own), attnT)
        output_projection(nc, c, "out3", attnT, HC, wo, [(wo_loaded, 32)], bo[:])


TOPK = 64
PREFIX = 4
MASKED = -1.5e38
REPLACED = -float(2 ** 127)


def self_attention_1(nc, T, c):
    SK = S + PREFIX
    WIDTH = (P + PREFIX, SK)
    with ExitStack() as ctx:
        t = Tiles(nc, ctx, "self1", c["finished"])
        w = {n: t.sb(n, [P, HC, HID]) for n in ("wq", "wk", "wv", "wo")}
        rows = t.sb("rows", [1, 2, HID])
        cols = t.sb("cols", [P, 2, HC])
        pv = t.sb("pv", [PREFIX, HID])
        kT = t.sb("kT", [P, NG, SK])
        xnT = t.sb("xnT", [P, HC, S])
        attn, attnT = t.sb("attn", [P, QT, HID]), t.sb("attnT", [P, HC, S])
        small_loaded, loaded = t.sem("small_loaded"), [t.sem(f"loaded{i}") for i in range(4)]

        def load_weights(sp):
            for sem, (name, tile) in zip(loaded, w.items()):
                sp.dma_start(tile[:], T[name + "_s1"].rearrange("(k p) n -> p k n", p=P)).then_inc(sem, 16)
            sp.dma_start(rows[:], T["rows_s1"]).then_inc(small_loaded, 16)
            sp.dma_start(cols[:], T["cols_s1"]).then_inc(small_loaded, 16)
            sp.dma_start(pv[:], T["pv"]).then_inc(small_loaded, 16)
            sp.dma_start(kT[:, :, S:SK], T["pkT"]).then_inc(small_loaded, 16)

        layernorm_transposed(nc, c, "norm4", c["x"], xnT, load_weights)
        with ExitStack() as ctx2:
            t = Tiles(nc, ctx2, "self1a", c["finished"])
            qT, v = t.sb("qT", [P, NG, S]), t.sb("v", [P, QT, HID])
            mask = t.sb("mask", [P, QT, SK])
            scores, work, probs = (t.sb(n, [P, 2, SK]) for n in ("scores", "work", "probs"))
            top = t.sb("top", [P, 2, TOPK // 8, 8])
            negmax, sums, rinv = t.sb("negmax", [P, 2]), t.sb("sums", [P, 2]), t.sb("rinv", [P, 2])
            probsT = t.sb("probsT", [P, 2, 3 * P])
            qk_ps, s_ps, t_ps, o_ps = (t.psum(n, [P, 2, CH]) for n in ("qk_ps", "s_ps", "t_ps", "o_ps"))
            mask_made, proj_done, proj_read, s_done, chain, masked, max_done, exp_done, normed, t_done, t_copied, \
                o_done, search_done = map(t.sem, (
                    "mask_made", "proj_done", "proj_read", "s_done", "chain", "masked", "max_done", "exp_done",
                    "normed", "t_done", "t_copied", "o_done", "search_done"))
            units = [(h, q) for h in range(H) for q in range(QT)]
            block = ctx2.enter_context(nc.Block())

            @block.gpsimd
            def _(pool):
                nc.gpsimd.memset(mask[:], 0.0).then_inc(mask_made, 1)
                pool.wait_ge(mask_made, 1)
                for q in range(QT):
                    nc.gpsimd.affine_select(out=mask[:, q, :], in_=mask[:, q, :], compare_op=ALU.is_ge, fill=MASKED,
                                            base=q * P + PREFIX, pattern=[[-1, SK]],
                                            channel_multiplier=1).then_inc(mask_made, 1)

            @block.tensor
            def _(pe):
                for n, (name, sem) in enumerate(zip(("wq", "wk"), loaded)):
                    pe.wait_ge(sem, 16)
                    for g in range(NG):
                        i = n * NG + g
                        at_least(pe, proj_read, i - 1)
                        for k in range(HC):
                            last = nc.tensor.matmul(qk_ps[:, i % 2, 0:S], w[name][:, k, g * P:(g + 1) * P],
                                                    xnT[:, k, :], start=(k == 0), stop=(k == HC - 1))
                        last.then_inc(proj_done, 1)
                pe.wait_ge(loaded[2], 16)
                pe.wait_ge(small_loaded, 64)
                for q in range(QT):
                    for k in range(HC):
                        nc.tensor.matmul(o_ps[:, q, :], xnT[:, k, q * P:(q + 1) * P], w["wv"][:, k, :],
                                         start=(k == 0), stop=False)
                    nc.tensor.matmul(o_ps[:, q, :], c["ones"][0:1, :], rows[:, 0, :],
                                     start=False, stop=True).then_inc(proj_done, 1)
                for i in range(len(units) + 2):
                    if i < len(units):
                        h, q = units[i]
                        if i == 0:
                            pe.wait_ge(proj_read, 2 * NG)
                        at_least(pe, masked, i - 1)
                        r, g = slice(h % HG * HD, (h % HG + 1) * HD), h // HG
                        nc.tensor.matmul(s_ps[:, i % 2, 0:WIDTH[q]], qT[r, g, q * P:(q + 1) * P],
                                         kT[r, g, 0:WIDTH[q]], start=True, stop=True).then_inc(s_done, 1)
                    if 0 <= i - 1 < len(units):
                        n = i - 1
                        h, q = units[n]
                        pe.wait_ge(normed, n + 1)
                        at_least(pe, t_copied, n - 1)
                        for j, at in enumerate(range(0, WIDTH[q], P)):
                            m = min(P, WIDTH[q] - at)
                            last = nc.tensor.transpose(t_ps[0:m, n % 2, j * P:(j + 1) * P],
                                                       probs[:, n % 2, at:at + m], c["ident"][:])
                        last.then_inc(t_done, 1)
                    if 0 <= i - 2 < len(units):
                        n = i - 2
                        h, q = units[n]
                        pe.wait_ge(t_copied, n + 1)
                        if n == 0:
                            pe.wait_ge(proj_read, 2 * NG + 2)
                        at, out = slice(h * HD, (h + 1) * HD), o_ps[:, q, h * HD:(h + 1) * HD]
                        full = WIDTH[q] // P
                        for j in range(full):
                            nc.tensor.matmul(out, probsT[:, n % 2, j * P:(j + 1) * P], v[:, j, at],
                                             start=(j == 0), stop=False)
                        rest = v[0:PREFIX, 1, at] if q == 0 else pv[:, at]
                        nc.tensor.matmul(out, probsT[0:PREFIX, n % 2, full * P:(full + 1) * P], rest,
                                         start=False, stop=True).then_inc(o_done, 1)

            @block.scalar
            def _(act):
                act.wait_ge(small_loaded, 64)
                for i in range(2 * NG):
                    n, g = i // NG, i % NG
                    act.wait_ge(proj_done, i + 1)
                    target = qT[:, g, :] if n == 0 else kT[:, g, 0:S]
                    nc.scalar.activation(target, qk_ps[:, i % 2, 0:S], ACT.Identity,
                                         bias=cols[:, n, g:g + 1]).then_inc(proj_read, 1)
                for q in range(QT):
                    act.wait_ge(proj_done, 2 * NG + q + 1)
                    nc.scalar.activation(v[:, q, :], o_ps[:, q, :], ACT.Copy).then_inc(proj_read, 1)
                for i in range(len(units) + 1):
                    if i < len(units):
                        h, q = units[i]
                        act.wait_ge(max_done, i + 1)
                        at_least(act, normed, i - 1)
                        at_least(act, t_done, i - 1)
                        nc.scalar.activation(probs[:, i % 2, 0:WIDTH[q]], scores[:, i % 2, 0:WIDTH[q]], ACT.Exp,
                                             bias=negmax[:, i % 2:i % 2 + 1]).then_inc(exp_done, 1)
                    if i > 0:
                        n = i - 1
                        q = units[n][1]
                        act.wait_ge(t_done, n + 1)
                        at_least(act, o_done, n - 1)
                        full = WIDTH[q] // P
                        nc.scalar.activation(probsT[:, n % 2, 0:full * P], t_ps[:, n % 2, 0:full * P], ACT.Copy)
                        at = slice(full * P, (full + 1) * P)
                        nc.scalar.activation(probsT[0:PREFIX, n % 2, at], t_ps[0:PREFIX, n % 2, at],
                                             ACT.Copy).then_inc(t_copied, 1)

            @block.vector
            def _(dve):
                steps = [0]

                def then_wait(instruction):
                    steps[0] += 1
                    instruction.then_inc(chain, 1)
                    dve.wait_ge(chain, steps[0])

                dve.wait_ge(mask_made, 3)
                for i, (h, q) in enumerate(units):
                    b, W = i % 2, WIDTH[q]
                    dve.wait_ge(s_done, i + 1)
                    at_least(dve, exp_done, i - 1)
                    nc.vector.scalar_tensor_tensor(scores[:, b, 0:W], s_ps[:, b, 0:W], SCALE1, mask[:, q, 0:W],
                                                   ALU.mult, ALU.add).then_inc(masked, 1)
                    dve.wait_ge(masked, i + 1)
                    for r in range(TOPK // 8):
                        source = scores if r == 0 else work
                        then_wait(nc.vector.max(top[:, b, r, :], source[:, b, 0:W]))
                        if r == 0:
                            nc.vector.tensor_scalar(negmax[:, b:b + 1], top[:, b, 0, 0:1], -1.0, None,
                                                    ALU.mult).then_inc(max_done, 1)
                        then_wait(nc.vector.match_replace(work[:, b, 0:W], top[:, b, r, :], source[:, b, 0:W],
                                                          REPLACED))
                    dve.wait_ge(exp_done, i + 1)
                    then_wait(nc.vector.scalar_tensor_tensor(probs[:, b, 0:W], work[:, b, 0:W], REPLACED,
                                                             probs[:, b, 0:W], ALU.is_equal, ALU.mult,
                                                             accum_out=sums[:, b:b + 1]))
                    then_wait(nc.vector.reciprocal(rinv[:, b:b + 1], sums[:, b:b + 1]))
                    nc.vector.tensor_scalar(probs[:, b, 0:W], probs[:, b, 0:W], rinv[:, b:b + 1], None,
                                            ALU.mult).then_inc(normed, 1)
                dve.wait_ge(o_done, len(units))
                for q in range(QT):
                    nc.vector.tensor_copy(attn[:, q, :], o_ps[:, q, :])
        transpose_tokens(nc, c, "turn4", (attn,), attnT)
        output_projection(nc, c, "out4", attnT, HC, w["wo"], [(loaded[3], 16)], rows[:, 1, :])


ROUND = 12582912.0


def feed_forward_1(nc, T, c):
    INNER = 2048
    NI = INNER // P
    with ExitStack() as ctx:
        t = Tiles(nc, ctx, "ffn1", c["finished"])
        w1, w2 = t.sb("w1", [P, HC, INNER]), t.sb("w2", [P, NI, HID])
        w1q, w2q = t.sb("w1q", [P, HC, INNER], BF16), t.sb("w2q", [P, NI, HID], BF16)
        b1, b2 = t.sb("b1", [P, INNER]), t.sb("b2", [P, HID])
        h = t.sb("h", [P, QT, INNER])
        hq = t.sb("hq", [P, INNER], BF16)
        aT1, aT2 = t.sb("aT1", [P, HC, S], BF16), t.sb("aT2", [P, NI, S], BF16)
        wsum, wmean, winv = t.sb("wsum", [P, 2]), t.sb("wmean", [P, 2]), t.sb("winv", [P, 2])
        xn = t.sb("xn", [P, QT, HID])
        stats, mv = t.sb("stats", [P, 4, 6]), t.sb("mv", [P, 2])
        logvar, rstd = t.sb("logvar", [P, 1]), t.sb("rstd", [P, 1])
        peak, step, inv_step = t.sb("peak", [P, 1]), t.sb("step", [P, 1]), t.sb("inv_step", [P, 1])
        scale = t.sb("scale", [P, 2, QT])
        loaded = [t.sem("loaded0"), t.sem("loaded1")]
        chain, moments_done, log_done, rstd_done, abs_done, wsum_done, wmean_ready, w_rounded = map(
            t.sem, ("chain", "moments_done", "log_done", "rstd_done", "abs_done", "wsum_done", "wmean_ready",
                    "w_rounded"))
        a_ready, a_turned, a_copied, y1_done, h_ready, gelu_done, y2_done = map(
            t.sem, ("a_ready", "a_turned", "a_copied", "y1_done", "h_ready", "gelu_done", "y2_done"))
        turned, w_ps = t.psum("turned", [P, NI, P], BF16), t.psum("w_ps", [P, 2])
        y_ps = t.psum("y_ps", [P, 4, CH])
        block = ctx.enter_context(nc.Block())

        @block.sync
        def _(sp):
            sp.dma_start(w1[:], T["w1T"].rearrange("(k p) n -> p k n", p=P)).then_inc(loaded[0], 16)
            sp.dma_start(b1[:], T["b1"].to_broadcast([P, INNER])).then_inc(loaded[0], 16)
            sp.dma_start(w2[:], T["w2T"].rearrange("(k p) n -> p k n", p=P)).then_inc(loaded[1], 16)
            sp.dma_start(b2[:], T["b2"].to_broadcast([P, HID])).then_inc(loaded[1], 16)

        flat = [(w1[:].rearrange("p k n -> p (k n)"), w1q[:].rearrange("p k n -> p (k n)")),
                (w2[:].rearrange("p k n -> p (k n)"), w2q[:].rearrange("p k n -> p (k n)"))]

        @block.scalar
        def _(act):
            def token_rstd(n):
                act.wait_ge(moments_done, n + 1)
                nc.scalar.activation(logvar[:], mv[:, 1:2], ACT.Ln, bias=c["eps5"][:]).then_inc(log_done, 1)
                act.wait_ge(log_done, n + 1)
                nc.scalar.activation(rstd[:], logvar[:], ACT.Exp, scale=-0.5).then_inc(rstd_done, 1)

            def copy_turned(target, n, chunks):
                act.wait_ge(a_turned, n + 1)
                nc.scalar.activation(target, turned[:, 0:chunks, :], ACT.Copy).then_inc(a_copied, 1)

            for i in range(2):
                act.wait_ge(loaded[i], 32)
                at_least(act, abs_done, 2 * i)
                nc.scalar.activation(h[:].rearrange("p q n -> p (q n)"), flat[i][0][:, 0:2 * INNER], ACT.Abs,
                                     accum_out=wsum[:, i:i + 1]).then_inc(abs_done, 1)
                act.wait_ge(abs_done, 2 * i + 1)
                nc.scalar.activation(h[:].rearrange("p q n -> p (q n)"), flat[i][0][:, 2 * INNER:], ACT.Abs,
                                     accum_out=wmean[:, i:i + 1]).then_inc(abs_done, 1)
            for q in range(QT):
                token_rstd(2 * q)
                token_rstd(2 * q + 1)
                copy_turned(aT1[:, :, q * P:(q + 1) * P], q, HC)
            for q in range(QT):
                act.wait_ge(h_ready, 4 * q + 4)
                nc.scalar.activation(h[:, q, :], h[:, q, :], ACT.Gelu).then_inc(gelu_done, 1)
            for q in range(QT):
                token_rstd(2 * QT + q)
                copy_turned(aT2[:, :, q * P:(q + 1) * P], QT + q, NI)

        @block.tensor
        def _(pe):
            pe.wait_ge(wsum_done, 1)
            nc.tensor.matmul(w_ps[:], c["ones"][:], wsum[:], start=True, stop=True).then_inc(wmean_ready, 1)
            for q in range(QT):
                pe.wait_ge(a_ready, q + 1)
                at_least(pe, a_copied, q)
                for k in range(HC):
                    last = nc.tensor.transpose(turned[:, k, :], hq[:, k * P:(k + 1) * P], c["identb"][:])
                last.then_inc(a_turned, 1)
            pe.wait_ge(w_rounded, 1)
            for q in range(QT):
                pe.wait_ge(a_copied, q + 1)
                for n in range(4):
                    at_least(pe, h_ready, 4 * (q - 1) + n + 1)
                    for k in range(HC):
                        last = nc.tensor.matmul(y_ps[:, n, :], aT1[:, k, q * P:(q + 1) * P],
                                                w1q[:, k, n * CH:(n + 1) * CH], start=(k == 0), stop=(k == HC - 1))
                    last.then_inc(y1_done, 1)
            for q in range(QT):
                pe.wait_ge(a_ready, QT + q + 1)
                pe.wait_ge(a_copied, QT + q)
                for k in range(NI):
                    last = nc.tensor.transpose(turned[:, k, :], hq[:, k * P:(k + 1) * P], c["identb"][:])
                last.then_inc(a_turned, 1)
            pe.wait_ge(w_rounded, 2)
            for q in range(QT):
                pe.wait_ge(a_copied, QT + q + 1)
                pe.wait_ge(h_ready, 8)
                for k in range(NI):
                    last = nc.tensor.matmul(y_ps[:, q, :], aT2[:, k, q * P:(q + 1) * P], w2q[:, k, :],
                                            start=(k == 0), stop=(k == NI - 1))
                last.then_inc(y2_done, 1)

        @block.vector
        def _(dve):
            steps = [0]

            def then_wait(instruction):
                steps[0] += 1
                instruction.then_inc(chain, 1)
                dve.wait_ge(chain, steps[0])

            def normalise(src, dst, n):
                parts = src.shape[-1] // CH
                for i in range(parts):
                    then_wait(nc.vector.bn_stats(stats[:, i, :], src[:, i * CH:(i + 1) * CH]))
                nc.vector.bn_aggr(mv[:], stats[:, 0:parts, :].rearrange("p a b -> p (a b)")).then_inc(moments_done, 1)
                dve.wait_ge(moments_done, n + 1)
                dve.wait_ge(rstd_done, n + 1)
                then_wait(nc.vector.tensor_scalar(dst, src, mv[:, 0:1], rstd[:], ALU.subtract, ALU.mult))

            def quantise(src, factor, width):
                then_wait(nc.vector.tensor_reduce(peak[:], src, AX_X, ALU.max, apply_absolute_value=True))
                then_wait(nc.vector.tensor_scalar(step[:], peak[:], 1e-5, 1.0 / 127.0, ALU.max, ALU.mult))
                then_wait(nc.vector.reciprocal(inv_step[:], step[:]))
                then_wait(nc.vector.tensor_tensor(factor, step[:], wmean[:, 0:1] if width == HID else wmean[:, 1:2],
                                                  ALU.mult))
                then_wait(nc.vector.tensor_scalar(src, src, inv_step[:], ROUND, ALU.mult, ALU.add))
                then_wait(nc.vector.tensor_scalar(src, src, ROUND, 127.0, ALU.subtract, ALU.min))
                nc.vector.tensor_scalar(hq[:, 0:width], src, -128.0, None, ALU.max).then_inc(a_ready, 1)

            dve.wait_ge(abs_done, 4)
            nc.vector.tensor_tensor(wsum[:], wsum[:], wmean[:], ALU.add).then_inc(wsum_done, 1)
            dve.wait_ge(wmean_ready, 1)
            then_wait(nc.vector.tensor_scalar(wmean[:], w_ps[:], 1.0 / (HID * INNER), 1e-8, ALU.mult, ALU.max))
            then_wait(nc.vector.reciprocal(winv[:], wmean[:]))
            for i in range(2):
                raw, rounded = flat[i]
                then_wait(nc.vector.tensor_scalar(raw, raw, winv[:, i:i + 1], ROUND, ALU.mult, ALU.add))
                then_wait(nc.vector.tensor_scalar(raw, raw, ROUND, 1.0, ALU.subtract, ALU.min))
                nc.vector.tensor_scalar(rounded, raw, -1.0, None, ALU.max).then_inc(w_rounded, 1)
            for q in range(QT):
                normalise(c["x"][:, q, :], xn[:, q, :], 2 * q)
                normalise(xn[:, q, :], xn[:, q, :], 2 * q + 1)
                at_least(dve, a_turned, q)
                quantise(xn[:, q, :], scale[:, 0, q:q + 1], HID)
            for q in range(QT):
                for n in range(4):
                    cols = slice(n * CH, (n + 1) * CH)
                    dve.wait_ge(y1_done, 4 * q + n + 1)
                    nc.vector.scalar_tensor_tensor(h[:, q, cols], y_ps[:, n, :], scale[:, 0, q:q + 1], b1[:, cols],
                                                   ALU.mult, ALU.add).then_inc(h_ready, 1)
            for q in range(QT):
                dve.wait_ge(gelu_done, q + 1)
                normalise(h[:, q, :], h[:, q, :], 2 * QT + q)
                dve.wait_ge(a_turned, QT + q)
                quantise(h[:, q, :], scale[:, 1, q:q + 1], INNER)
            for q in range(QT):
                dve.wait_ge(y2_done, q + 1)
                then_wait(nc.vector.scalar_tensor_tensor(xn[:, q, :], y_ps[:, q, :], scale[:, 1, q:q + 1], b2[:],
                                                         ALU.mult, ALU.add))
                nc.vector.tensor_tensor(c["x"][:, q, :], c["x"][:, q, :], xn[:, q, :], ALU.add)


def store_output(nc, c, out):
    with nc.semaphore("result_stored") as stored, nc.Block() as block:
        @block.sync
        def _(sp):
            sp.dma_start(out.rearrange("a (t p) n -> p (a t) n", p=P), c["x"][:]).then_inc(stored, 16)
            sp.wait_ge(stored, 16)


def perceiver(nc, T, out):
    with ExitStack() as ctx:
        finished = []
        keep = Tiles(nc, ctx, "keep", finished)
        c = {"ident": keep.sb("ident", [P, P]), "identb": keep.sb("identb", [P, P], BF16),
             "ones": keep.sb("ones", [P, P]), "eps5": keep.sb("eps5", [P, 1]), "eps6": keep.sb("eps6", [P, 1]),
             "x": keep.sb("x", [P, QT, HID]), "finished": finished}
        with ExitStack() as ctx_context:
            t = Tiles(nc, ctx_context, "context", finished)
            ctxT_hi, ctxT_lo = t.sb("ctxT_hi", [P, CC, KV], F32R), t.sb("ctxT_lo", [P, CC, KV], F32R)
            cross_attention_0(nc, T, c, ctxT_hi, ctxT_lo)
            clear_semaphores(nc, finished)
            self_attention_0(nc, T, c)
            feed_forward_0(nc, T, c)
            clear_semaphores(nc, finished)
            cross_attention_1(nc, T, c, ctxT_hi, ctxT_lo)
        clear_semaphores(nc, finished)
        self_attention_1(nc, T, c)
        feed_forward_1(nc, T, c)
        store_output(nc, c, out)


def kernel(**inputs):
    import numpy as np
    import concourse.bacc as bacc
    from concourse.bass_utils import run_bass_kernel_spmd

    v = {name: np.asarray(a) for name, a in inputs.items()}
    ctx = v["ctx_1024"][0]

    def by_head(w):
        return w.reshape(CC, P, H, D).transpose(2, 1, 0, 3).reshape(H * P, CC * D)

    def by_group(w):
        return w.reshape(-1, NG, HG, 2, HD).transpose(0, 1, 3, 2, 4).reshape(-1, NG, 2 * P)

    wkv1 = by_group(np.concatenate([v["L1_xattn_Wk"], v["L1_xattn_Wv"]], axis=1))
    bkv1 = by_group(np.concatenate([v["L1_xattn_bk"], v["L1_xattn_bv"]])[None])
    four = lambda name: np.tile(v[name], HG)[:, None]
    laid_out = {
        "wkv1": wkv1.reshape(CC, P, NG, 2 * P).transpose(2, 1, 0, 3).reshape(NG * P, CC * 2 * P),
        "bk1": bkv1[:, :, :P].reshape(1, HID), "bv1": bkv1[:, :, P:].reshape(1, HID),
        "affine_k1": np.concatenate([four("L1_xattn_kn_w"), four("L1_xattn_kn_b")], axis=1),
        "affine1": np.concatenate([four("L1_xattn_" + n) for n in ("qn_w", "qn_b", "kn_dca_w", "kn_dca_b")], axis=1),
        "wq1": v["L1_xattn_Wq"], "bq1": v["L1_xattn_bq"][None],
        "wkv_dca": v["L1_xattn_Wkv_dca"], "bkv_dca": v["L1_xattn_bkv_dca"][None],
        **{f"w{n}_s1": v[f"L1_attn_W{n}"] for n in "qkvo"},
        "rows_s1": np.stack([v["L1_attn_bv"], v["L1_attn_bo"]])[None],
        "cols_s1": np.stack([v["L1_attn_bq"], v["L1_attn_bk"]]).reshape(2, HC, P).transpose(2, 0, 1),
        "pv": v["L1_attn_pv"][0], "pkT": v["L1_attn_pk"][0].reshape(PREFIX, NG, P).transpose(2, 1, 0),
        "w1T": v["L1_ffn_w1"].T, "w2T": v["L1_ffn_w2"].T, "b1": v["L1_ffn_b1"][None], "b2": v["L1_ffn_b2"][None],
        "wo1": v["L1_xattn_Wo"], "bo1": v["L1_xattn_bo"][None],
        "x": v["x"][0], "ctx": ctx, "ctxT": ctx.T,
        "wq0": v["L0_xattn_Wq"], "wk0": by_head(v["L0_xattn_Wk"]), "wv0": by_head(v["L0_xattn_Wv"]),
        "wo0": v["L0_xattn_Wo"], "gq": v["L0_xattn_gq"][:, None], "gk": v["L0_xattn_gk"][:, None],
        "wq_s0": v["L0_attn_Wq"].T, "wk_s0": v["L0_attn_Wk"].T, "wv_s0": v["L0_attn_Wv"].T,
        "wo_s0": v["L0_attn_Wo"].T, "bo_s0": v["L0_attn_bo"][None],
        "gate": v["L0_ffn_gate_w"], "up": v["L0_ffn_up_w"], "down": v["L0_ffn_down_w"],
        "expert": v["L0_ffn_expert_weight"], "gamma": v["L0_ffn_ln_gamma"][None], "beta": v["L0_ffn_ln_beta"][None],
    }
    laid_out = {f"in_{n}": np.ascontiguousarray(a) for n, a in laid_out.items()}
    nc = bacc.Bacc("TRN2", target_bir_lowering=False, num_devices=1)
    T = {n[3:]: nc.dram_tensor(n, a.shape, mybir.dt.from_np(a.dtype), kind="ExternalInput").ap()
         for n, a in laid_out.items()}
    out = nc.dram_tensor("out_x", (1, S, HID), F32, kind="ExternalOutput").ap()
    perceiver(nc, T, out)
    r = run_bass_kernel_spmd(nc, [laid_out], core_ids=[0])
    return r.results[0]["out_x"]
```

```python
from contextlib import ExitStack

import concourse.bass as bass
from concourse import mybir

F32 = mybir.dt.float32
F32R = mybir.dt.float32r
BF16 = mybir.dt.bfloat16
ACT = mybir.ActivationFunctionType
ALU = mybir.AluOpType
AX_X = mybir.AxisListType.X

P = 128
S = 256
QT = S // P
HID = 512
HC = HID // P
KV = 4096
CD = 256
CC = CD // P
NT = KV // P
CH = 512
NCH = KV // CH
TPC = CH // P
H = 16
D = 128
LOWEST = -3.0e38
LAST_STAGE = 6
TURN_AT, OUTPUT_AT = 1, 2


def at_least(eng, sem, value):
    if not isinstance(value, int) or value > 0:
        eng.wait_ge(sem, value)


def heads_loop(eng, nc_engine, body):
    body(0, True, False, False)
    body(1, True, True, False)
    with nc_engine.Fori(2, H - 1) as h:
        body(h, True, True, True)
    body(H - 1, True, True, True)
    body(H, False, True, True)
    body(H + 1, False, False, True)


class Tiles:

    def __init__(self, nc, ctx, stage, finished=None):
        self.nc, self.ctx, self.stage = nc, ctx, stage
        if finished is not None:
            self.used = []
            ctx.callback(lambda: finished.extend(self.used))

    def sb(self, name, shape, dt=F32):
        return self.ctx.enter_context(self.nc.sbuf_tensor(f"{self.stage}_{name}", shape, dt))

    def psum(self, name, shape, dt=F32):
        return self.ctx.enter_context(self.nc.psum_tensor(f"{self.stage}_{name}", shape, dt))

    def sem(self, name):
        handle = self.ctx.enter_context(self.nc.semaphore(f"{self.stage}_{name}"))
        self.used.append(handle.num)
        return handle


def clear_semaphores(nc, finished):
    with nc.Block() as block:
        @block.gpsimd
        def _(pool):
            first = None
            for n in sorted(finished):
                if first is None:
                    first = n
                if n + 1 not in finished:
                    nc.gpsimd.sem_clear(range(first, n + 1))
                    first = None
    finished.clear()


def setup_constants(nc, T, c):
    with ExitStack() as ctx:
        t = Tiles(nc, ctx, "setup", c["finished"])
        zeroed, made, loaded = t.sem("zeroed"), t.sem("made"), t.sem("loaded")
        block = ctx.enter_context(nc.Block())

        @block.sync
        def _(sp):
            sp.dma_start(c["x"][:], T["x"].rearrange("(t p) n -> p t n", p=P)).then_inc(loaded, 16)
            sp.wait_ge(loaded, 16)

        @block.scalar
        def _(act):
            nc.scalar.preload_act_table_set("natural_log_exp_and_others")

        @block.gpsimd
        def _(pool):
            nc.gpsimd.memset(c["ident"][:], 0.0).then_inc(zeroed, 1)
            nc.gpsimd.memset(c["ones"][:], 1.0)
            nc.gpsimd.memset(c["eps5"][:], 1e-5)
            nc.gpsimd.memset(c["eps6"][:], 1e-6)
            pool.wait_ge(zeroed, 1)
            nc.gpsimd.affine_select(out=c["ident"][:], in_=c["ident"][:], compare_op=ALU.not_equal, fill=1.0, base=0,
                                    pattern=[[-1, P]], channel_multiplier=1).then_inc(made, 1)


def layernorm_transposed(nc, c, stage, x, xnT, prefetch=None):
    with ExitStack() as ctx:
        t = Tiles(nc, ctx, stage, c["finished"])
        stats, mv = t.sb("stats", [P, QT, 6]), t.sb("mv", [P, QT, 2])
        logvar, rstd = t.sb("logvar", [P, QT]), t.sb("rstd", [P, QT])
        xn = t.sb("xn", [P, QT, HID])
        turned = t.psum("turned", [P, QT, HID])
        stats_done, moments_done, log_done, rstd_done, normed, transposed = map(
            t.sem, ("stats_done", "moments_done", "log_done", "rstd_done", "normed", "transposed"))
        block = ctx.enter_context(nc.Block())

        if prefetch:
            @block.sync
            def _(sp):
                prefetch(sp)

        @block.vector
        def _(dve):
            for q in range(QT):
                nc.vector.bn_stats(stats[:, q, :], x[:, q, :]).then_inc(stats_done, 1)
            for q in range(QT):
                dve.wait_ge(stats_done, q + 1)
                nc.vector.bn_aggr(mv[:, q, :], stats[:, q, :]).then_inc(moments_done, 1)
            dve.wait_ge(moments_done, QT)
            dve.wait_ge(rstd_done, 1)
            for q in range(QT):
                nc.vector.tensor_scalar(xn[:, q, :], x[:, q, :], mv[:, q, 0:1], rstd[:, q:q + 1],
                                        ALU.subtract, ALU.mult).then_inc(normed, 1)

        @block.scalar
        def _(act):
            act.wait_ge(moments_done, QT)
            nc.scalar.activation(logvar[:], mv[:, :, 1], ACT.Ln, bias=c["eps5"][:]).then_inc(log_done, 1)
            act.wait_ge(log_done, 1)
            nc.scalar.activation(rstd[:], logvar[:], ACT.Exp, scale=-0.5).then_inc(rstd_done, 1)
            for q in range(QT):
                act.wait_ge(transposed, q + 1)
                nc.scalar.activation(xnT[:, :, q * P:(q + 1) * P],
                                     turned[:, q, :].rearrange("p (k t) -> p k t", k=HC), ACT.Copy)

        @block.tensor
        def _(pe):
            for q in range(QT):
                pe.wait_ge(normed, q + 1)
                for k in range(HC):
                    last = nc.tensor.transpose(turned[:, q, k * P:(k + 1) * P], xn[:, q, k * P:(k + 1) * P],
                                               c["ident"][:])
                last.then_inc(transposed, 1)


def cross0_queries(nc, T, c, xnT, qT, ctxT_hi, ctxT_lo, ctx_hl, wq, wq_loaded):
    NP = 8
    PIECE = 2048
    with ExitStack() as ctx:
        t = Tiles(nc, ctx, "queries0", c["finished"])
        raw = t.sb("raw", [P, 2, PIECE])
        gq, gk, gqk = t.sb("gq", [P, 1]), t.sb("gk", [P, 1]), t.sb("gqk", [P, 1])
        squares, log_ms, rrms = t.sb("squares", [P, 2, S]), t.sb("log_ms", [P, 2, S]), t.sb("rrms", [P, 2, S])
        q_ps = t.psum("q_ps", [P, 2, CH])
        ms_ps = t.psum("ms_ps", [P, 2, CH])
        g_loaded, g_done = t.sem("g_loaded"), t.sem("g_done")
        raw_loaded = [t.sem("raw_loaded0"), t.sem("raw_loaded1")]
        hi_done, lo_done = t.sem("hi_done"), t.sem("lo_done")
        q_done, sq_done, ms_done, log_done, rrms_done, qT_done = map(
            t.sem, ("q_done", "sq_done", "ms_done", "log_done", "rrms_done", "qT_done"))
        block = ctx.enter_context(nc.Block())

        def piece(i):
            if i < 4:
                k, half = i // 2, (i % 2) * PIECE
                src = T["ctxT"][k * P:(k + 1) * P, half:half + PIECE]
                return src, raw[:, i % 2, :], ctxT_hi[:, k, half:half + PIECE], ctxT_lo[:, k, half:half + PIECE]
            n = PIECE // CD
            tiles = slice((i - 4) * n, (i - 3) * n)
            src = T["ctx"].rearrange("(t p) n -> p t n", p=P)[:, tiles, :]
            return (src, raw[:, i % 2, :].rearrange("p (t n) -> p t n", n=CD),
                    ctx_hl[:, tiles, 0:CD], ctx_hl[:, tiles, CD:2 * CD])

        @block.sync
        def _(sp):
            sp.dma_start(gq[:], T["gq"]).then_inc(g_loaded, 16)
            sp.dma_start(gk[:], T["gk"]).then_inc(g_loaded, 16)
            for i in range(NP):
                src, dst, _, _ = piece(i)
                if i >= 2:
                    sp.wait_ge(hi_done, i - 1)
                    sp.wait_ge(lo_done, i - 1)
                sp.dma_start(dst, src).then_inc(raw_loaded[i % 2], 16)

        @block.vector
        def _(dve):
            dve.wait_ge(g_loaded, 32)
            nc.vector.tensor_scalar(gqk[:], gq[:], gk[:], float(D) ** -0.5, ALU.mult, ALU.mult).then_inc(g_done, 1)
            dve.wait_ge(g_done, 1)
            for h in range(H):
                dve.wait_ge(rrms_done, h + 1)
                nc.vector.scalar_tensor_tensor(qT[:, h, :], q_ps[:, h % 2, 0:S], gqk[:], rrms[:, h % 2, :],
                                               ALU.mult, ALU.mult).then_inc(qT_done, 1)
                if h % 2:
                    _, src, hi, lo = piece(h // 2)
                    dve.wait_ge(hi_done, h // 2 + 1)
                    nc.vector.tensor_tensor(lo, src, hi.bitcast(F32), ALU.subtract).then_inc(lo_done, 1)

        @block.scalar
        def _(act):
            for h in range(H):
                b = h % 2
                act.wait_ge(q_done, h + 1)
                at_least(act, ms_done, h - 1)
                nc.scalar.activation(squares[:, b, :], q_ps[:, b, 0:S], ACT.Square).then_inc(sq_done, 1)
                act.wait_ge(ms_done, h + 1)
                at_least(act, rrms_done, h - 1)
                nc.scalar.activation(log_ms[:, b, :], ms_ps[:, b, 0:S], ACT.Ln, bias=c["eps5"][:],
                                     scale=1.0 / D).then_inc(log_done, 1)
                act.wait_ge(log_done, h + 1)
                at_least(act, qT_done, h - 1)
                nc.scalar.activation(rrms[:, b, :], log_ms[:, b, :], ACT.Exp, scale=-0.5).then_inc(rrms_done, 1)
                if h % 2:
                    i = h // 2
                    _, src, hi, _ = piece(i)
                    act.wait_ge(raw_loaded[i % 2], 16 * (i // 2 + 1))
                    nc.scalar.activation(hi, src, ACT.Copy).then_inc(hi_done, 1)

        @block.tensor
        def _(pe):
            def project(h):
                if h % 4 == 0:
                    pe.wait_ge(wq_loaded[h // 4], 16)
                at_least(pe, qT_done, h - 1)
                for k in range(HC):
                    last = nc.tensor.matmul(q_ps[:, h % 2, 0:S], wq[:, k, h * D:(h + 1) * D], xnT[:, k, :],
                                            start=(k == 0), stop=(k == HC - 1))
                last.then_inc(q_done, 1)

            project(0)
            for h in range(H):
                if h + 1 < H:
                    project(h + 1)
                pe.wait_ge(sq_done, h + 1)
                at_least(pe, log_done, h - 1)
                nc.tensor.matmul(ms_ps[:, h % 2, 0:S], c["ones"][:], squares[:, h % 2, :],
                                 start=True, stop=True).then_inc(ms_done, 1)


def cross0_attention(nc, T, c, qT, ctxT_hi, ctxT_lo, ctx_hl):
    with ExitStack() as ctx:
        t = Tiles(nc, ctx, "cross0", c["finished"])
        wk_raw = t.sb("wk_raw", [P, CC * D])
        wk_hi, wk_lo = t.sb("wk_hi", [P, CC * D], F32R), t.sb("wk_lo", [P, CC * D], F32R)
        wv = t.sb("wv", [P, CC * D])
        q_hi, q_lo = t.sb("q_hi", [P, S], F32R), t.sb("q_lo", [P, S], F32R)
        k_hi, k_lo = t.sb("k_hi", [P, CH], F32R), t.sb("k_lo", [P, CH], F32R)
        squares = t.sb("squares", [P, CH])
        sq_hi, sq_lo = t.sb("sq_hi", [P, CH], F32R), t.sb("sq_lo", [P, CH], F32R)
        ones = c["ones"][:].bitcast(F32R)
        rrms = t.sb("rrms", [P, CH])
        probs = t.sb("probs", [P, QT, KV])
        pt_hi, pt_lo = t.sb("pt_hi", [P, QT, CH], F32R), t.sb("pt_lo", [P, QT, CH], F32R)
        chunk_max, negmax = t.sb("chunk_max", [P, QT, NCH]), t.sb("negmax", [P, QT])
        chunk_sum, rowsum, rinv = t.sb("chunk_sum", [P, QT, NCH]), t.sb("rowsum", [P, QT]), t.sb("rinv", [P, QT])
        low_part = c["x"][:, 0, :].rearrange("p (q n) -> p q n", q=QT)
        pc = c["x"][:, 1, :].rearrange("p (q n) -> p q n", q=QT)
        pcT = c["x"][:, 0, :]
        k_ps, ms_ps = t.psum("k_ps", [P, CH]), t.psum("ms_ps", [P, CH])
        s_ps, t_ps, pc_ps = (t.psum("s_ps", [P, QT, CH]), t.psum("t_ps", [P, QT, CH]),
                             t.psum("pc_ps", [P, QT, 2 * CD]))
        wk_loaded, wv_loaded = t.sem("wk_loaded"), t.sem("wv_loaded")
        wk_split, q_split = t.sem("wk_split"), t.sem("q_split")
        k_done, khi_done, klo_done, sq_done, sqhi_done, sqlo_done, ms_done, log_done, rrms_done = map(
            t.sem, ("k_done", "khi_done", "klo_done", "sq_done", "sqhi_done", "sqlo_done",
                    "ms_done", "log_done", "rrms_done"))
        s_done, scored, exp_done, t_done, pthi_done, ptlo_done, pc_done = map(
            t.sem, ("s_done", "scored", "exp_done", "t_done", "pthi_done", "ptlo_done", "pc_done"))
        max_done, sum_done, rinv_done, lowpart_done, norm_done = map(
            t.sem, ("max_done", "sum_done", "rinv_done", "lowpart_done", "norm_done"))
        pcT_turned, pcT_done, out_done, stored = map(t.sem, ("pcT_turned", "pcT_done", "out_done", "stored"))
        may_score = t.sem("may_score")
        block = ctx.enter_context(nc.Block())

        def following(h, ch):
            if ch + 1 < NCH:
                return h, ch + 1
            return None if isinstance(h, int) and h == H - 1 else (h + 1, 0)

        @block.sync
        def _(sp):
            def load_wk(h):
                at_least(sp, wk_split, 2 * h)
                sp.dma_start(wk_raw[:], T["wk0"][bass.ds(h * P, P), :]).then_inc(wk_loaded, 16)

            def load_wv(g):
                at_least(sp, out_done, g)
                sp.dma_start(wv[:], T["wv0"][bass.ds(g * P, P), :]).then_inc(wv_loaded, 16)

            load_wk(0)
            load_wk(1)
            load_wk(2)
            load_wv(0)
            with nc.sync.Fori(3, H) as h:
                load_wk(h)
                load_wv(h - 2)
            load_wv(H - 2)
            load_wv(H - 1)

        @block.tensor
        def _(pe):
            def keys(h, ch):
                if ch == 0:
                    pe.wait_ge(wk_split, 2 * h + 2)
                n = 8 * h + ch
                at_least(pe, khi_done, n)
                at_least(pe, klo_done, n)
                at_least(pe, sq_done, n)
                cols = slice(ch * CH, (ch + 1) * CH)
                for k in range(CC):
                    w = slice(k * D, (k + 1) * D)
                    nc.tensor.matmul(k_ps[:], wk_hi[:, w], ctxT_hi[:, k, cols], start=(k == 0), stop=False)
                    nc.tensor.matmul(k_ps[:], wk_hi[:, w], ctxT_lo[:, k, cols], start=False, stop=False)
                    last = nc.tensor.matmul(k_ps[:], wk_lo[:, w], ctxT_hi[:, k, cols],
                                            start=False, stop=(k == CC - 1))
                last.then_inc(k_done, 1)

            def sums(h, ch):
                pe.wait_ge(sqhi_done, 8 * h + ch + 1)
                pe.wait_ge(sqlo_done, 8 * h + ch + 1)
                at_least(pe, log_done, 8 * h + ch)
                nc.tensor.matmul(ms_ps[:], ones, sq_hi[:], start=True, stop=False)
                nc.tensor.matmul(ms_ps[:], ones, sq_lo[:], start=False, stop=True).then_inc(ms_done, 1)

            def scores(h, ch):
                if ch == 0:
                    pe.wait_ge(q_split, 2 * h + 2)
                pe.wait_ge(khi_done, 8 * h + ch + 1)
                pe.wait_ge(klo_done, 8 * h + ch + 1)
                for q in range(QT):
                    at_least(pe, scored, 16 * h + 2 * ch + q - 1)
                    rows = slice(q * P, (q + 1) * P)
                    nc.tensor.matmul(s_ps[:, q, :], q_hi[:, rows], k_hi[:], start=True, stop=False)
                    nc.tensor.matmul(s_ps[:, q, :], q_hi[:, rows], k_lo[:], start=False, stop=False)
                    nc.tensor.matmul(s_ps[:, q, :], q_lo[:, rows], k_hi[:],
                                     start=False, stop=True).then_inc(s_done, 1)

            def transposes(g, ch, tiles=range(QT)):
                for q in tiles:
                    pe.wait_ge(exp_done, 16 * g + 2 * ch + q + 1)
                    for j in range(TPC):
                        at = ch * CH + j * P
                        last = nc.tensor.transpose(t_ps[:, q, j * P:(j + 1) * P], probs[:, q, at:at + P],
                                                   c["ident"][:])
                    last.then_inc(t_done, 1)

            def values(g, ch, tiles=range(QT)):
                for q in tiles:
                    pe.wait_ge(pthi_done, 16 * g + 2 * ch + q + 1)
                    pe.wait_ge(ptlo_done, 16 * g + 2 * ch + q + 1)
                    if ch == 0:
                        at_least(pe, norm_done, 2 * g + q - 1)
                    for j in range(TPC):
                        tile, cols = ch * TPC + j, slice(j * P, (j + 1) * P)
                        nc.tensor.matmul(pc_ps[:, q, :], pt_hi[:, q, cols], ctx_hl[:, tile, :],
                                         start=(tile == 0), stop=False)
                        last = nc.tensor.matmul(pc_ps[:, q, 0:CD], pt_lo[:, q, cols], ctx_hl[:, tile, 0:CD],
                                                start=False, stop=(tile == NT - 1))
                    last.then_inc(pc_done, 1)

            def turn_pc(o):
                pe.wait_ge(norm_done, 2 * o + 2)
                for q in range(QT):
                    for k in range(CC):
                        last = nc.tensor.transpose(ms_ps[:, k * S + q * P:k * S + (q + 1) * P],
                                                   pc[:, q, k * P:(k + 1) * P], c["ident"][:])
                last.then_inc(pcT_turned, 1)

            def output(o):
                pe.wait_ge(pcT_done, o + 1)
                pe.wait_ge(wv_loaded, 16 * o + 16)
                for k in range(CC):
                    last = nc.tensor.matmul(ms_ps[:, 0:S], wv[:, k * D:(k + 1) * D], pcT[:, k * S:(k + 1) * S],
                                            start=(k == 0), stop=(k == CC - 1))
                last.then_inc(out_done, 1)

            def body(h, has_scores, has_values, has_output):
                g, o = h - 1, h - 2
                alone = has_values and not has_scores
                if alone:
                    transposes(g, 0)
                for ch in range(NCH):
                    ahead = following(h, ch) if has_scores else None
                    if has_values and has_scores:
                        transposes(g, ch)
                    if has_scores:
                        scores(h, ch)
                    if ahead:
                        keys(*ahead)
                    if has_output and ch in (TURN_AT, OUTPUT_AT):
                        pe.wait_ge(log_done, 8 * h + ch + 1 if has_scores else 8 * H)
                        (turn_pc if ch == TURN_AT else output)(o)
                    if alone:
                        for q in range(QT):
                            values(g, ch, [q])
                            if ch + 1 < NCH:
                                transposes(g, ch + 1, [q])
                    elif has_values:
                        values(g, ch)
                    if ahead:
                        if has_output and ch == TURN_AT:
                            pe.wait_ge(pcT_done, o + 1)
                        if has_output and ch == OUTPUT_AT:
                            pe.wait_ge(stored, o + 1)
                        sums(*ahead)

            keys(0, 0)
            sums(0, 0)
            heads_loop(pe, nc.tensor, body)

        @block.scalar
        def _(act):
            def keys_high(h, ch):
                act.wait_ge(k_done, 8 * h + ch + 1)
                at_least(act, ms_done, 8 * h + ch)
                nc.scalar.activation(sq_hi[:], k_ps[:], ACT.Square).then_inc(sqhi_done, 1)
                at_least(act, sqlo_done, 8 * h + ch)
                nc.scalar.activation(squares[:], k_ps[:], ACT.Square).then_inc(sq_done, 1)
                at_least(act, s_done, 16 * h + 2 * ch)
                nc.scalar.activation(k_hi[:], k_ps[:], ACT.Copy).then_inc(khi_done, 1)

            def keys_rrms(h, ch):
                n = 8 * h + ch
                act.wait_ge(ms_done, n + 1)
                at_least(act, scored, 2 * n)
                nc.scalar.activation(rrms[:], ms_ps[:], ACT.Ln, bias=c["eps5"][:],
                                     scale=1.0 / D).then_inc(log_done, 1)
                act.wait_ge(log_done, n + 1)
                nc.scalar.activation(rrms[:], rrms[:], ACT.Exp, scale=-0.5).then_inc(rrms_done, 1)

            def exps(g, ch):
                if ch == 0:
                    act.wait_ge(max_done, g + 1)
                    at_least(act, sum_done, g)
                cols = slice(ch * CH, (ch + 1) * CH)
                for q in range(QT):
                    nc.scalar.activation(probs[:, q, cols], probs[:, q, cols], ACT.Exp, bias=negmax[:, q:q + 1],
                                         accum_out=chunk_sum[:, q, ch:ch + 1]).then_inc(exp_done, 1)

            def body(h, has_scores, has_values, has_output):
                g = h - 1
                for ch in range(NCH):
                    ahead = following(h, ch) if has_scores else None
                    if has_values:
                        for q in range(QT):
                            n = 16 * g + 2 * ch + q
                            act.wait_ge(t_done, n + 1)
                            at_least(act, pc_done, n - 1)
                            nc.scalar.activation(pt_hi[:, q, :], t_ps[:, q, :], ACT.Copy).then_inc(pthi_done, 1)
                    if ahead:
                        keys_high(*ahead)
                    if has_values and ch + 1 < NCH:
                        exps(g, ch + 1)
                    if has_scores and ch == NCH - 1:
                        exps(h, 0)
                    if has_values and ch == NCH - 1:
                        act.wait_ge(rinv_done, g + 1)
                        for q in range(QT):
                            act.wait_ge(pc_done, 16 * g + 15 + q)
                            at_least(act, norm_done, 2 * g + q - 1)
                            at_least(act, out_done, g)
                            nc.scalar.activation(low_part[:, q, :], pc_ps[:, q, CD:2 * CD], ACT.Copy,
                                                 scale=rinv[:, q:q + 1]).then_inc(lowpart_done, 1)
                    if ahead:
                        keys_rrms(*ahead)

            keys_high(0, 0)
            keys_rrms(0, 0)
            heads_loop(act, nc.scalar, body)

        @block.vector
        def _(dve):
            def split_wk(h):
                dve.wait_ge(wk_loaded, 16 * h + 16)
                at_least(dve, k_done, 8 * h)
                nc.vector.tensor_copy(wk_hi[:], wk_raw[:]).then_inc(wk_split, 1)
                dve.wait_ge(wk_split, 2 * h + 1)
                nc.vector.tensor_tensor(wk_lo[:], wk_raw[:], wk_hi[:].bitcast(F32),
                                        ALU.subtract).then_inc(wk_split, 1)

            def split_q(h):
                at_least(dve, s_done, 16 * h)
                q_h = qT[:, bass.ds(h * S, S)]
                nc.vector.tensor_scalar(q_hi[:], q_h, 1.0, None, ALU.mult).then_inc(q_split, 1)
                dve.wait_ge(q_split, 2 * h + 1)
                nc.vector.tensor_tensor(q_lo[:], q_h, q_hi[:].bitcast(F32), ALU.subtract).then_inc(q_split, 1)

            def keys_low(h, ch):
                dve.wait_ge(sq_done, 8 * h + ch + 1)
                at_least(dve, ms_done, 8 * h + ch)
                nc.vector.tensor_tensor(sq_lo[:], squares[:], sq_hi[:].bitcast(F32),
                                        ALU.subtract).then_inc(sqlo_done, 1)
                dve.wait_ge(khi_done, 8 * h + ch + 1)
                at_least(dve, s_done, 16 * h + 2 * ch)
                nc.vector.tensor_tensor(k_lo[:], k_ps[:], k_hi[:].bitcast(F32), ALU.subtract).then_inc(klo_done, 1)

            def body(h, has_scores, has_values, has_output):
                g, o = h - 1, h - 2
                for ch in range(NCH):
                    ahead = following(h, ch) if has_scores else None
                    if has_values:
                        for q in range(QT):
                            n = 16 * g + 2 * ch + q
                            dve.wait_ge(pthi_done, n + 1)
                            at_least(dve, pc_done, n - 1)
                            nc.vector.tensor_tensor(pt_lo[:, q, :], t_ps[:, q, :], pt_hi[:, q, :].bitcast(F32),
                                                    ALU.subtract).then_inc(ptlo_done, 1)
                    if has_scores:
                        dve.wait_ge(rrms_done, 8 * h + ch + 1)
                        if ch == 0:
                            at_least(dve, max_done, h)
                        for q in range(QT):
                            n = 16 * h + 2 * ch + q
                            dve.wait_ge(s_done, n + 1)
                            at_least(dve, t_done, n - 15)
                            nc.vector.sem_inc(may_score, 1)
                            nc.vector.tensor_tensor_reduce(
                                out=probs[:, q, ch * CH:(ch + 1) * CH], in0=s_ps[:, q, :], in1=rrms[:], scale=1.0,
                                scalar=LOWEST, op0=ALU.mult, op1=ALU.max,
                                accum_out=chunk_max[:, q, ch:ch + 1]).then_inc(scored, 1)
                    if has_values and ch == NCH - 1:
                        dve.wait_ge(exp_done, 16 * g + 16)
                        at_least(dve, lowpart_done, 2 * g)
                        nc.vector.tensor_reduce(rowsum[:], chunk_sum[:], AX_X, ALU.add).then_inc(sum_done, 1)
                    if has_scores and ch == NCH - 1:
                        dve.wait_ge(scored, 16 * h + 16)
                        at_least(dve, exp_done, 16 * h)
                        nc.vector.tensor_reduce(negmax[:], chunk_max[:], AX_X, ALU.max,
                                                negate=True).then_inc(max_done, 1)
                    if has_values and ch == NCH - 1:
                        dve.wait_ge(sum_done, g + 1)
                        nc.vector.reciprocal(rinv[:], rowsum[:]).then_inc(rinv_done, 1)
                    if has_output and ch == TURN_AT:
                        dve.wait_ge(pcT_turned, o + 1)
                        at_least(dve, out_done, o)
                        nc.vector.tensor_copy(pcT, ms_ps[:]).then_inc(pcT_done, 1)
                    if has_output and ch == OUTPUT_AT:
                        dve.wait_ge(out_done, o + 1)
                        dve.wait_ge(q_split, 2 * o + 2)
                        nc.vector.tensor_scalar(qT[:, bass.ds(o * S, S)], ms_ps[:, 0:S], 1.0, None,
                                                ALU.mult).then_inc(stored, 1)
                    if ahead:
                        keys_low(*ahead)
                    if ahead and ch == NCH - 2 and following(h, NCH - 1):
                        split_wk(h + 1)
                    if ahead and ch == NCH - 1:
                        split_q(h + 1)
                    if has_values and ch == NCH - 1:
                        dve.wait_ge(rinv_done, g + 1)
                        at_least(dve, pcT_turned, g)
                        for q in range(QT):
                            dve.wait_ge(lowpart_done, 2 * g + q + 1)
                            nc.vector.scalar_tensor_tensor(pc[:, q, :], pc_ps[:, q, 0:CD], rinv[:, q:q + 1],
                                                           low_part[:, q, :], ALU.mult,
                                                           ALU.add).then_inc(norm_done, 1)

            split_wk(0)
            split_q(0)
            keys_low(0, 0)
            heads_loop(dve, nc.vector, body)


def output_projection(nc, c, stage, attnT, n_k, w, w_ready, bias_row=None, prefetch=None):
    with ExitStack() as ctx:
        t = Tiles(nc, ctx, stage, c["finished"])
        y_ps = t.psum("y_ps", [P, QT, HID])
        y_done = t.sem("y_done")
        block = ctx.enter_context(nc.Block())

        if prefetch:
            @block.sync
            def _(sp):
                prefetch(sp)

        @block.tensor
        def _(pe):
            for n, (sem, value) in enumerate(w_ready):
                pe.wait_ge(sem, value)
                for k in range(n * n_k // len(w_ready), (n + 1) * n_k // len(w_ready)):
                    for q in range(QT):
                        last = nc.tensor.matmul(y_ps[:, q, :], attnT[:, k, q * P:(q + 1) * P], w[:, k, :],
                                                start=(k == 0), stop=(k == n_k - 1 and bias_row is None))
                        if k == n_k - 1:
                            if bias_row is not None:
                                last = nc.tensor.matmul(y_ps[:, q, :], c["ones"][0:1, :], bias_row,
                                                        start=False, stop=True)
                            last.then_inc(y_done, 1)

        @block.vector
        def _(dve):
            for q in range(QT):
                dve.wait_ge(y_done, q + 1)
                nc.vector.tensor_tensor(c["x"][:, q, :], c["x"][:, q, :], y_ps[:, q, :], ALU.add)


class Layer0Buffers:

    def __init__(self, nc, ctx, finished):
        self.t = Tiles(nc, ctx, "layer0", finished)
        self.heads = self.t.sb("heads", [P, H, S])

    def allocate_rest(self):
        sb, sem = self.t.sb, self.t.sem
        self.rows_w = sb("rows_w", [P, H, HID])
        self.wide_w = sb("wide_w", [P, HC, H * D])
        self.key_w, self.value_w = sb("key_w", [P, HC, HID]), sb("value_w", [P, HC, HID])
        self.xnT = sb("xnT", [P, HC, S])
        self.wk_loaded, self.wv_loaded = sem("wk_loaded"), sem("wv_loaded")
        self.wq_loaded = [sem(f"wq_loaded{i}") for i in range(4)]


def cross_attention_0(nc, T, c, buffers, ctxT_hi, ctxT_lo):
    with ExitStack() as ctx:
        t = Tiles(nc, ctx, "layer0cross", c["finished"])
        qT = buffers.heads
        qT_flat = qT[:].rearrange("p h s -> p (h s)")
        with ExitStack() as ctx2:
            t2 = Tiles(nc, ctx2, "layer0cross_in", c["finished"])
            ctx_hl = t2.sb("ctx_hl", [P, NT, 2 * CD], F32R)
            with ExitStack() as ctx3:
                t3 = Tiles(nc, ctx3, "layer0cross_q", c["finished"])
                wq = t3.sb("wq", [P, HC, H * D])
                xnT = t3.sb("xnT", [P, HC, S])
                wq_loaded = [t.sem(f"wq_loaded{i}") for i in range(4)]
                setup_constants(nc, T, c)

                def load_wq(sp):
                    for i in range(4):
                        cols = slice(i * 512, (i + 1) * 512)
                        sp.dma_start(wq[:, :, cols], T["wq0"].rearrange("(k p) n -> p k n", p=P)[:, :, cols])\
                          .then_inc(wq_loaded[i], 16)

                layernorm_transposed(nc, c, "norm0", c["x"], xnT, load_wq)
                cross0_queries(nc, T, c, xnT, qT, ctxT_hi, ctxT_lo, ctx_hl, wq, wq_loaded)
            cross0_attention(nc, T, c, qT_flat, ctxT_hi, ctxT_lo, ctx_hl)
        buffers.allocate_rest()
        wo = buffers.rows_w
        wo_loaded = [t.sem(f"wo_loaded{i}") for i in range(4)]
        x_loaded = t.sem("x_loaded")
        with nc.Block() as block:
            @block.sync
            def _(sp):
                sp.dma_start(c["x"][:], T["x"].rearrange("(t p) n -> p t n", p=P)).then_inc(x_loaded, 16)
                for i in range(4):
                    sp.dma_start(wo[:, 4 * i:4 * i + 4, :],
                                 T["wo0"].rearrange("(h p) n -> p h n", p=P)[:, 4 * i:4 * i + 4, :])\
                      .then_inc(wo_loaded[i], 16)
                load_self_attention_0(sp, T, buffers)
                sp.wait_ge(x_loaded, 16)
        output_projection(nc, c, "out0", qT, H, wo, [(s, 16) for s in wo_loaded])


def block_mask(nc, pool, sem, mask, blocks, rows, width):
    n = 0
    for op in range(3):
        if op == 0:
            last = nc.gpsimd.memset(mask[:], 1.0)
        elif op == 1:
            last = nc.gpsimd.affine_select(out=mask[:], in_=mask[:], compare_op=ALU.is_ge, fill=0.0, base=0,
                                           pattern=[[-rows, blocks], [0, width]], channel_multiplier=1)
        else:
            last = nc.gpsimd.affine_select(out=mask[:], in_=mask[:], compare_op=ALU.is_ge, fill=0.0, base=rows - 1,
                                           pattern=[[rows, blocks], [0, width]], channel_multiplier=-1)
        last.then_inc(sem, 1)
        n += 1
        pool.wait_ge(sem, n)


def load_self_attention_0(sp, T, buffers):
    sp.dma_start(buffers.key_w[:], T["wk_s0"].rearrange("(k p) n -> p k n", p=P)).then_inc(buffers.wk_loaded, 16)
    sp.dma_start(buffers.value_w[:], T["wv_s0"].rearrange("(k p) n -> p k n", p=P)).then_inc(buffers.wv_loaded, 16)
    for i in range(4):
        cols = slice(i * 512, (i + 1) * 512)
        sp.dma_start(buffers.wide_w[:, :, cols], T["wq_s0"].rearrange("(k p) n -> p k n", p=P)[:, :, cols])\
          .then_inc(buffers.wq_loaded[i], 16)


def self_attention_0(nc, T, c, buffers, load_next):
    KH = 4
    with ExitStack() as ctx:
        t = Tiles(nc, ctx, "self0", c["finished"])
        wq, wk, wv, wo = buffers.wide_w, buffers.key_w, buffers.value_w, buffers.rows_w
        wk_loaded, wv_loaded, wq_loaded = buffers.wk_loaded, buffers.wv_loaded, buffers.wq_loaded
        xnT, attnT = buffers.xnT, buffers.heads
        bo, wo_loaded = t.sb("bo", [1, HID]), t.sem("wo_loaded")

        def load_wo(sp):
            sp.dma_start(wo[:], T["wo_s0"].rearrange("(h p) n -> p h n", p=P)).then_inc(wo_loaded, 16)
            sp.dma_start(bo[:], T["bo_s0"]).then_inc(wo_loaded, 16)

        layernorm_transposed(nc, c, "norm1", c["x"], xnT, load_wo)
        with ExitStack() as ctx2:
            t = Tiles(nc, ctx2, "self0a", c["finished"])
            W = 3 * P
            kT, v = t.sb("kT", [P, KH, S]), t.sb("v", [P, QT, KH * D])
            qT = t.sb("qT", [P, 2, S])
            mask = t.sb("mask", [P, W])
            scores, probsT = t.sb("scores", [P, 2, W]), t.sb("probsT", [P, 2, W])
            negmax, sums, rinv = t.sb("negmax", [P, 2, QT]), t.sb("sums", [P, 2, QT]), t.sb("rinv", [P, 2, QT])
            q_ps, s_ps, t_ps, o_ps = (t.psum(n, [P, 2, CH]) for n in ("q_ps", "s_ps", "t_ps", "o_ps"))
            mask_made, kv_done, kv_copied = t.sem("mask_made"), t.sem("kv_done"), t.sem("kv_copied")
            q_done, q_copied, s_done, masked, max_done, exp_done, rinv_done, normed = map(
                t.sem, ("q_done", "q_copied", "s_done", "masked", "max_done", "exp_done", "rinv_done", "normed"))
            t_done, t_copied, o_done, o_copied = map(t.sem, ("t_done", "t_copied", "o_done", "o_copied"))
            parts = [(0, slice(0, P)), (1, slice(P, W))]
            block = ctx2.enter_context(nc.Block())

            @block.gpsimd
            def _(pool):
                nc.gpsimd.memset(mask[:], 0.0).then_inc(mask_made, 1)
                pool.wait_ge(mask_made, 1)
                for cols in (slice(0, P), slice(2 * P, W)):
                    nc.gpsimd.affine_select(out=mask[:, cols], in_=mask[:, cols], compare_op=ALU.is_ge, fill=LOWEST,
                                            base=0, pattern=[[-1, P]], channel_multiplier=1).then_inc(mask_made, 1)

            @block.tensor
            def _(pe):
                pe.wait_ge(wk_loaded, 16)
                for kh in range(KH):
                    out = s_ps[:, kh // 2, (kh % 2) * S:(kh % 2 + 1) * S]
                    for k in range(HC):
                        last = nc.tensor.matmul(out, wk[:, k, kh * D:(kh + 1) * D], xnT[:, k, :],
                                                start=(k == 0), stop=(k == HC - 1))
                last.then_inc(kv_done, 1)
                pe.wait_ge(wv_loaded, 16)
                for q in range(QT):
                    for k in range(HC):
                        last = nc.tensor.matmul(t_ps[:, q, :], xnT[:, k, q * P:(q + 1) * P], wv[:, k, :],
                                                start=(k == 0), stop=(k == HC - 1))
                last.then_inc(kv_done, 1)
                for i in range(H + 4):
                    if i < H:
                        h = i
                        if h % 4 == 0:
                            pe.wait_ge(wq_loaded[h // 4], 16)
                        at_least(pe, q_copied, h - 1)
                        for k in range(HC):
                            last = nc.tensor.matmul(q_ps[:, h % 2, 0:S], wq[:, k, h * D:(h + 1) * D], xnT[:, k, :],
                                                    start=(k == 0), stop=(k == HC - 1))
                        last.then_inc(q_done, 1)
                    if 0 <= i - 1 < H:
                        h = i - 1
                        pe.wait_ge(q_copied, h + 1)
                        if h == 0:
                            pe.wait_ge(kv_copied, 2)
                        at_least(pe, masked, h - 1)
                        kh = h // (H // KH)
                        nc.tensor.matmul(s_ps[:, h % 2, 0:P], qT[:, h % 2, 0:P], kT[:, kh, 0:P],
                                         start=True, stop=True)
                        nc.tensor.matmul(s_ps[:, h % 2, P:W], qT[:, h % 2, P:S], kT[:, kh, :],
                                         start=True, stop=True).then_inc(s_done, 1)
                    if 0 <= i - 3 < H:
                        h = i - 3
                        pe.wait_ge(normed, 2 * h + 2)
                        at_least(pe, t_copied, h - 1)
                        for j in range(3):
                            last = nc.tensor.transpose(t_ps[:, h % 2, j * P:(j + 1) * P],
                                                       scores[:, h % 2, j * P:(j + 1) * P], c["ident"][:])
                        last.then_inc(t_done, 1)
                    if 0 <= i - 4 < H:
                        h = i - 4
                        kh = h // (H // KH)
                        pe.wait_ge(t_copied, h + 1)
                        at_least(pe, o_copied, h - 1)
                        nc.tensor.matmul(o_ps[:, h % 2, 0:S], v[:, 0, kh * D:(kh + 1) * D], probsT[:, h % 2, 0:S],
                                         start=True, stop=False)
                        nc.tensor.matmul(o_ps[:, h % 2, P:S], v[:, 1, kh * D:(kh + 1) * D], probsT[:, h % 2, S:W],
                                         start=False, stop=True).then_inc(o_done, 1)

            @block.scalar
            def _(act):
                act.wait_ge(kv_done, 1)
                nc.scalar.activation(kT[:].rearrange("p h s -> p (h s)"), s_ps[:].rearrange("p b n -> p (b n)"),
                                     ACT.Copy).then_inc(kv_copied, 1)
                act.wait_ge(kv_done, 2)
                nc.scalar.activation(v[:], t_ps[:], ACT.Copy).then_inc(kv_copied, 1)
                for i in range(H + 4):
                    if i < H:
                        act.wait_ge(q_done, i + 1)
                        at_least(act, s_done, i - 1)
                        nc.scalar.activation(qT[:, i % 2, :], q_ps[:, i % 2, 0:S], ACT.Copy).then_inc(q_copied, 1)
                    if 0 <= i - 1 < H:
                        h = i - 1
                        act.wait_ge(max_done, 2 * h + 2)
                        at_least(act, rinv_done, h - 1)
                        for q, cols in parts:
                            nc.scalar.activation(scores[:, h % 2, cols], scores[:, h % 2, cols], ACT.Exp,
                                                 bias=negmax[:, h % 2, q:q + 1],
                                                 accum_out=sums[:, h % 2, q:q + 1]).then_inc(exp_done, 1)
                    if 0 <= i - 3 < H:
                        h = i - 3
                        act.wait_ge(t_done, h + 1)
                        at_least(act, o_done, h - 1)
                        nc.scalar.activation(probsT[:, h % 2, :], t_ps[:, h % 2, 0:W], ACT.Copy).then_inc(t_copied, 1)

            @block.vector
            def _(dve):
                dve.wait_ge(mask_made, 3)
                for i in range(H + 4):
                    if i < H:
                        h = i
                        dve.wait_ge(s_done, h + 1)
                        at_least(dve, t_done, h - 1)
                        nc.vector.tensor_tensor(scores[:, h % 2, :], s_ps[:, h % 2, 0:W], mask[:],
                                                ALU.add).then_inc(masked, 1)
                        dve.wait_ge(masked, h + 1)
                        at_least(dve, exp_done, 2 * h - 2)
                        for q, cols in parts:
                            nc.vector.tensor_reduce(negmax[:, h % 2, q:q + 1], scores[:, h % 2, cols], AX_X,
                                                    ALU.max, negate=True).then_inc(max_done, 1)
                    if 0 <= i - 1 < H:
                        h = i - 1
                        dve.wait_ge(exp_done, 2 * h + 2)
                        at_least(dve, normed, 2 * h - 2)
                        nc.vector.reciprocal(rinv[:, h % 2, :], sums[:, h % 2, :]).then_inc(rinv_done, 1)
                        dve.wait_ge(rinv_done, h + 1)
                        for q, cols in parts:
                            nc.vector.tensor_scalar(scores[:, h % 2, cols], scores[:, h % 2, cols],
                                                    rinv[:, h % 2, q:q + 1], None, ALU.mult).then_inc(normed, 1)
                    if 0 <= i - 4 < H:
                        h = i - 4
                        dve.wait_ge(o_done, h + 1)
                        nc.vector.tensor_copy(attnT[:, h, :], o_ps[:, h % 2, 0:S]).then_inc(o_copied, 1)
        output_projection(nc, c, "out1", attnT, H, wo, [(wo_loaded, 32)], bo[:], load_next)


E = 8
INNER = 2048
NI = INNER // P


class SmallWeights0:

    def __init__(self, nc, ctx, finished):
        t = Tiles(nc, ctx, "ffn0small", finished)
        self.gate = t.sb("gate", [P, HC, E])
        self.gamma, self.beta = t.sb("gamma", [P, HID]), t.sb("beta", [P, HID])
        self.loaded, self.up_loaded = t.sem("loaded"), [t.sem(f"up_loaded{i}") for i in range(4)]

    def load(self, sp, T, buffers):
        sp.dma_start(self.gate[:], T["gate"].rearrange("(k p) n -> p k n", p=P)).then_inc(self.loaded, 16)
        sp.dma_start(buffers.key_w[:], T["expert"].rearrange("(k p) n -> p k n", p=P)).then_inc(self.loaded, 16)
        for i in range(4):
            cols = slice(i * 512, (i + 1) * 512)
            sp.dma_start(buffers.wide_w[:, :, cols], T["up"].rearrange("(k p) n -> p k n", p=P)[:, :, cols])\
              .then_inc(self.up_loaded[i], 16)


def feed_forward_0(nc, T, c, buffers, small):
    with ExitStack() as ctx:
        t = Tiles(nc, ctx, "ffn0", c["finished"])
        up, down, expert, gate = buffers.wide_w, buffers.rows_w, buffers.key_w, small.gate
        gamma, beta = small.gamma, small.beta
        xnT = buffers.xnT
        small_loaded, up_loaded = small.loaded, small.up_loaded
        affine_loaded = t.sem("affine_loaded")
        down_loaded = [t.sem(f"down_loaded{i}") for i in range(4)]

        def load_down(sp):
            for i in range(4):
                part = slice(4 * i, 4 * i + 4)
                sp.dma_start(down[:, part, :], T["down"].rearrange("(i p) n -> p i n", p=P)[:, part, :])\
                  .then_inc(down_loaded[i], 16)
            sp.dma_start(gamma[:], T["gamma"].to_broadcast([P, HID])).then_inc(affine_loaded, 16)
            sp.dma_start(beta[:], T["beta"].to_broadcast([P, HID])).then_inc(affine_loaded, 16)

        layernorm_transposed(nc, c, "norm2", c["x"], xnT, load_down)
        with ExitStack() as ctx2:
            t = Tiles(nc, ctx2, "ffn0a", c["finished"])
            relu, hT = t.sb("relu", [P, 2, S]), buffers.heads
            top, route = t.sb("top", [P, QT, 8]), t.sb("route", [P, QT])
            y = t.sb("y", [P, QT, HID])
            stats, mv = t.sb("stats", [P, QT, 6]), t.sb("mv", [P, QT, 2])
            logvar, rstd = t.sb("logvar", [P, QT]), t.sb("rstd", [P, QT])
            gate_ps, expert_ps = t.psum("gate_ps", [P, QT, E]), t.psum("expert_ps", [P, QT, HID])
            up_ps, y_ps = t.psum("up_ps", [P, 2, CH]), t.psum("y_ps", [P, QT, HID])
            gate_done, up_done, relu_done, h_done, y_done, chain, moments_done, log_done, rstd_done = map(
                t.sem, ("gate_done", "up_done", "relu_done", "h_done", "y_done", "chain", "moments_done",
                        "log_done", "rstd_done"))
            block = ctx2.enter_context(nc.Block())

            @block.tensor
            def _(pe):
                pe.wait_ge(small_loaded, 32)
                for q in range(QT):
                    for k in range(HC):
                        nc.tensor.matmul(gate_ps[:, q, :], xnT[:, k, q * P:(q + 1) * P], gate[:, k, :],
                                         start=(k == 0), stop=(k == HC - 1))
                    for k in range(HC):
                        last = nc.tensor.matmul(expert_ps[:, q, :], xnT[:, k, q * P:(q + 1) * P], expert[:, k, :],
                                                start=(k == 0), stop=(k == HC - 1))
                last.then_inc(gate_done, 1)
                for i in range(NI + 1):
                    if i < NI:
                        if i % 4 == 0:
                            pe.wait_ge(up_loaded[i // 4], 16)
                        at_least(pe, relu_done, i - 1)
                        for k in range(HC):
                            last = nc.tensor.matmul(up_ps[:, i % 2, 0:S], up[:, k, i * P:(i + 1) * P], xnT[:, k, :],
                                                    start=(k == 0), stop=(k == HC - 1))
                        last.then_inc(up_done, 1)
                    if i > 0:
                        if (i - 1) % 4 == 0:
                            pe.wait_ge(down_loaded[(i - 1) // 4], 16)
                        pe.wait_ge(h_done, i)
                        for q in range(QT):
                            last = nc.tensor.matmul(y_ps[:, q, :], hT[:, i - 1, q * P:(q + 1) * P], down[:, i - 1, :],
                                                    start=(i == 1), stop=(i == NI))
                last.then_inc(y_done, 1)

            @block.scalar
            def _(act):
                for i in range(NI):
                    act.wait_ge(up_done, i + 1)
                    at_least(act, h_done, i - 1)
                    nc.scalar.activation(relu[:, i % 2, :], up_ps[:, i % 2, 0:S], ACT.Relu).then_inc(relu_done, 1)
                act.wait_ge(moments_done, QT)
                nc.scalar.activation(logvar[:], mv[:, :, 1], ACT.Ln, bias=c["eps5"][:]).then_inc(log_done, 1)
                act.wait_ge(log_done, 1)
                nc.scalar.activation(rstd[:], logvar[:], ACT.Exp, scale=-0.5).then_inc(rstd_done, 1)

            @block.vector
            def _(dve):
                steps = [0]

                def then_wait(instruction):
                    steps[0] += 1
                    instruction.then_inc(chain, 1)
                    dve.wait_ge(chain, steps[0])

                dve.wait_ge(gate_done, 1)
                for q in range(QT):
                    then_wait(nc.vector.max(top[:, q, :], gate_ps[:, q, :]))
                then_wait(nc.vector.tensor_tensor(route[:], top[:, :, 0], top[:, :, 1], ALU.add))
                for i in range(NI):
                    dve.wait_ge(relu_done, i + 1)
                    nc.vector.tensor_tensor(hT[:, i, :], relu[:, i % 2, :], relu[:, i % 2, :],
                                            ALU.mult).then_inc(h_done, 1)
                for q in range(QT):
                    then_wait(nc.vector.tensor_scalar(y[:, q, :], expert_ps[:, q, :], route[:, q:q + 1], None,
                                                      ALU.mult))
                dve.wait_ge(y_done, 1)
                for q in range(QT):
                    then_wait(nc.vector.tensor_tensor(y[:, q, :], y[:, q, :], y_ps[:, q, :], ALU.add))
                for q in range(QT):
                    then_wait(nc.vector.bn_stats(stats[:, q, :], y[:, q, :]))
                for q in range(QT):
                    nc.vector.bn_aggr(mv[:, q, :], stats[:, q, :]).then_inc(moments_done, 1)
                dve.wait_ge(moments_done, QT)
                dve.wait_ge(rstd_done, 1)
                dve.wait_ge(affine_loaded, 32)
                for q in range(QT):
                    then_wait(nc.vector.tensor_scalar(y[:, q, :], y[:, q, :], mv[:, q, 0:1], rstd[:, q:q + 1],
                                                      ALU.subtract, ALU.mult))
                for q in range(QT):
                    then_wait(nc.vector.tensor_tensor(y[:, q, :], y[:, q, :], gamma[:], ALU.mult))
                for q in range(QT):
                    then_wait(nc.vector.tensor_tensor(y[:, q, :], y[:, q, :], beta[:], ALU.add))
                nc.vector.tensor_tensor(c["x"][:], c["x"][:], y[:], ALU.add)


def group_layernorm(nc, dve, then_wait, c, tiles, src, dst, groups, width, sums_ready, rstd_ready):
    total, var_sum, rstd, centered, squares = tiles
    as_groups = lambda a: a.rearrange("p (g w) -> p g w", w=width)
    wide = lambda a: a.unsqueeze(2).to_broadcast([P, groups, width])
    then_wait(nc.vector.tensor_reduce(total, as_groups(src), AX_X, ALU.add))
    then_wait(nc.vector.tensor_scalar(total, total, -1.0 / width, None, ALU.mult))
    then_wait(nc.vector.tensor_tensor(as_groups(centered), as_groups(src), wide(total), ALU.add))
    then_wait(nc.vector.tensor_tensor(squares, centered, centered, ALU.mult))
    nc.vector.tensor_reduce(var_sum, as_groups(squares), AX_X, ALU.add).then_inc(sums_ready, 1)
    dve.wait_ge(rstd_ready, 1)
    then_wait(nc.vector.tensor_tensor(as_groups(dst), as_groups(centered), wide(rstd), ALU.mult))


def group_rstd(nc, act, c, width, var_sum, log_var, rstd, sums_ready, log_done, rstd_ready):
    act.wait_ge(sums_ready, 1)
    nc.scalar.activation(log_var, var_sum, ACT.Ln, bias=c["eps6"][:], scale=1.0 / width).then_inc(log_done, 1)
    act.wait_ge(log_done, 1)
    nc.scalar.activation(rstd, log_var, ACT.Exp, scale=-0.5).then_inc(rstd_ready, 1)


HD = 32
HG = P // HD
NG = H // HG
DCA = 16
MAIN = KV - DCA
SCALE1 = float(HD) ** -0.5


def cross1_queries(nc, T, c, xnT, qT, own, ctxT_hi, ctxT_lo, tiles, q_loaded, loaded):
    with ExitStack() as ctx:
        t = Tiles(nc, ctx, "queries1", c["finished"])
        wq, bq, wd, bd, bv, affine = (tiles[n] for n in ("wq", "bq", "wd", "bd", "bv", "affine"))
        mask_k, mask_v = t.sb("mask_k", [P, HG, DCA]), t.sb("mask_v", [P, P // DCA, HD])
        yT = t.sb("yT", [P, CC, P // DCA, DCA])
        q, qn = t.sb("q", [P, QT * HID]), t.sb("qn", [P, QT * HID])
        k, kn = t.sb("k", [P, HID]), t.sb("kn", [P, HID])
        centered, squares = t.sb("centered", [P, QT * HID]), t.sb("squares", [P, QT * HID])
        total, var_sum, log_var, rstd = (t.sb(n, [P, 4 * HID // HD]) for n in ("total", "var_sum", "log_var", "rstd"))
        kT = t.sb("kT", [P, NG, HG * DCA])
        vb = t.sb("vb", [P, 2, 8 * HD])
        prob, probT = t.sb("prob", [P, QT * H * DCA]), t.sb("probT", [P, 4 * P])
        best = t.sb("best", [P, QT * H])
        ps = t.psum("ps", [P, 8, CH])
        masks_made, mask_k_steps, mask_v_steps = map(
            t.sem, ("masks_made", "mask_k_steps", "mask_v_steps"))
        chain, y_made, projected, sums_q, sums_k, log_q, log_k, rstd_q, rstd_k = map(
            t.sem, ("chain", "y_made", "projected", "sums_q", "sums_k", "log_q", "log_k", "rstd_q", "rstd_k"))
        q_normed, k_normed, q_turned, k_turned, operands, scored, shifted, exped, p_normed, p_turned, p_copied, \
            out_done = map(t.sem, ("q_normed", "k_normed", "q_turned", "k_turned", "operands", "scored", "shifted",
                                   "exped", "p_normed", "p_turned", "p_copied", "out_done"))
        block = ctx.enter_context(nc.Block())
        NQ, NK = QT * HID // HD, HID // HD

        @block.gpsimd
        def _(pool):
            block_mask(nc, pool, mask_k_steps, mask_k, HG, HD, DCA)
            block_mask(nc, pool, mask_v_steps, mask_v, P // DCA, DCA, HD)
            nc.gpsimd.sem_inc(masks_made, 1)

        @block.tensor
        def _(pe):
            pe.wait_ge(q_loaded, 32)
            for qt in range(QT):
                for kk in range(HC):
                    nc.tensor.matmul(ps[:, qt, :], xnT[:, kk, qt * P:(qt + 1) * P], wq[:, kk, :],
                                     start=(kk == 0), stop=False)
                last = nc.tensor.matmul(ps[:, qt, :], c["ones"][0:1, :], bq[:], start=False, stop=True)
            last.then_inc(projected, 1)
            pe.wait_ge(loaded, 64)
            pe.wait_ge(y_made, CC)
            for part in range(2):
                cols = slice(part * HID, (part + 1) * HID)
                for kk in range(CC):
                    nc.tensor.matmul(ps[:, 2 + part, :], yT[:, kk].rearrange("p r t -> p (r t)"), wd[:, kk, cols],
                                     start=(kk == 0), stop=False)
                last = nc.tensor.matmul(ps[:, 2 + part, :], c["ones"][0:1, :], bd[:, cols], start=False, stop=True)
            last.then_inc(projected, 1)
            pe.wait_ge(q_normed, 1)
            for qt in range(QT):
                for g in range(NG):
                    last = nc.tensor.transpose(ps[:, 4 + qt, g * P:(g + 1) * P],
                                               qn[:, qt * HID + g * P:qt * HID + (g + 1) * P], c["ident"][:])
            last.then_inc(q_turned, 1)
            pe.wait_ge(k_normed, 1)
            for g in range(NG):
                last = nc.tensor.transpose(ps[:, 6, g * P:(g + 1) * P], kn[:, g * P:(g + 1) * P], c["ident"][:])
            last.then_inc(k_turned, 1)
            pe.wait_ge(operands, 1)
            for qt in range(QT):
                for g in range(NG):
                    at = qt * H * DCA + g * HG * DCA
                    last = nc.tensor.matmul(ps[:, 7, at:at + HG * DCA], qT[:, g, qt * P:(qt + 1) * P], kT[:, g, :],
                                            start=True, stop=True)
            last.then_inc(scored, 1)
            pe.wait_ge(p_normed, 1)
            for n in range(4):
                last = nc.tensor.transpose(ps[:, 0, n * P:(n + 1) * P], prob[:, n * P:(n + 1) * P], c["ident"][:])
            last.then_inc(p_turned, 1)
            pe.wait_ge(p_copied, 1)
            for qt in range(QT):
                for half in range(2):
                    last = nc.tensor.matmul(ps[:, 1 + qt, half * S:(half + 1) * S],
                                            probT[:, (2 * qt + half) * P:(2 * qt + half + 1) * P], vb[:, half, :],
                                            start=True, stop=True)
            last.then_inc(out_done, 1)

        @block.scalar
        def _(act):
            group_rstd(nc, act, c, HD, var_sum[:, 0:NQ], log_var[:, 0:NQ], rstd[:, 0:NQ], sums_q, log_q, rstd_q)
            group_rstd(nc, act, c, HD, var_sum[:, NQ:NQ + NK], log_var[:, NQ:NQ + NK], rstd[:, NQ:NQ + NK],
                       sums_k, log_k, rstd_k)
            act.wait_ge(shifted, 1)
            nc.scalar.activation(prob[:], prob[:], ACT.Exp, scale=SCALE1).then_inc(exped, 1)
            act.wait_ge(p_turned, 1)
            nc.scalar.activation(probT[:], ps[:, 0, :], ACT.Copy).then_inc(p_copied, 1)

        @block.vector
        def _(dve):
            steps = [0]

            def then_wait(instruction):
                steps[0] += 1
                instruction.then_inc(chain, 1)
                dve.wait_ge(chain, steps[0])

            for kk in range(CC):
                wide = lambda a: a[:, kk:kk + 1, MAIN:KV].to_broadcast([P, P // DCA, DCA])
                nc.vector.tensor_tensor(yT[:, kk], wide(ctxT_hi).bitcast(F32), wide(ctxT_lo).bitcast(F32),
                                        ALU.add).then_inc(y_made, 1)
            dve.wait_ge(projected, 1)
            for qt in range(QT):
                then_wait(nc.vector.tensor_copy(q[:, qt * HID:(qt + 1) * HID], ps[:, qt, :]))
            group_layernorm(nc, dve, then_wait, c, (total[:, 0:NQ], var_sum[:, 0:NQ], rstd[:, 0:NQ], centered[:],
                                                    squares[:]), q[:], qn[:], NQ, HD, sums_q, rstd_q)
            nc.vector.sem_inc(q_normed, 1)
            dve.wait_ge(projected, 2)
            then_wait(nc.vector.tensor_copy(k[:], ps[:, 2, :]))
            group_layernorm(nc, dve, then_wait, c,
                            (total[:, NQ:NQ + NK], var_sum[:, NQ:NQ + NK], rstd[:, NQ:NQ + NK], centered[:, 0:HID],
                             squares[:, 0:HID]), k[:], kn[:], NK, HD, sums_k, rstd_k)
            nc.vector.sem_inc(k_normed, 1)
            dve.wait_ge(masks_made, 1)
            for half in range(2):
                then_wait(nc.vector.tensor_tensor(vb[:, half, :], ps[:, 3, half * S:(half + 1) * S],
                                                  mask_v[:].rearrange("p b w -> p (b w)"), ALU.mult))
            dve.wait_ge(loaded, 64)
            dve.wait_ge(q_turned, 1)
            for qt in range(QT):
                then_wait(nc.vector.tensor_scalar(qT[:, :, qt * P:(qt + 1) * P],
                                                  ps[:, 4 + qt, :].rearrange("p (g s) -> p g s", g=NG),
                                                  affine[:, 0:1], affine[:, 1:2], ALU.mult, ALU.add))
            dve.wait_ge(k_turned, 1)
            for g in range(NG):
                then_wait(nc.vector.tensor_scalar(kT[:, g, :], ps[:, 6, g * P:g * P + HG * DCA],
                                                  affine[:, 2:3], affine[:, 3:4], ALU.mult, ALU.add))
                then_wait(nc.vector.tensor_tensor(kT[:, g, :], kT[:, g, :], mask_k[:].rearrange("p b w -> p (b w)"),
                                                  ALU.mult))
            nc.vector.sem_inc(operands, 1)
            dve.wait_ge(scored, 1)
            as_groups = lambda a: a.rearrange("p (g w) -> p g w", w=DCA)
            wide = best[:].unsqueeze(2).to_broadcast([P, QT * H, DCA])
            then_wait(nc.vector.tensor_reduce(best[:], as_groups(ps[:, 7, :]), AX_X, ALU.max))
            nc.vector.tensor_tensor(as_groups(prob[:]), as_groups(ps[:, 7, :]), wide, ALU.subtract)\
              .then_inc(shifted, 1)
            dve.wait_ge(exped, 1)
            then_wait(nc.vector.tensor_reduce(best[:], as_groups(prob[:]), AX_X, ALU.add))
            then_wait(nc.vector.reciprocal(best[:], best[:]))
            nc.vector.tensor_tensor(as_groups(prob[:]), as_groups(prob[:]), wide, ALU.mult).then_inc(p_normed, 1)
            dve.wait_ge(out_done, 1)
            for qt in range(QT):
                nc.vector.tensor_tensor(own[:, qt, :], ps[:, 1 + qt, :], bv[:], ALU.add)


def cross1_attention(nc, T, c, qT, attn, ctxT_hi, ctxT_lo):
    NU = NCH
    GW = 2 * HG * HD
    with ExitStack() as ctx:
        t = Tiles(nc, ctx, "cross1", c["finished"])
        w_raw = t.sb("w_raw", [P, CC, GW])
        w_hi, w_lo = t.sb("w_hi", [P, CC, GW], F32R), t.sb("w_lo", [P, CC, GW], F32R)
        bk_raw, bk_high, bk_rows = t.sb("bk_raw", [2, P]), t.sb("bk_high", [2, P], F32R), t.sb("bk_rows", [2, P], F32R)
        row_kinds = t.sb("row_kinds", [2, 2])
        of_high, of_raw = row_kinds[:, 0:1], row_kinds[:, 1:2]
        ones_r = t.sb("ones_r", [2, P], F32R)
        affine = t.sb("affine", [P, 2])
        w_mean, b_mean = t.sb("w_mean", [P, CC * HG]), t.sb("b_mean", [2, HG])
        q_hi, q_lo = t.sb("q_hi", [P, S], F32R), t.sb("q_lo", [P, S], F32R)
        kT_hi, kT_lo = t.sb("kT_hi", [P, KV], F32R), t.sb("kT_lo", [P, KV], F32R)
        v_hl = t.sb("v_hl", [P, NT, HG, 2 * HD], F32R)
        var_sum, log_var, rstd = (t.sb(n, [P, TPC * HG]) for n in ("var_sum", "log_var", "rstd"))
        probs = t.sb("probs", [P, QT, KV])
        pt_hi, pt_lo = t.sb("pt_hi", [P, 2, QT, CH], F32R), t.sb("pt_lo", [P, 2, QT, CH], F32R)
        work = t.sb("work", [P, CH])
        squares, kn = work, work
        k_full = t.sb("k_full", [P, CH])
        chunk_max, chunk_sum = t.sb("chunk_max", [P, QT, NCH]), t.sb("chunk_sum", [P, QT, NCH])
        of_rows = t.sb("of_rows", [P, 3 * QT])
        negmax, rowsum, rinv = (of_rows[:, i * QT:(i + 1) * QT] for i in range(3))
        outT = w_raw[:, 0, :]
        add_parts = t.sb("add_parts", [P, 2, HD])
        ps = t.psum("ps", [P, 8, CH])

        def kv_banks(before, u):
            first = 2 * (u % 2) if before is None else 2
            return ps[:, first:first + 2, :].rearrange("p b (t n) -> p (b t) n", n=GW)

        bias_rows_ready = t.sem("bias_rows_ready")
        w_loaded, const_loaded, prepared, w_ready, q_ready = map(
            t.sem, ("w_loaded", "const_loaded", "prepared", "w_ready", "q_ready"))
        kv_done, sq_done, vhi_done, sums_done, log_done, rstd_done, kn_done, vlo_done = map(
            t.sem, ("kv_done", "sq_done", "vhi_done", "sums_done", "log_done", "rstd_done", "kn_done", "vlo_done"))
        kt_done, khi_done, kfull_done, klo_done = map(t.sem, ("kt_done", "khi_done", "kfull_done", "klo_done"))
        s_done, scored, exp_done, t_done, pthi_done, ptlo_done = map(
            t.sem, ("s_done", "scored", "exp_done", "t_done", "pthi_done", "ptlo_done"))
        o_done = t.sem("o_done")
        max_done, sum_done, rinv_done, outT_done, turned_back, norm_done, chain_w = map(
            t.sem, ("max_done", "sum_done", "rinv_done", "outT_done", "turned_back", "norm_done",
                    "chain_w"))
        block = ctx.enter_context(nc.Block())

        def groups_loop(nc_engine, steps, units):
            units(None, 0)
            steps(0)
            units(0, 1)
            with nc_engine.Fori(1, NG - 1) as g:
                steps(g)
                units(g, g + 1)
            steps(NG - 1)
            units(NG - 1, None)

        def turned_bank(j, ch):
            return 0 if j == HG - 1 else 2 * (ch % 2)

        def width(ch):
            return min(CH, MAIN - ch * CH)

        @block.sync
        def _(sp):
            sp.dma_start(affine[:], T["affine_k1"]).then_inc(const_loaded, 16)

            def load(g):
                sp.dma_start(w_raw[:].rearrange("p k n -> p (k n)"), T["wkv1"][bass.ds(g * P, P), :])\
                  .then_inc(w_loaded, 16)
                sp.dma_start(bk_raw[:], T["bk1"][0:1, bass.ds(g * P, P)].to_broadcast([2, P])).then_inc(w_loaded, 16)

            def load_next(g):
                sp.wait_ge(w_ready, g + 1)
                sp.wait_ge(turned_back, HG * g + 2)
                load(g + 1)

            load(0)
            load_next(0)
            with nc.sync.Fori(1, NG - 1) as g:
                load_next(g)

        @block.gpsimd
        def _(pool):
            nc.gpsimd.memset(probs[:, :, MAIN:KV], 0.0).then_inc(prepared, 1)
            nc.gpsimd.memset(of_high, -1.0).then_inc(bias_rows_ready, 1)
            nc.gpsimd.memset(of_raw, 1.0).then_inc(bias_rows_ready, 1)
            pool.wait_ge(bias_rows_ready, 2)
            nc.gpsimd.memset(row_kinds[0:1, 0:1], 1.0).then_inc(bias_rows_ready, 1)
            nc.gpsimd.memset(row_kinds[0:1, 1:2], 0.0).then_inc(bias_rows_ready, 1)

            nc.gpsimd.tensor_copy(add_parts[:], c["ident"][:].rearrange("p (h s n) -> p h s n", h=2, s=2)[:, :, 0, :])\
                .then_inc(bias_rows_ready, 1)
            pool.wait_ge(bias_rows_ready, 5)
            nc.gpsimd.tensor_tensor(add_parts[:], add_parts[:],
                                    c["ident"][:].rearrange("p (h s n) -> p h s n", h=2, s=2)[:, :, 1, :],
                                    ALU.add).then_inc(prepared, 1)

            def steps(g):
                pass

            def units(before, g):
                for u in range(NU - 1 if g is not None else 0):
                    n = NU * g + u
                    cols = slice(u * CH, (u + 1) * CH)
                    pool.wait_ge(kfull_done, n + 1)
                    nc.gpsimd.tensor_tensor(kT_lo[:, cols], k_full[:], kT_hi[:, cols].bitcast(F32),
                                            ALU.subtract).then_inc(klo_done, 1)

            groups_loop(nc.gpsimd, steps, units)

        @block.tensor
        def _(pe):
            def keys_values(before, g, u):
                n = NU * g + u
                if u == 0:
                    pe.wait_ge(w_ready, g + 1)
                    if isinstance(g, int) and g == 0:
                        pe.wait_ge(prepared, 3)
                lag = 1 if before is None else 0
                at_least(pe, kn_done, n - lag)
                at_least(pe, vlo_done, n - lag)
                for j in range(TPC):
                    out = kv_banks(before, u)[:, j, :]
                    tile = slice((u * TPC + j) * P, (u * TPC + j + 1) * P)
                    for k in range(CC):
                        nc.tensor.matmul(out, ctxT_hi[:, k, tile], w_hi[:, k, :], start=(k == 0), stop=False)
                        nc.tensor.matmul(out, ctxT_hi[:, k, tile], w_lo[:, k, :], start=False, stop=False)
                        nc.tensor.matmul(out, ctxT_lo[:, k, tile], w_hi[:, k, :], start=False, stop=False)
                    last = nc.tensor.matmul(out[:, 0:P], ones_r[:], bk_rows[:], start=False, stop=True)
                last.then_inc(kv_done, 1)

            def turn_keys(g, u):
                n = NU * g + u
                pe.wait_ge(kn_done, n + 1)
                at_least(pe, kfull_done, n)
                if u == 0:
                    at_least(pe, norm_done, 2 * HG * g - 2)
                for j in range(TPC):
                    last = nc.tensor.transpose(ps[:, 4, j * P:(j + 1) * P], kn[:, j * P:(j + 1) * P],
                                               c["ident"][:])
                last.then_inc(kt_done, 1)

            def scores(g, j, ch):
                rows = slice(j * HD, (j + 1) * HD)
                cols = slice(ch * CH, ch * CH + width(ch))
                h = HG * g + j
                if j == 0 and ch == 0:
                    pe.wait_ge(q_ready, 2 * g + 2)
                if j == 0:
                    pe.wait_ge(klo_done, NU * g + ch + 1)
                for q in range(QT):
                    at_least(pe, scored, 16 * h + 2 * ch + q - 1)
                    out = ps[:, 6 + q, 0:width(ch)]
                    tokens = slice(q * P, (q + 1) * P)
                    nc.tensor.matmul(out, q_hi[rows, tokens], kT_hi[rows, cols], start=True, stop=False)
                    nc.tensor.matmul(out, q_hi[rows, tokens], kT_lo[rows, cols], start=False, stop=False)
                    nc.tensor.matmul(out, q_lo[rows, tokens], kT_hi[rows, cols],
                                     start=False, stop=True).then_inc(s_done, 1)

            def transposes(g, j, ch):
                for q in range(QT):
                    pe.wait_ge(exp_done, 16 * (HG * g + j) + 2 * ch + q + 1)
                    for i in range(TPC):
                        at = ch * CH + i * P
                        last = nc.tensor.transpose(ps[:, turned_bank(j, ch) + q, i * P:(i + 1) * P], probs[:, q, at:at + P],
                                                   c["ident"][:])
                    last.then_inc(t_done, 1)

            def values(g, j, ch):
                h = HG * g + j
                n = 16 * h + 2 * ch
                pe.wait_ge(pthi_done, n + 2)
                pe.wait_ge(ptlo_done, n + 2)
                if ch == 0:
                    at_least(pe, norm_done, 2 * h - 2)
                if ch == 0 and j == 0:
                    pe.wait_ge(kfull_done, NU * g + NU)
                    pe.wait_ge(vlo_done, NU * g + NU)
                out = ps[:, 4 + j % 2, 0:S].rearrange("p (q t) -> p q t", q=QT)
                heads = slice(j - j % 2, j - j % 2 + 2)
                for i in range(TPC):
                    tile, cols = ch * TPC + i, slice(i * P, (i + 1) * P)
                    v = v_hl[:, tile, heads, :].rearrange("p h n -> p (h n)")
                    nc.tensor.matmul(out, v, pt_hi[:, ch % 2, :, cols], start=(tile == 0), stop=False)
                    last = nc.tensor.matmul(out, v, pt_lo[:, ch % 2, :, cols], start=False, stop=(tile == NT - 1))
                last.then_inc(o_done, 1)

            def turn_back(g, j):
                pe.wait_ge(outT_done, HG * g + j + 1)
                for q in range(QT):
                    last = nc.tensor.matmul(ps[:, 4 + j % 2, S + q * HD:S + (q + 1) * HD],
                                            outT[:, q * P:(q + 1) * P], add_parts[:, j % 2, :],
                                            start=True, stop=True)
                last.then_inc(turned_back, 1)

            def steps(g):
                for j in range(1, HG):
                    for ch in range(NCH):
                        transposes(g, j - 1, ch)
                        scores(g, j, ch)
                        if ch > 0:
                            values(g, j - 1, ch - 1)
                        if j > 1 and ch == 1:
                            turn_back(g, j - 2)
                    values(g, j - 1, NCH - 1)

            def units(before, g):
                for u in range(NU + 2):
                    if before is not None:
                        if 0 < u < NCH or u == NCH and g is None:
                            values(before, HG - 1, u - 1)
                        if u < NCH:
                            transposes(before, HG - 1, u)
                        if u == 0:
                            turn_back(before, HG - 2)
                    if before is None and u < NU:
                        keys_values(before, g, u)
                    if g is not None:
                        if u > 1:
                            scores(g, 0, u - 2)
                        if 0 < u <= NU:
                            turn_keys(g, u - 1)
                        if before is not None and u == NU:
                            values(before, HG - 1, NCH - 1)
                        if before is not None and u < NU:
                            keys_values(before, g, u)
                if before is not None:
                    turn_back(before, HG - 1)

            groups_loop(nc.tensor, steps, units)

        @block.scalar
        def _(act):
            nc.scalar.activation(ones_r[:], c["ones"][0:2, :], ACT.Copy).then_inc(prepared, 1)
            act.wait_ge(const_loaded, 16)

            def exps(h, ch):
                if ch == 0:
                    act.wait_ge(max_done, h + 1)
                    at_least(act, sum_done, h)
                cols = slice(ch * CH, ch * CH + width(ch))
                for q in range(QT):
                    nc.scalar.activation(probs[:, q, cols], probs[:, q, cols], ACT.Exp, bias=negmax[:, q:q + 1],
                                         accum_out=chunk_sum[:, q, ch:ch + 1]).then_inc(exp_done, 1)

            def probs_high(h, j, ch):
                for q in range(QT):
                    n = 16 * h + 2 * ch + q
                    act.wait_ge(t_done, n + 1)
                    at_least(act, o_done, 8 * h + ch - 1)
                    nc.scalar.activation(pt_hi[:, ch % 2, q, :], ps[:, turned_bank(j, ch) + q, :],
                                         ACT.Copy).then_inc(pthi_done, 1)

            def copy_output(g, j):
                h = HG * g + j
                act.wait_ge(o_done, 8 * h + 8)
                at_least(act, turned_back, h)
                if j >= HG - 2:
                    act.wait_ge(w_ready, NG if isinstance(g, int) and g == NG - 1 else g + 2)
                nc.scalar.activation(outT, ps[:, 4 + j % 2, 0:S], ACT.Copy).then_inc(outT_done, 1)

            def squares_of_keys(before, g, u):
                n = NU * g + u
                act.wait_ge(kv_done, n + 1)
                at_least(act, kt_done, n)
                nc.scalar.activation(squares[:].rearrange("p (t n) -> p t n", t=TPC), kv_banks(before, u)[:, :, 0:P],
                                     ACT.Square).then_inc(sq_done, 1)

            def values_high(before, g, u):
                if before is not None:
                    act.wait_ge(o_done, 8 * (HG * before + HG - 1) + u + 1)
                tiles = slice(u * TPC, (u + 1) * TPC)
                nc.scalar.activation(v_hl[:, tiles, :, 0:HD],
                                     kv_banks(before, u)[:, :, P:2 * P].rearrange("p t (h d) -> p t h d", h=HG),
                                     ACT.Copy).then_inc(vhi_done, 1)

            def keys_rstd(g, u):
                n = NU * g + u
                act.wait_ge(sums_done, n + 1)
                at_least(act, rstd_done, n)
                nc.scalar.activation(log_var[:], var_sum[:], ACT.Ln, bias=c["eps6"][:],
                                     scale=1.0 / HD).then_inc(log_done, 1)
                act.wait_ge(log_done, n + 1)
                at_least(act, kn_done, n)
                nc.scalar.activation(rstd[:], log_var[:], ACT.Exp, scale=-0.5).then_inc(rstd_done, 1)

            def keys_high(g, u):
                cols = slice(u * CH, (u + 1) * CH)
                act.wait_ge(kt_done, NU * g + u + 1)
                if u == 0:
                    at_least(act, s_done, 64 * g)
                nc.scalar.activation(kT_hi[:, cols], ps[:, 4, :], ACT.Identity,
                                     bias=affine[:, 1:2], scale=affine[:, 0:1]).then_inc(khi_done, 1)

            def steps(g):
                for j in range(1, HG):
                    h = HG * g + j - 1
                    for ch in range(NCH):
                        probs_high(h, j - 1, ch)
                        if ch + 1 < NCH:
                            exps(h, ch + 1)
                        else:
                            exps(h + 1, 0)
                    copy_output(g, j - 1)

            def units(before, g):
                for u in range(NU + 1):
                    if g is not None and u > 0:
                        squares_of_keys(before, g, u - 1)
                        if u < NU:
                            values_high(before, g, u - 1)
                        keys_rstd(g, u - 1)
                    if before is not None and u < NCH:
                        h = HG * before + HG - 1
                        probs_high(h, HG - 1, u)
                    if g is not None and u > 0:
                        keys_high(g, u - 1)
                        if u == NU:
                            values_high(before, g, u - 1)
                    if before is not None and u + 1 < NCH:
                        exps(h, u + 1)
                if before is not None:
                    copy_output(before, HG - 1)
                if g is not None:
                    exps(HG * g, 0)

            groups_loop(nc.scalar, steps, units)

        @block.vector
        def _(dve):
            def normalise(g, j):
                h = HG * g + j
                dve.wait_ge(rinv_done, h + 1)
                dve.wait_ge(turned_back, h + 1)
                for q in range(QT):
                    at = S + q * HD
                    nc.vector.tensor_scalar(attn[:, bass.ds(q * HID + g * P + j * HD, HD)],
                                            ps[:, 4 + j % 2, at:at + HD], rinv[:, q:q + 1], None,
                                            ALU.mult).then_inc(norm_done, 1)

            def scale_scores(h, ch):
                if ch == 0:
                    at_least(dve, max_done, h)
                for q in range(QT):
                    n = 16 * h + 2 * ch + q
                    dve.wait_ge(s_done, n + 1)
                    at_least(dve, t_done, n - 15)
                    nc.vector.tensor_scalar(probs[:, q, ch * CH:ch * CH + width(ch)],
                                            ps[:, 6 + q, 0:width(ch)], SCALE1, None, ALU.mult, ALU.max,
                                            accum_out=chunk_max[:, q, ch:ch + 1]).then_inc(scored, 1)

            def greatest(h):
                dve.wait_ge(scored, 16 * h + 16)
                at_least(dve, exp_done, 16 * h)
                nc.vector.tensor_reduce(negmax, chunk_max[:], AX_X, ALU.max, negate=True).then_inc(max_done, 1)

            keys = w_raw[:, :, 0:P].rearrange("p k (h d) -> p k h d", h=HG)
            mean = w_mean[:].rearrange("p (k h) -> p k h", h=HG)
            bias = bk_raw[:].rearrange("p (h d) -> p h d", h=HG)

            def prepare_weights(g, part):
                done = [11 * g + (0, 3, 6, 9)[part]]

                def then_wait(instruction):
                    done[0] = done[0] + 1
                    instruction.then_inc(chain_w, 1)
                    dve.wait_ge(chain_w, done[0])

                if part == 0:
                    dve.wait_ge(w_loaded, 32 * g + 32)
                    if isinstance(g, int) and g == 0:
                        dve.wait_ge(bias_rows_ready, 4)
                    at_least(dve, kv_done, NU * g)
                    then_wait(nc.vector.tensor_reduce(mean, keys, AX_X, ALU.add))
                    then_wait(nc.vector.tensor_reduce(b_mean[:], bias, AX_X, ALU.add))
                    then_wait(nc.vector.tensor_scalar(w_mean[:], w_mean[:], -1.0 / HD, None, ALU.mult))
                elif part == 1:
                    then_wait(nc.vector.tensor_scalar(b_mean[:], b_mean[:], -1.0 / HD, None, ALU.mult))
                    then_wait(nc.vector.tensor_tensor(keys, keys, mean.unsqueeze(3).to_broadcast([P, CC, HG, HD]),
                                                      ALU.add))
                    then_wait(nc.vector.tensor_tensor(bias, bias, b_mean[:].unsqueeze(2).to_broadcast([2, HG, HD]),
                                                      ALU.add))
                elif part == 2:
                    then_wait(nc.vector.tensor_copy(w_hi[:], w_raw[:]))
                    then_wait(nc.vector.tensor_copy(bk_high[:], bk_raw[:]))
                    then_wait(nc.vector.tensor_scalar(bk_raw[:], bk_raw[:], of_raw, None, ALU.mult))
                else:
                    then_wait(nc.vector.scalar_tensor_tensor(bk_rows[:], bk_high[:].bitcast(F32), of_high, bk_raw[:],
                                                             ALU.mult, ALU.add))
                    then_wait(nc.vector.tensor_tensor(w_lo[:], w_raw[:], w_hi[:].bitcast(F32), ALU.subtract))
                    nc.vector.sem_inc(w_ready, 1)

            def split_queries(g):
                at_least(dve, s_done, 64 * g)
                q_g = qT[:, bass.ds(g * S, S)]
                nc.vector.tensor_scalar(q_hi[:], q_g, 1.0, None, ALU.mult).then_inc(q_ready, 1)
                dve.wait_ge(q_ready, 2 * g + 1)
                nc.vector.tensor_tensor(q_lo[:], q_g, q_hi[:].bitcast(F32), ALU.subtract).then_inc(q_ready, 1)

            def probs_low(h, j, ch):
                for q in range(QT):
                    n = 16 * h + 2 * ch + q
                    dve.wait_ge(pthi_done, n + 1)
                    at_least(dve, o_done, 8 * h + ch - 1)
                    nc.vector.tensor_tensor(pt_lo[:, ch % 2, q, :], ps[:, turned_bank(j, ch) + q, :],
                                            pt_hi[:, ch % 2, q, :].bitcast(F32), ALU.subtract).then_inc(ptlo_done, 1)

            def sum_rows(h):
                dve.wait_ge(exp_done, 16 * h + 16)
                at_least(dve, norm_done, 2 * h)
                nc.vector.tensor_reduce(rowsum, chunk_sum[:], AX_X, ALU.add).then_inc(sum_done, 1)

            def invert_rows(h):
                dve.wait_ge(sum_done, h + 1)
                nc.vector.reciprocal(rinv, rowsum).then_inc(rinv_done, 1)

            def variances(g, u):
                n = NU * g + u
                dve.wait_ge(sq_done, n + 1)
                at_least(dve, log_done, n)
                nc.vector.tensor_reduce(var_sum[:], squares[:].rearrange("p (n d) -> p n d", d=HD), AX_X,
                                        ALU.add).then_inc(sums_done, 1)

            def values_low(before, g, u):
                dve.wait_ge(vhi_done, NU * g + u + 1)
                tiles = slice(u * TPC, (u + 1) * TPC)
                nc.vector.tensor_tensor(
                    v_hl[:, tiles, :, HD:2 * HD],
                    kv_banks(before, u)[:, :, P:2 * P].rearrange("p t (h d) -> p t h d", h=HG),
                    v_hl[:, tiles, :, 0:HD].bitcast(F32), ALU.subtract).then_inc(vlo_done, 1)

            def keys_normed(before, g, u):
                dve.wait_ge(rstd_done, NU * g + u + 1)
                nc.vector.tensor_tensor(
                    kn[:].rearrange("p (t h d) -> p t h d", t=TPC, h=HG),
                    kv_banks(before, u)[:, :, 0:P].rearrange("p t (h d) -> p t h d", h=HG),
                    rstd[:].rearrange("p (t h) -> p t h", t=TPC).unsqueeze(3).to_broadcast([P, TPC, HG, HD]),
                    ALU.mult).then_inc(kn_done, 1)

            def keys_full(g, u):
                n = NU * g + u
                dve.wait_ge(khi_done, n + 1)
                at_least(dve, klo_done, n)
                nc.vector.tensor_scalar(k_full[:], ps[:, 4, :], affine[:, 0:1], affine[:, 1:2],
                                        ALU.mult, ALU.add).then_inc(kfull_done, 1)

            def steps(g):
                has_next = not (isinstance(g, int) and g == NG - 1)
                for j in range(1, HG):
                    h = HG * g + j
                    for ch in range(NCH):
                        probs_low(h - 1, j - 1, ch)
                        scale_scores(h, ch)
                        if j > 1 and ch == 1:
                            normalise(g, j - 2)
                        if j == HG - 1 and 3 <= ch < 7 and has_next:
                            prepare_weights(g + 1, ch - 3)
                    sum_rows(h - 1)
                    greatest(h)
                    invert_rows(h - 1)

            def units(before, g):
                for u in range(NU + 2):
                    if g is not None and 0 < u <= NU:
                        variances(g, u - 1)
                        if u < NU:
                            values_low(before, g, u - 1)
                        keys_normed(before, g, u - 1)
                    if g is not None and u == NU:
                        scale_scores(HG * g, u - 2)
                    if before is not None and u < NCH:
                        probs_low(HG * before + HG - 1, HG - 1, u)
                    if before is not None and u == 0:
                        normalise(before, HG - 2)
                        if g is not None:
                            split_queries(g)
                    if g is not None and 0 < u <= NU:
                        keys_full(g, u - 1)
                    if g is not None and u == NU:
                        dve.wait_ge(kfull_done, NU * g + NU)
                        cols = slice((NU - 1) * CH, NU * CH)
                        nc.vector.tensor_tensor(kT_lo[:, cols], k_full[:], kT_hi[:, cols].bitcast(F32),
                                                ALU.subtract).then_inc(klo_done, 1)
                        values_low(before, g, u - 1)
                    if g is not None and u > 1 and u != NU:
                        scale_scores(HG * g, u - 2)
                if before is not None:
                    sum_rows(HG * before + HG - 1)
                if g is not None:
                    greatest(HG * g)
                if before is not None:
                    invert_rows(HG * before + HG - 1)
                    normalise(before, HG - 1)

            for part in range(4):
                prepare_weights(0, part)
            split_queries(0)
            groups_loop(nc.vector, steps, units)


def transpose_tokens(nc, c, stage, parts, outT):
    with ExitStack() as ctx:
        t = Tiles(nc, ctx, stage, c["finished"])
        turned = t.psum("turned", [P, QT, HID])
        summed, transposed = t.sem("summed"), t.sem("transposed")
        block = ctx.enter_context(nc.Block())

        @block.vector
        def _(dve):
            for q in range(QT):
                if len(parts) == 2:
                    nc.vector.tensor_tensor(parts[0][:, q, :], parts[0][:, q, :], parts[1][:, q, :],
                                            ALU.add).then_inc(summed, 1)
                else:
                    nc.vector.sem_inc(summed, 1)

        @block.tensor
        def _(pe):
            for q in range(QT):
                pe.wait_ge(summed, q + 1)
                for k in range(HC):
                    last = nc.tensor.transpose(turned[:, q, k * P:(k + 1) * P], parts[0][:, q, k * P:(k + 1) * P],
                                               c["ident"][:])
                last.then_inc(transposed, 1)

        @block.scalar
        def _(act):
            for q in range(QT):
                act.wait_ge(transposed, q + 1)
                nc.scalar.activation(outT[:, :, q * P:(q + 1) * P],
                                     turned[:, q, :].rearrange("p (k t) -> p k t", k=HC), ACT.Copy)


def cross_attention_1(nc, T, c, ctxT_hi, ctxT_lo):
    with ExitStack() as ctx:
        t = Tiles(nc, ctx, "layer1cross", c["finished"])
        qT = t.sb("qT", [P, NG, S])
        own = t.sb("own", [P, QT, HID])
        attn = t.sb("attn", [P, QT, HID])
        with ExitStack() as ctx2:
            t2 = Tiles(nc, ctx2, "layer1cross_in", c["finished"])
            xnT = t2.sb("xnT", [P, HC, S])
            tiles = {n: t2.sb(n, shape) for n, shape in (
                ("wq", [P, HC, HID]), ("bq", [1, HID]), ("wd", [P, CC, 2 * HID]), ("bd", [1, 2 * HID]),
                ("bv", [P, HID]), ("affine", [P, 4]))}
            q_loaded, loaded = t2.sem("q_loaded"), t2.sem("loaded")

            def load_weights(sp):
                sp.dma_start(tiles["wq"][:], T["wq1"].rearrange("(k p) n -> p k n", p=P)).then_inc(q_loaded, 16)
                sp.dma_start(tiles["bq"][:], T["bq1"]).then_inc(q_loaded, 16)
                sp.dma_start(tiles["wd"][:], T["wkv_dca"].rearrange("(k p) n -> p k n", p=P)).then_inc(loaded, 16)
                sp.dma_start(tiles["bd"][:], T["bkv_dca"]).then_inc(loaded, 16)
                sp.dma_start(tiles["affine"][:], T["affine1"]).then_inc(loaded, 16)
                sp.dma_start(tiles["bv"][:], T["bv1"].to_broadcast([P, HID])).then_inc(loaded, 16)

            layernorm_transposed(nc, c, "norm3", c["x"], xnT, load_weights)
            cross1_queries(nc, T, c, xnT, qT, own, ctxT_hi, ctxT_lo, tiles, q_loaded, loaded)
        cross1_attention(nc, T, c, qT[:].rearrange("p g s -> p (g s)"), attn[:].rearrange("p q n -> p (q n)"),
                         ctxT_hi, ctxT_lo)
        wo, bo = t.sb("wo", [P, HC, HID]), t.sb("bo", [1, HID])
        attnT = t.sb("attnT", [P, HC, S])
        wo_loaded = t.sem("wo_loaded")
        with nc.Block() as block:
            @block.sync
            def _(sp):
                sp.dma_start(wo[:], T["wo1"].rearrange("(k p) n -> p k n", p=P)).then_inc(wo_loaded, 16)
                sp.dma_start(bo[:], T["bo1"]).then_inc(wo_loaded, 16)
        transpose_tokens(nc, c, "turn3", (attn, own), attnT)
        output_projection(nc, c, "out3", attnT, HC, wo, [(wo_loaded, 32)], bo[:])


TOPK = 64
PREFIX = 4
MASKED = -1.5e38
REPLACED = -float(2 ** 127)


ROUND = 12582912.0
MEANS_AT = 5


class FfnWeights:

    def __init__(self, nc, ctx, finished):
        t = Tiles(nc, ctx, "ffn1w", finished)
        self.w1, self.w2 = t.sb("w1", [P, HC, INNER]), t.sb("w2", [P, NI, HID])
        self.w1q, self.w2q = t.sb("w1q", [P, HC, INNER], BF16), t.sb("w2q", [P, NI, HID], BF16)
        self.b1, self.b2 = t.sb("b1", [P, INNER]), t.sb("b2", [P, HID])
        self.half_sum = t.sb("half_sum", [P, 4])
        self.wsum, self.wmean, self.winv = t.sb("wsum", [P, 2]), t.sb("wmean", [P, 2]), t.sb("winv", [P, 2])
        self.identb = t.sb("identb", [P, P], BF16)
        self.loaded = [t.sem("loaded0"), t.sem("loaded1")]

    def load(self, sp, T):
        sp.dma_start(self.w1[:], T["w1T"].rearrange("(k p) n -> p k n", p=P)).then_inc(self.loaded[0], 16)
        sp.dma_start(self.b1[:], T["b1"].to_broadcast([P, INNER])).then_inc(self.loaded[0], 16)
        sp.dma_start(self.w2[:], T["w2T"].rearrange("(k p) n -> p k n", p=P)).then_inc(self.loaded[1], 16)
        sp.dma_start(self.b2[:], T["b2"].to_broadcast([P, HID])).then_inc(self.loaded[1], 16)

    def half(self, n):
        raw, rounded = ((self.w1, self.w1q), (self.w2, self.w2q))[n // 2]
        cols = slice(n % 2 * 2 * INNER, (n % 2 + 1) * 2 * INNER)
        return raw[:].rearrange("p k n -> p (k n)")[:, cols], rounded[:].rearrange("p k n -> p (k n)")[:, cols]


def self_attention_1(nc, T, c, fw):
    SK = S + PREFIX
    WIDTH = (P + PREFIX, SK)
    with ExitStack() as ctx:
        t = Tiles(nc, ctx, "self1", c["finished"])
        w = {n: t.sb(n, [P, HC, HID]) for n in ("wq", "wk", "wv", "wo")}
        rows = t.sb("rows", [1, 2, HID])
        cols = t.sb("cols", [P, 2, HC])
        pv = t.sb("pv", [PREFIX, HID])
        kT = t.sb("kT", [P, NG, SK])
        xnT = t.sb("xnT", [P, HC, S])
        attn, attnT = t.sb("attn", [P, QT, HID]), t.sb("attnT", [P, HC, S])
        small_loaded, loaded = t.sem("small_loaded"), [t.sem(f"loaded{i}") for i in range(4)]

        def load_weights(sp):
            for sem, (name, tile) in zip(loaded, w.items()):
                sp.dma_start(tile[:], T[name + "_s1"].rearrange("(k p) n -> p k n", p=P)).then_inc(sem, 16)
            sp.dma_start(rows[:], T["rows_s1"]).then_inc(small_loaded, 16)
            sp.dma_start(cols[:], T["cols_s1"]).then_inc(small_loaded, 16)
            sp.dma_start(pv[:], T["pv"]).then_inc(small_loaded, 16)
            sp.dma_start(kT[:, :, S:SK], T["pkT"]).then_inc(small_loaded, 16)
            fw.load(sp, T)

        layernorm_transposed(nc, c, "norm4", c["x"], xnT, load_weights)
        with ExitStack() as ctx2:
            t = Tiles(nc, ctx2, "self1a", c["finished"])
            qT, v = t.sb("qT", [P, NG, S]), t.sb("v", [P, QT, HID])
            mask = t.sb("mask", [P, QT, SK])
            scores, work, probs = (t.sb(n, [P, 2, SK]) for n in ("scores", "work", "probs"))
            top = t.sb("top", [P, 2, TOPK // 8, 8])
            negmax, sums, rinv = t.sb("negmax", [P, 2]), t.sb("sums", [P, 2]), t.sb("rinv", [P, 2])
            probsT = t.sb("probsT", [P, 2, 3 * P])
            qk_ps, s_ps, t_ps, o_ps = (t.psum(n, [P, 2, CH]) for n in ("qk_ps", "s_ps", "t_ps", "o_ps"))
            chain = [t.sem(f"chain{q}") for q in range(QT)]
            mask_made, proj_done, proj_read, s_done, masked, max_done, exp_done, normed, t_done, t_copied, \
                o_done, search_done = map(t.sem, (
                    "mask_made", "proj_done", "proj_read", "s_done", "masked", "max_done", "exp_done",
                    "normed", "t_done", "t_copied", "o_done", "search_done"))
            abs_done, wsum_done, wmean_ready, winv_ready, bias_made, shifted, above = map(t.sem, (
                "abs_done", "wsum_done", "wmean_ready", "winv_ready", "bias_made", "shifted", "above"))
            winv_steps = t.sem("winv_steps")
            rinv_done = t.sem("rinv_done")
            round_up, round_down = t.sb("round_up", [P, 1]), t.sb("round_down", [P, 1])
            def pair(h):
                return [(QT * h + q, (h, q)) for q in range(QT)]

            block = ctx2.enter_context(nc.Block())

            @block.gpsimd
            def _(pool):
                nc.gpsimd.memset(mask[:], 0.0).then_inc(mask_made, 1)
                nc.gpsimd.tensor_copy(fw.identb[:], c["ident"][:])
                nc.gpsimd.memset(round_up[:], ROUND).then_inc(bias_made, 1)
                nc.gpsimd.memset(round_down[:], 1.0 - ROUND).then_inc(bias_made, 1)
                pool.wait_ge(mask_made, 1)
                for q in range(QT):
                    nc.gpsimd.affine_select(out=mask[:, q, :], in_=mask[:, q, :], compare_op=ALU.is_ge, fill=MASKED,
                                            base=q * P + PREFIX, pattern=[[-1, SK]],
                                            channel_multiplier=1).then_inc(mask_made, 1)
                for n in range(4):
                    raw, rounded = fw.half(n)
                    pool.wait_ge(above, n + 1)
                    nc.gpsimd.tensor_scalar(rounded, raw, 2.0, 1.0, ALU.min, ALU.subtract)

            @block.tensor
            def _(pe):
                def score(p):
                    for i, (h, q) in pair(p):
                        at_least(pe, masked, i - 1)
                        r, g = slice(h % HG * HD, (h % HG + 1) * HD), h // HG
                        nc.tensor.matmul(s_ps[:, q, 0:WIDTH[q]], qT[r, g, q * P:(q + 1) * P],
                                         kT[r, g, 0:WIDTH[q]], start=True, stop=True).then_inc(s_done, 1)

                def turn(p):
                    for n, (h, q) in pair(p):
                        pe.wait_ge(normed, n + 1)
                        at_least(pe, t_copied, n - 1)
                        for j, at in enumerate(range(0, WIDTH[q], P)):
                            m = min(P, WIDTH[q] - at)
                            last = nc.tensor.transpose(t_ps[0:m, q, j * P:(j + 1) * P],
                                                       probs[:, q, at:at + m], c["ident"][:])
                        last.then_inc(t_done, 1)

                def output(p):
                    for n, (h, q) in pair(p):
                        pe.wait_ge(t_copied, n + 1)
                        if n == 0:
                            pe.wait_ge(proj_read, 2 * NG + 2)
                        at, out = slice(h * HD, (h + 1) * HD), o_ps[:, q, h * HD:(h + 1) * HD]
                        full = WIDTH[q] // P
                        for j in range(full):
                            nc.tensor.matmul(out, probsT[:, q, j * P:(j + 1) * P], v[:, j, at],
                                             start=(j == 0), stop=False)
                        rest = v[0:PREFIX, 1, at] if q == 0 else pv[:, at]
                        nc.tensor.matmul(out, probsT[0:PREFIX, q, full * P:(full + 1) * P], rest,
                                         start=False, stop=True).then_inc(o_done, 1)

                def project(i):
                    n, g = i % 2, i // 2
                    if g == 0:
                        pe.wait_ge(loaded[n], 16)
                    at_least(pe, proj_read, i - 1)
                    for k in range(HC):
                        last = nc.tensor.matmul(qk_ps[:, n, 0:S], w["wq" if n == 0 else "wk"][:, k, g * P:(g + 1) * P],
                                                xnT[:, k, :], start=(k == 0), stop=(k == HC - 1))
                    last.then_inc(proj_done, 1)

                project(0)
                project(1)
                pe.wait_ge(proj_read, 2)
                pe.wait_ge(small_loaded, 64)
                score(0)
                project(2)
                project(3)
                score(1)
                for i in range(4, 2 * NG):
                    project(i)
                pe.wait_ge(loaded[2], 16)
                for q in range(QT):
                    for k in range(HC):
                        nc.tensor.matmul(o_ps[:, q, :], xnT[:, k, q * P:(q + 1) * P], w["wv"][:, k, :],
                                         start=(k == 0), stop=False)
                    nc.tensor.matmul(o_ps[:, q, :], c["ones"][0:1, :], rows[:, 0, :],
                                     start=False, stop=True).then_inc(proj_done, 1)
                for p in range(H):
                    if 0 < p < H - 1:
                        if p + 1 == HG:
                            pe.wait_ge(proj_read, 2 * NG)
                        score(p + 1)
                    if p == MEANS_AT:
                        pe.wait_ge(wsum_done, 1)
                        nc.tensor.matmul(qk_ps[:, 0, 0:2], c["ones"][:], fw.wsum[:],
                                         start=True, stop=True).then_inc(wmean_ready, 1)
                    turn(p)
                    if p > 0:
                        output(p - 1)
                output(H - 1)

            @block.scalar
            def _(act):
                act.wait_ge(small_loaded, 64)
                def read_projection(i):
                    n, g = i % 2, i // 2
                    act.wait_ge(proj_done, i + 1)
                    target = qT[:, g, :] if n == 0 else kT[:, g, 0:S]
                    nc.scalar.activation(target, qk_ps[:, n, 0:S], ACT.Identity,
                                         bias=cols[:, n, g:g + 1]).then_inc(proj_read, 1)

                def exps(p):
                    for i, (h, q) in pair(p):
                        act.wait_ge(max_done, i + 1)
                        nc.scalar.activation(probs[:, q, 0:WIDTH[q]], scores[:, q, 0:WIDTH[q]], ACT.Exp,
                                             bias=negmax[:, q:q + 1]).then_inc(exp_done, 1)

                def round_weights(step):
                    if step < 4:
                        act.wait_ge(fw.loaded[step // 2], 32)
                        raw, rounded = fw.half(step)
                        nc.scalar.activation(rounded, raw, ACT.Abs,
                                             accum_out=fw.half_sum[:, step:step + 1]).then_inc(abs_done, 1)
                        return
                    n = (step - 4) // 2
                    raw, _ = fw.half(n)
                    if step % 2 == 0:
                        act.wait_ge(winv_ready, 1)
                        act.wait_ge(bias_made, 2)
                        nc.scalar.activation(raw, raw, ACT.Identity, bias=round_up[:],
                                             scale=fw.winv[:, n // 2:n // 2 + 1]).then_inc(shifted, 1)
                    else:
                        act.wait_ge(shifted, n + 1)
                        nc.scalar.activation(raw, raw, ACT.Relu, bias=round_down[:]).then_inc(above, 1)

                for i in range(4):
                    read_projection(i)
                exps(0)
                for i in range(4, 2 * NG):
                    read_projection(i)
                for q in range(QT):
                    act.wait_ge(proj_done, 2 * NG + q + 1)
                    nc.scalar.activation(v[:, q, :], o_ps[:, q, :], ACT.Copy).then_inc(proj_read, 1)
                for p in range(H):
                    if p > 0:
                        exps(p)
                    if MEANS_AT - 4 <= p < MEANS_AT:
                        round_weights(p - (MEANS_AT - 4))
                    if MEANS_AT < p <= MEANS_AT + 8:
                        round_weights(4 + p - (MEANS_AT + 1))
                    for n, (h, q) in pair(p):
                        act.wait_ge(rinv_done, n + 1)
                        nc.scalar.activation(probs[:, q, 0:WIDTH[q]], probs[:, q, 0:WIDTH[q]], ACT.Copy,
                                             scale=rinv[:, q:q + 1]).then_inc(normed, 1)
                    for n, (h, q) in pair(p):
                        act.wait_ge(t_done, n + 1)
                        at_least(act, o_done, n - 1)
                        full = WIDTH[q] // P
                        nc.scalar.activation(probsT[:, q, 0:full * P], t_ps[:, q, 0:full * P], ACT.Copy)
                        at = slice(full * P, (full + 1) * P)
                        nc.scalar.activation(probsT[0:PREFIX, q, at], t_ps[0:PREFIX, q, at],
                                             ACT.Copy).then_inc(t_copied, 1)

            @block.vector
            def _(dve):
                steps = [0] * QT

                def link(q, instruction):
                    steps[q] += 1
                    instruction.then_inc(chain[q], 1)

                def linked(q):
                    dve.wait_ge(chain[q], steps[q])

                dve.wait_ge(mask_made, 3)
                for h in range(H):
                    if h == MEANS_AT:
                        dve.wait_ge(abs_done, 4)
                        nc.vector.tensor_reduce(fw.wsum[:], fw.half_sum[:].rearrange("p (w n) -> p w n", w=2), AX_X,
                                                ALU.add).then_inc(wsum_done, 1)
                    for i, (_, q) in pair(h):
                        W = WIDTH[q]
                        dve.wait_ge(s_done, i + 1)
                        at_least(dve, exp_done, i - 1)
                        nc.vector.scalar_tensor_tensor(scores[:, q, 0:W], s_ps[:, q, 0:W], SCALE1, mask[:, q, 0:W],
                                                       ALU.mult, ALU.add).then_inc(masked, 1)
                    for r in range(TOPK // 8):
                        source = scores if r == 0 else work
                        for i, (_, q) in pair(h):
                            if r == 0:
                                dve.wait_ge(masked, i + 1)
                            else:
                                linked(q)
                            link(q, nc.vector.max(top[:, q, r, :], source[:, q, 0:WIDTH[q]]))
                        for i, (_, q) in pair(h):
                            linked(q)
                            link(q, nc.vector.match_replace(work[:, q, 0:WIDTH[q]], top[:, q, r, :],
                                                            source[:, q, 0:WIDTH[q]], REPLACED))
                            if r == 0:
                                nc.vector.tensor_scalar(negmax[:, q:q + 1], top[:, q, 0, 0:1], -1.0, None,
                                                        ALU.mult).then_inc(max_done, 1)
                    for i, (_, q) in pair(h):
                        dve.wait_ge(exp_done, i + 1)
                        linked(q)
                        link(q, nc.vector.scalar_tensor_tensor(probs[:, q, 0:WIDTH[q]], work[:, q, 0:WIDTH[q]], REPLACED,
                                                               probs[:, q, 0:WIDTH[q]], ALU.is_equal, ALU.mult,
                                                               accum_out=sums[:, q:q + 1]))
                    for i, (_, q) in pair(h):
                        linked(q)
                        at_least(dve, normed, i - 1)
                        nc.vector.reciprocal(rinv[:, q:q + 1], sums[:, q:q + 1]).then_inc(rinv_done, 1)
                    if h == MEANS_AT:
                        dve.wait_ge(wmean_ready, 1)
                        nc.vector.tensor_scalar(fw.wmean[:], qk_ps[:, 0, 0:2], 1.0 / (HID * INNER), 1e-8, ALU.mult,
                                                ALU.max).then_inc(winv_steps, 1)
                        dve.wait_ge(winv_steps, 1)
                        nc.vector.reciprocal(fw.winv[:], fw.wmean[:]).then_inc(winv_ready, 1)
                dve.wait_ge(o_done, QT * H)
                for q in range(QT):
                    nc.vector.tensor_copy(attn[:, q, :], o_ps[:, q, :])
        transpose_tokens(nc, c, "turn4", (attn,), attnT)
        output_projection(nc, c, "out4", attnT, HC, w["wo"], [(loaded[3], 16)], rows[:, 1, :])


def feed_forward_1(nc, c, fw):
    with ExitStack() as ctx:
        t = Tiles(nc, ctx, "ffn1", c["finished"])
        w1q, w2q, b1, b2, wmean = fw.w1q, fw.w2q, fw.b1, fw.b2, fw.wmean
        h = t.sb("h", [P, QT, INNER])
        hq = t.sb("hq", [P, INNER], BF16)
        aT1, aT2 = t.sb("aT1", [P, HC, S], BF16), t.sb("aT2", [P, NI, S], BF16)
        xn = t.sb("xn", [P, QT, HID])
        stats, mv = t.sb("stats", [P, QT, 4, 6]), t.sb("mv", [P, QT, 2])
        logvar, rstd = t.sb("logvar", [P, QT]), t.sb("rstd", [P, QT])
        peak, step, inv_step = t.sb("peak", [P, 1]), t.sb("step", [P, 1]), t.sb("inv_step", [P, 1])
        scale = t.sb("scale", [P, 2, QT])
        chain, moments_done, log_done, rstd_done = map(t.sem, ("chain", "moments_done", "log_done", "rstd_done"))
        a_ready, a_turned, a_copied, y1_done, h_ready, gelu_done, y2_done = map(
            t.sem, ("a_ready", "a_turned", "a_copied", "y1_done", "h_ready", "gelu_done", "y2_done"))
        turned = t.psum("turned", [P, NI, P], BF16)
        y_ps = t.psum("y_ps", [P, 4, CH])
        block = ctx.enter_context(nc.Block())

        @block.scalar
        def _(act):
            def token_rstd(n):
                q = slice(n % QT, n % QT + 1)
                act.wait_ge(moments_done, n + 1)
                nc.scalar.activation(logvar[:, q], mv[:, n % QT, 1:2], ACT.Ln, bias=c["eps5"][:]).then_inc(log_done, 1)
                act.wait_ge(log_done, n + 1)
                nc.scalar.activation(rstd[:, q], logvar[:, q], ACT.Exp, scale=-0.5).then_inc(rstd_done, 1)

            def copy_turned(target, n, chunks):
                act.wait_ge(a_turned, n + 1)
                nc.scalar.activation(target, turned[:, 0:chunks, :], ACT.Copy).then_inc(a_copied, 1)

            for n in range(2 * QT):
                token_rstd(n)
            for q in range(QT):
                copy_turned(aT1[:, :, q * P:(q + 1) * P], q, HC)
            for q in range(QT):
                act.wait_ge(h_ready, 4 * q + 4)
                nc.scalar.activation(h[:, q, :], h[:, q, :], ACT.Gelu).then_inc(gelu_done, 1)
            nc.scalar.preload_act_table_set("natural_log_exp_and_others")
            for q in range(QT):
                token_rstd(2 * QT + q)
            for q in range(QT):
                copy_turned(aT2[:, :, q * P:(q + 1) * P], QT + q, NI)

        @block.tensor
        def _(pe):
            for q in range(QT):
                pe.wait_ge(a_ready, q + 1)
                at_least(pe, a_copied, q)
                for k in range(HC):
                    last = nc.tensor.transpose(turned[:, k, :], hq[:, k * P:(k + 1) * P], fw.identb[:])
                last.then_inc(a_turned, 1)
            for q in range(QT):
                pe.wait_ge(a_copied, q + 1)
                for n in range(4):
                    at_least(pe, h_ready, 4 * (q - 1) + n + 1)
                    for k in range(HC):
                        last = nc.tensor.matmul(y_ps[:, n, :], aT1[:, k, q * P:(q + 1) * P],
                                                w1q[:, k, n * CH:(n + 1) * CH], start=(k == 0), stop=(k == HC - 1))
                    last.then_inc(y1_done, 1)
            for q in range(QT):
                pe.wait_ge(a_ready, QT + q + 1)
                pe.wait_ge(a_copied, QT + q)
                for k in range(NI):
                    last = nc.tensor.transpose(turned[:, k, :], hq[:, k * P:(k + 1) * P], fw.identb[:])
                last.then_inc(a_turned, 1)
            for q in range(QT):
                pe.wait_ge(a_copied, QT + q + 1)
                pe.wait_ge(h_ready, 8)
                for k in range(NI):
                    last = nc.tensor.matmul(y_ps[:, q, :], aT2[:, k, q * P:(q + 1) * P], w2q[:, k, :],
                                            start=(k == 0), stop=(k == NI - 1))
                last.then_inc(y2_done, 1)

        @block.vector
        def _(dve):
            steps = [0]

            def then_wait(instruction):
                steps[0] += 1
                instruction.then_inc(chain, 1)
                dve.wait_ge(chain, steps[0])

            def moments(src, n):
                parts = src.shape[-1] // CH
                at_least(dve, moments_done, n - 1)
                for i in range(parts):
                    steps[0] += 1
                    nc.vector.bn_stats(stats[:, n % QT, i, :], src[:, i * CH:(i + 1) * CH]).then_inc(chain, 1)
                dve.wait_ge(chain, steps[0])
                nc.vector.bn_aggr(mv[:, n % QT, :], stats[:, n % QT, 0:parts, :].rearrange("p a b -> p (a b)"))\
                  .then_inc(moments_done, 1)

            def normalise(src, dst, n):
                dve.wait_ge(moments_done, n + 1)
                dve.wait_ge(rstd_done, n + 1)
                then_wait(nc.vector.tensor_scalar(dst, src, mv[:, n % QT, 0:1], rstd[:, n % QT:n % QT + 1],
                                                  ALU.subtract, ALU.mult))

            def quantise(src, factor, width):
                then_wait(nc.vector.tensor_reduce(peak[:], src, AX_X, ALU.max, apply_absolute_value=True))
                then_wait(nc.vector.tensor_scalar(step[:], peak[:], 1e-5, 1.0 / 127.0, ALU.max, ALU.mult))
                then_wait(nc.vector.reciprocal(inv_step[:], step[:]))
                then_wait(nc.vector.tensor_tensor(factor, step[:], wmean[:, 0:1] if width == HID else wmean[:, 1:2],
                                                  ALU.mult))
                then_wait(nc.vector.tensor_scalar(src, src, inv_step[:], ROUND, ALU.mult, ALU.add))
                then_wait(nc.vector.tensor_scalar(src, src, ROUND, 127.0, ALU.subtract, ALU.min))
                nc.vector.tensor_scalar(hq[:, 0:width], src, -128.0, None, ALU.max).then_inc(a_ready, 1)

            for n, source in enumerate((c["x"], xn)):
                for q in range(QT):
                    moments(source[:, q, :], QT * n + q)
                for q in range(QT):
                    normalise(source[:, q, :], xn[:, q, :], QT * n + q)
            for q in range(QT):
                at_least(dve, a_turned, q)
                quantise(xn[:, q, :], scale[:, 0, q:q + 1], HID)
            for q in range(QT):
                for n in range(4):
                    cols = slice(n * CH, (n + 1) * CH)
                    dve.wait_ge(y1_done, 4 * q + n + 1)
                    nc.vector.scalar_tensor_tensor(h[:, q, cols], y_ps[:, n, :], scale[:, 0, q:q + 1], b1[:, cols],
                                                   ALU.mult, ALU.add).then_inc(h_ready, 1)
            for q in range(QT):
                dve.wait_ge(gelu_done, q + 1)
                moments(h[:, q, :], 2 * QT + q)
            for q in range(QT):
                normalise(h[:, q, :], h[:, q, :], 2 * QT + q)
                dve.wait_ge(a_turned, QT + q)
                quantise(h[:, q, :], scale[:, 1, q:q + 1], INNER)
            for q in range(QT):
                dve.wait_ge(y2_done, q + 1)
                then_wait(nc.vector.scalar_tensor_tensor(xn[:, q, :], y_ps[:, q, :], scale[:, 1, q:q + 1], b2[:],
                                                         ALU.mult, ALU.add))
                nc.vector.tensor_tensor(c["x"][:, q, :], c["x"][:, q, :], xn[:, q, :], ALU.add)


def store_output(nc, c, out):
    with nc.semaphore("result_stored") as stored, nc.Block() as block:
        @block.sync
        def _(sp):
            sp.dma_start(out.rearrange("a (t p) n -> p (a t) n", p=P), c["x"][:]).then_inc(stored, 16)
            sp.wait_ge(stored, 16)


def perceiver(nc, T, out):
    with ExitStack() as ctx:
        finished = []
        keep = Tiles(nc, ctx, "keep", finished)
        c = {"ident": keep.sb("ident", [P, P]), 
             "ones": keep.sb("ones", [P, P]), "eps5": keep.sb("eps5", [P, 1]), "eps6": keep.sb("eps6", [P, 1]),
             "x": keep.sb("x", [P, QT, HID]), "finished": finished}
        with ExitStack() as ctx_context:
            t = Tiles(nc, ctx_context, "context", finished)
            ctxT_hi, ctxT_lo = t.sb("ctxT_hi", [P, CC, KV], F32R), t.sb("ctxT_lo", [P, CC, KV], F32R)
            with ExitStack() as ctx_layer0:
                buffers = Layer0Buffers(nc, ctx_layer0, finished)
                cross_attention_0(nc, T, c, buffers, ctxT_hi, ctxT_lo)
                clear_semaphores(nc, finished)
                small = SmallWeights0(nc, ctx_layer0, finished)
                self_attention_0(nc, T, c, buffers, lambda sp: small.load(sp, T, buffers))
                feed_forward_0(nc, T, c, buffers, small)
            clear_semaphores(nc, finished)
            cross_attention_1(nc, T, c, ctxT_hi, ctxT_lo)
        clear_semaphores(nc, finished)
        fw = FfnWeights(nc, ctx, finished)
        self_attention_1(nc, T, c, fw)
        feed_forward_1(nc, c, fw)
        store_output(nc, c, out)


def kernel(**inputs):
    import numpy as np
    import concourse.bacc as bacc
    from concourse.bass_utils import run_bass_kernel_spmd

    v = {name: np.asarray(a) for name, a in inputs.items()}
    ctx = v["ctx_1024"][0]

    def by_head(w):
        return w.reshape(CC, P, H, D).transpose(2, 1, 0, 3).reshape(H * P, CC * D)

    def by_group(w):
        return w.reshape(-1, NG, HG, 2, HD).transpose(0, 1, 3, 2, 4).reshape(-1, NG, 2 * P)

    wkv1 = by_group(np.concatenate([v["L1_xattn_Wk"], v["L1_xattn_Wv"]], axis=1))
    bkv1 = by_group(np.concatenate([v["L1_xattn_bk"], v["L1_xattn_bv"]])[None])
    four = lambda name: np.tile(v[name], HG)[:, None]
    laid_out = {
        "wkv1": wkv1.reshape(CC, P, NG, 2 * P).transpose(2, 1, 0, 3).reshape(NG * P, CC * 2 * P),
        "bk1": bkv1[:, :, :P].reshape(1, HID), "bv1": bkv1[:, :, P:].reshape(1, HID),
        "affine_k1": np.concatenate([four("L1_xattn_kn_w"), four("L1_xattn_kn_b")], axis=1),
        "affine1": np.concatenate([four("L1_xattn_" + n) for n in ("qn_w", "qn_b", "kn_dca_w", "kn_dca_b")], axis=1),
        "wq1": v["L1_xattn_Wq"], "bq1": v["L1_xattn_bq"][None],
        "wkv_dca": v["L1_xattn_Wkv_dca"], "bkv_dca": v["L1_xattn_bkv_dca"][None],
        **{f"w{n}_s1": v[f"L1_attn_W{n}"] for n in "qkvo"},
        "rows_s1": np.stack([v["L1_attn_bv"], v["L1_attn_bo"]])[None],
        "cols_s1": np.stack([v["L1_attn_bq"], v["L1_attn_bk"]]).reshape(2, HC, P).transpose(2, 0, 1),
        "pv": v["L1_attn_pv"][0], "pkT": v["L1_attn_pk"][0].reshape(PREFIX, NG, P).transpose(2, 1, 0),
        "w1T": v["L1_ffn_w1"].T, "w2T": v["L1_ffn_w2"].T, "b1": v["L1_ffn_b1"][None], "b2": v["L1_ffn_b2"][None],
        "wo1": v["L1_xattn_Wo"], "bo1": v["L1_xattn_bo"][None],
        "x": v["x"][0], "ctx": ctx, "ctxT": ctx.T,
        "wq0": v["L0_xattn_Wq"], "wk0": by_head(v["L0_xattn_Wk"]), "wv0": by_head(v["L0_xattn_Wv"]),
        "wo0": v["L0_xattn_Wo"], "gq": v["L0_xattn_gq"][:, None], "gk": v["L0_xattn_gk"][:, None],
        "wq_s0": v["L0_attn_Wq"].T, "wk_s0": v["L0_attn_Wk"].T, "wv_s0": v["L0_attn_Wv"].T,
        "wo_s0": v["L0_attn_Wo"].T, "bo_s0": v["L0_attn_bo"][None],
        "gate": v["L0_ffn_gate_w"], "up": v["L0_ffn_up_w"], "down": v["L0_ffn_down_w"],
        "expert": v["L0_ffn_expert_weight"], "gamma": v["L0_ffn_ln_gamma"][None], "beta": v["L0_ffn_ln_beta"][None],
    }
    laid_out = {f"in_{n}": np.ascontiguousarray(a) for n, a in laid_out.items()}
    nc = bacc.Bacc("TRN2", target_bir_lowering=False, num_devices=1)
    T = {n[3:]: nc.dram_tensor(n, a.shape, mybir.dt.from_np(a.dtype), kind="ExternalInput").ap()
         for n, a in laid_out.items()}
    out = nc.dram_tensor("out_x", (1, S, HID), F32, kind="ExternalOutput").ap()
    perceiver(nc, T, out)
    r = run_bass_kernel_spmd(nc, [laid_out], core_ids=[0])
    return r.results[0]["out_x"]
```
